# Optimizing a Trainium2 kernel written in Bass

```python
import numpy as np
import jax
import jax.numpy as jnp

def _softmax(x, axis=-1):
    return jax.nn.softmax(x, axis=axis)
def _gelu(x):
    return jax.nn.gelu(x, approximate=True)
def _silu(x):
    return jax.nn.silu(x)
def _sigmoid(x):
    return jax.nn.sigmoid(x)
def _layernorm(x, axis=-1, eps=1e-5):
    m = jnp.mean(x, axis=axis, keepdims=True)
    v = jnp.var(x, axis=axis, keepdims=True)
    return (x - m) / jnp.sqrt(v + eps)
def _scatter_add(tgt, idx, src, axis=0):
    return tgt.at[idx].add(src)
def _segment_sum(src, seg, n):
    return jax.ops.segment_sum(src, seg, n)

kernel_name = 'mk_adj_ffn_d4_adj_256_16a8cf'

def setup_inputs(seed: int = 0):
    np.random.seed(seed)
    _w = jnp.asarray
    def _rec_inputs():
        import jax
        import jax.numpy as jnp
        _gk = jax.random.key(seed)
        x = -0.0002928 + 1 * jax.random.normal(jax.random.fold_in(_gk, 1), (2708, 256), jnp.float32)
        _a = jax.random.bernoulli(jax.random.fold_in(_gk, 2), 0.0014771, (2708, 2708))
        _a = jnp.logical_or(_a, jnp.eye(2708, dtype=bool))
        _af = _a.astype(jnp.float32)
        _af = _af * jax.random.uniform(jax.random.fold_in(_gk, 3), (2708, 2708), jnp.float32, 0.05, 1)
        adj = _af
        return x, adj
    x, adj = _rec_inputs()
    def _L0_gnn_setup():
        import jax, jax.numpy as jnp
        import numpy as np
        N = 16384
        D = 256
        OUT = 256
        key = jax.random.key(seed)
        k1, k2, k3 = jax.random.split(key, 3)
        features = jax.random.normal(k1, (N, D), dtype=jnp.float32)
        adj = jax.random.uniform(k2, (N, N), dtype=jnp.float32)
        W = jax.random.normal(k3, (OUT, 2 * D), dtype=jnp.float32)
        return {'features': features, 'adj': adj, 'W': W}
    _L0_gnn_all = _L0_gnn_setup()
    _L0_gnn_in = {k: v for k, v in _L0_gnn_all.items() if k in ('W', )}
    del _L0_gnn_all

    def _L0_ffn_setup():
        import jax, jax.numpy as jnp
        import numpy as np
        B, K, D = (512, 16, 256)
        E = 32
        H = int(D * 0.25)
        key = jax.random.key(seed)
        ks = jax.random.split(key, 7)
        d_rs = D ** (-0.5)
        h_rs = H ** (-0.5)
        x = jax.random.normal(ks[0], (B, K, D), dtype=jnp.float32)
        router_w = jax.random.uniform(ks[1], (E, D), jnp.float32, -d_rs, d_rs)
        router_b = jax.random.uniform(ks[2], (E,), jnp.float32, -d_rs, d_rs)
        W1 = jax.random.uniform(ks[3], (E, D, H), jnp.float32, -h_rs, h_rs)
        b1 = jax.random.uniform(ks[4], (E, H), jnp.float32, -h_rs, h_rs)
        W2 = jax.random.uniform(ks[5], (E, H, D), jnp.float32, -d_rs, d_rs)
        b2 = jax.random.uniform(ks[6], (E, D), jnp.float32, -d_rs, d_rs)
        return {'x': x, 'router_w': router_w, 'router_b': router_b, 'W1': W1, 'b1': b1, 'W2': W2, 'b2': b2}
    _L0_ffn_all = _L0_ffn_setup()
    _L0_ffn_in = {k: v for k, v in _L0_ffn_all.items() if k in ('router_w', 'router_b', 'W1', 'b1', 'W2', 'b2', )}
    del _L0_ffn_all

    def _L1_gnn_setup():
        import jax, jax.numpy as jnp
        import numpy as np
        N = 8192
        EMB = 256
        EDGE_P = 0.004
        LN_EPS = 1e-05

        def _layernorm(h, g, b):
            mu = jnp.mean(h, axis=-1, keepdims=True)
            var = jnp.mean(jnp.square(h - mu), axis=-1, keepdims=True)
            return (h - mu) * jax.lax.rsqrt(var + LN_EPS) * g + b
        key = jax.random.key(seed)
        ks = jax.random.split(key, 10)
        x = jax.random.normal(ks[0], (N, EMB), dtype=jnp.float32)
        adj = (jax.random.uniform(ks[1], (N, N)) < EDGE_P).astype(jnp.float32)
        adj = jnp.fill_diagonal(adj, 1.0, inplace=False)
        s = 1.0 / np.sqrt(EMB)
        W1 = jax.random.normal(ks[2], (EMB, EMB), dtype=jnp.float32) * s
        b1 = jax.random.normal(ks[3], (EMB,), dtype=jnp.float32) * s
        W2 = jax.random.normal(ks[4], (EMB, EMB), dtype=jnp.float32) * s
        b2 = jax.random.normal(ks[5], (EMB,), dtype=jnp.float32) * s
        W3 = jax.random.normal(ks[6], (EMB, EMB), dtype=jnp.float32) * s
        b3 = jax.random.normal(ks[7], (EMB,), dtype=jnp.float32) * s
        ones = jnp.ones((EMB,), jnp.float32)
        zeros = jnp.zeros((EMB,), jnp.float32)
        return {'x': x, 'adj': adj, 'W1': W1, 'b1': b1, 'W2': W2, 'b2': b2, 'W3': W3, 'b3': b3, 'g1': ones, 'be1': zeros, 'g2': ones, 'be2': zeros, 'g3': ones, 'be3': zeros}
    _L1_gnn_all = _L1_gnn_setup()
    _L1_gnn_in = {k: v for k, v in _L1_gnn_all.items() if k in ('W1', 'b1', 'W2', 'b2', 'W3', 'b3', 'g1', 'be1', 'g2', 'be2', 'g3', 'be3', )}
    del _L1_gnn_all

    def _L1_ffn_setup():
        import jax, jax.numpy as jnp
        import numpy as np
        B, T, D, H, E = (16, 4096, 256, 512, 8)
        key = jax.random.key(seed)
        ks = jax.random.split(key, 5)
        x = jax.random.normal(ks[0], (B, T, D), dtype=jnp.float32)
        gate_w = jax.random.normal(ks[1], (D, E), dtype=jnp.float32) * 0.02
        gate_b = jnp.zeros((E,), dtype=jnp.float32)
        W1 = jax.random.normal(ks[2], (E, D, H), dtype=jnp.float32) * 0.02
        b1 = jnp.zeros((E, H), dtype=jnp.float32)
        W2 = jax.random.normal(ks[3], (E, H, D), dtype=jnp.float32) * 0.02
        b2 = jnp.zeros((E, D), dtype=jnp.float32)
        return {'x': x, 'gate_w': gate_w, 'gate_b': gate_b, 'W1': W1, 'b1': b1, 'W2': W2, 'b2': b2}
    _L1_ffn_all = _L1_ffn_setup()
    _L1_ffn_in = {k: v for k, v in _L1_ffn_all.items() if k in ('gate_w', 'gate_b', 'W1', 'b1', 'W2', 'b2', )}
    del _L1_ffn_all

    def _L2_gnn_setup():
        import jax, jax.numpy as jnp
        import numpy as np
        N = 6144
        HID = 256
        T = 700
        DENSITY = 0.05
        key = jax.random.key(seed)
        k1, k2, k3, k4, k5, k6 = jax.random.split(key, 6)
        h = jax.random.normal(k1, (N, HID), dtype=jnp.float32)
        a = jax.random.uniform(k2, (N, N), dtype=jnp.float32)
        mask = jax.random.uniform(k3, (N, N)) < DENSITY
        adj = jnp.where(mask, a, 0.0)
        simlar = jax.random.normal(k4, (N, N), dtype=jnp.float32)
        s = 1.0 / np.sqrt(HID)
        W_proj = jax.random.uniform(k5, (HID, HID), minval=-s, maxval=s, dtype=jnp.float32)
        b_proj = jnp.zeros((HID,), dtype=jnp.float32)
        W_gcn = jax.random.uniform(k6, (HID, HID), minval=-s, maxval=s, dtype=jnp.float32)
        b_gcn = jnp.zeros((HID,), dtype=jnp.float32)
        return {'h': h, 'adj': adj, 'simlar': simlar, 'W_proj': W_proj, 'b_proj': b_proj, 'W_gcn': W_gcn, 'b_gcn': b_gcn}
    _L2_gnn_all = _L2_gnn_setup()
    _L2_gnn_in = {k: v for k, v in _L2_gnn_all.items() if k in ('W_proj', 'b_proj', 'W_gcn', 'b_gcn', )}
    del _L2_gnn_all

    def _L2_ffn_setup():
        import jax, jax.numpy as jnp
        import numpy as np
        D_MODEL = 256
        EXPERT_DIM = 512
        NUM_EXPERTS = 8
        TOP_K = 2
        SEQ_LEN = 2048
        BATCH = 2
        key = jax.random.key(seed)
        ks = jax.random.split(key, 8)
        s = 0.02
        x = jax.random.normal(ks[0], (SEQ_LEN, BATCH, D_MODEL), dtype=jnp.float32)
        Wg = jax.random.normal(ks[1], (D_MODEL, NUM_EXPERTS), dtype=jnp.float32) * s
        bg = jax.random.normal(ks[2], (NUM_EXPERTS,), dtype=jnp.float32) * s
        bias = jnp.zeros((NUM_EXPERTS,), dtype=jnp.float32)
        W1 = jax.random.normal(ks[3], (NUM_EXPERTS, D_MODEL, EXPERT_DIM), dtype=jnp.float32) * s
        b1 = jax.random.normal(ks[4], (NUM_EXPERTS, EXPERT_DIM), dtype=jnp.float32) * s
        W2 = jax.random.normal(ks[5], (NUM_EXPERTS, EXPERT_DIM, D_MODEL), dtype=jnp.float32) * s
        b2 = jax.random.normal(ks[6], (NUM_EXPERTS, D_MODEL), dtype=jnp.float32) * s
        return {'x': x, 'Wg': Wg, 'bg': bg, 'bias': bias, 'W1': W1, 'b1': b1, 'W2': W2, 'b2': b2}
    _L2_ffn_all = _L2_ffn_setup()
    _L2_ffn_in = {k: v for k, v in _L2_ffn_all.items() if k in ('Wg', 'bg', 'bias', 'W1', 'b1', 'W2', 'b2', )}
    del _L2_ffn_all

    def _L3_gnn_setup():
        import jax, jax.numpy as jnp
        import numpy as np
        N = 4096
        IN = 256
        F = 64
        H = 4
        key = jax.random.key(seed)
        k1, k2, k3, k4, k5 = jax.random.split(key, 5)
        h = jax.random.normal(k1, (N, IN), jnp.float32)
        adj = jax.random.randint(k2, (N, N), 0, 2).astype(jnp.float32)
        adj = jnp.maximum(adj, jnp.eye(N, dtype=jnp.float32))
        Wm = (jax.random.normal(k3, (IN, H * F), jnp.float32) / np.sqrt(IN)).astype(jnp.float32)
        al = (jax.random.normal(k4, (F,), jnp.float32) / np.sqrt(2 * F)).astype(jnp.float32)
        ar = (jax.random.normal(k5, (F,), jnp.float32) / np.sqrt(2 * F)).astype(jnp.float32)
        return {'h': h, 'adj': adj, 'Wm': Wm, 'al': al, 'ar': ar}
    _L3_gnn_all = _L3_gnn_setup()
    _L3_gnn_in = {k: v for k, v in _L3_gnn_all.items() if k in ('Wm', 'al', 'ar', )}
    del _L3_gnn_all

    def _L3_ffn_setup():
        import jax, jax.numpy as jnp
        import numpy as np
        B, A = (4096, 8)
        IN, OUT = (256, 256)
        SH1, SH2 = (256, 128)
        EH1, EH2 = (128, 64)
        E, TOPK = (4, 2)

        def _shared_mlp(x, W1, b1, W2, b2, W3, b3):
            h = jax.nn.relu(x @ W1 + b1)
            h = jax.nn.relu(h @ W2 + b2)
            return h @ W3 + b3

        def _experts_mlp(x, eW1, eb1, eW2, eb2, eW3, eb3):
            h = jax.nn.relu(jnp.einsum('baf,efh->ebah', x, eW1) + eb1[:, None, None, :])
            h = jax.nn.relu(jnp.einsum('ebah,ehg->ebag', h, eW2) + eb2[:, None, None, :])
            o = jnp.einsum('ebag,ego->ebao', h, eW3) + eb3[:, None, None, :]
            return jnp.moveaxis(o, 0, -1)
        key = jax.random.key(seed)
        ks = jax.random.split(key, 16)
        s = 0.05
        return {'x': jax.random.normal(ks[0], (B, A, IN), jnp.float32), 'sW1': jax.random.normal(ks[1], (IN, SH1), jnp.float32) * s, 'sb1': jnp.zeros((SH1,), jnp.float32), 'sW2': jax.random.normal(ks[2], (SH1, SH2), jnp.float32) * s, 'sb2': jnp.zeros((SH2,), jnp.float32), 'sW3': jax.random.normal(ks[3], (SH2, OUT), jnp.float32) * s, 'sb3': jnp.zeros((OUT,), jnp.float32), 'eW1': jax.random.normal(ks[4], (E, IN, EH1), jnp.float32) * s, 'eb1': jnp.zeros((E, EH1), jnp.float32), 'eW2': jax.random.normal(ks[5], (E, EH1, EH2), jnp.float32) * s, 'eb2': jnp.zeros((E, EH2), jnp.float32), 'eW3': jax.random.normal(ks[6], (E, EH2, OUT), jnp.float32) * s, 'eb3': jnp.zeros((E, OUT), jnp.float32), 'gW': jax.random.normal(ks[7], (IN, E), jnp.float32) * s, 'gb': jnp.zeros((E,), jnp.float32)}
    _L3_ffn_all = _L3_ffn_setup()
    _L3_ffn_in = {k: v for k, v in _L3_ffn_all.items() if k in ('sW1', 'sb1', 'sW2', 'sb2', 'sW3', 'sb3', 'eW1', 'eb1', 'eW2', 'eb2', 'eW3', 'eb3', 'gW', 'gb', )}
    del _L3_ffn_all

    return {
        "x": x,
        "adj": adj,
        "L0_gnn_W": _L0_gnn_in["W"],
        "L0_ffn_router_w": _L0_ffn_in["router_w"],
        "L0_ffn_router_b": _L0_ffn_in["router_b"],
        "L0_ffn_W1": _L0_ffn_in["W1"],
        "L0_ffn_b1": _L0_ffn_in["b1"],
        "L0_ffn_W2": _L0_ffn_in["W2"],
        "L0_ffn_b2": _L0_ffn_in["b2"],
        "L1_gnn_W1": _L1_gnn_in["W1"],
        "L1_gnn_b1": _L1_gnn_in["b1"],
        "L1_gnn_W2": _L1_gnn_in["W2"],
        "L1_gnn_b2": _L1_gnn_in["b2"],
        "L1_gnn_W3": _L1_gnn_in["W3"],
        "L1_gnn_b3": _L1_gnn_in["b3"],
        "L1_gnn_g1": _L1_gnn_in["g1"],
        "L1_gnn_be1": _L1_gnn_in["be1"],
        "L1_gnn_g2": _L1_gnn_in["g2"],
        "L1_gnn_be2": _L1_gnn_in["be2"],
        "L1_gnn_g3": _L1_gnn_in["g3"],
        "L1_gnn_be3": _L1_gnn_in["be3"],
        "L1_ffn_gate_w": _L1_ffn_in["gate_w"],
        "L1_ffn_gate_b": _L1_ffn_in["gate_b"],
        "L1_ffn_W1": _L1_ffn_in["W1"],
        "L1_ffn_b1": _L1_ffn_in["b1"],
        "L1_ffn_W2": _L1_ffn_in["W2"],
        "L1_ffn_b2": _L1_ffn_in["b2"],
        "L2_gnn_W_proj": _L2_gnn_in["W_proj"],
        "L2_gnn_b_proj": _L2_gnn_in["b_proj"],
        "L2_gnn_W_gcn": _L2_gnn_in["W_gcn"],
        "L2_gnn_b_gcn": _L2_gnn_in["b_gcn"],
        "L2_ffn_Wg": _L2_ffn_in["Wg"],
        "L2_ffn_bg": _L2_ffn_in["bg"],
        "L2_ffn_bias": _L2_ffn_in["bias"],
        "L2_ffn_W1": _L2_ffn_in["W1"],
        "L2_ffn_b1": _L2_ffn_in["b1"],
        "L2_ffn_W2": _L2_ffn_in["W2"],
        "L2_ffn_b2": _L2_ffn_in["b2"],
        "L3_gnn_Wm": _L3_gnn_in["Wm"],
        "L3_gnn_al": _L3_gnn_in["al"],
        "L3_gnn_ar": _L3_gnn_in["ar"],
        "L3_ffn_sW1": _L3_ffn_in["sW1"],
        "L3_ffn_sb1": _L3_ffn_in["sb1"],
        "L3_ffn_sW2": _L3_ffn_in["sW2"],
        "L3_ffn_sb2": _L3_ffn_in["sb2"],
        "L3_ffn_sW3": _L3_ffn_in["sW3"],
        "L3_ffn_sb3": _L3_ffn_in["sb3"],
        "L3_ffn_eW1": _L3_ffn_in["eW1"],
        "L3_ffn_eb1": _L3_ffn_in["eb1"],
        "L3_ffn_eW2": _L3_ffn_in["eW2"],
        "L3_ffn_eb2": _L3_ffn_in["eb2"],
        "L3_ffn_eW3": _L3_ffn_in["eW3"],
        "L3_ffn_eb3": _L3_ffn_in["eb3"],
        "L3_ffn_gW": _L3_ffn_in["gW"],
        "L3_ffn_gb": _L3_ffn_in["gb"],
    }

def reference(x, adj, L0_gnn_W, L0_ffn_router_w, L0_ffn_router_b, L0_ffn_W1, L0_ffn_b1, L0_ffn_W2, L0_ffn_b2, L1_gnn_W1, L1_gnn_b1, L1_gnn_W2, L1_gnn_b2, L1_gnn_W3, L1_gnn_b3, L1_gnn_g1, L1_gnn_be1, L1_gnn_g2, L1_gnn_be2, L1_gnn_g3, L1_gnn_be3, L1_ffn_gate_w, L1_ffn_gate_b, L1_ffn_W1, L1_ffn_b1, L1_ffn_W2, L1_ffn_b2, L2_gnn_W_proj, L2_gnn_b_proj, L2_gnn_W_gcn, L2_gnn_b_gcn, L2_ffn_Wg, L2_ffn_bg, L2_ffn_bias, L2_ffn_W1, L2_ffn_b1, L2_ffn_W2, L2_ffn_b2, L3_gnn_Wm, L3_gnn_al, L3_gnn_ar, L3_ffn_sW1, L3_ffn_sb1, L3_ffn_sW2, L3_ffn_sb2, L3_ffn_sW3, L3_ffn_sb3, L3_ffn_eW1, L3_ffn_eb1, L3_ffn_eW2, L3_ffn_eb2, L3_ffn_eW3, L3_ffn_eb3, L3_ffn_gW, L3_ffn_gb):
    import jax
    import jax.numpy as jnp
    def _L0_gnn_ref(features, adj, W):
        import jax, jax.numpy as jnp
        import numpy as np
        N = 16384
        D = 256
        OUT = 256
        deg = adj.sum(axis=1, keepdims=True) + 1.0
        neigh = adj @ features / deg
        data = jnp.concatenate([features, neigh], axis=-1)
        return data @ W.T

    def _L0_ffn_ref(x, router_w, router_b, W1, b1, W2, b2):
        import jax, jax.numpy as jnp
        import numpy as np
        B, K, D = (512, 16, 256)
        E = 32
        H = int(D * 0.25)
        xf = x.reshape(-1, D)
        logits = xf @ router_w.T + router_b
        idx = jnp.argmax(logits, axis=-1)
        w1t = jnp.take(W1, idx, axis=0)
        h = jnp.einsum('nd,ndh->nh', xf, w1t) + jnp.take(b1, idx, axis=0)
        h = jax.nn.relu(h)
        w2t = jnp.take(W2, idx, axis=0)
        out = jnp.einsum('nh,nhd->nd', h, w2t) + jnp.take(b2, idx, axis=0)
        out = jax.nn.relu(out)
        return out.reshape(x.shape)

    def _L1_gnn_ref(x, adj, W1, b1, W2, b2, W3, b3, g1, be1, g2, be2, g3, be3):
        import jax, jax.numpy as jnp
        import numpy as np
        N = 8192
        EMB = 256
        EDGE_P = 0.004
        LN_EPS = 1e-05

        def _layernorm(h, g, b):
            mu = jnp.mean(h, axis=-1, keepdims=True)
            var = jnp.mean(jnp.square(h - mu), axis=-1, keepdims=True)
            return (h - mu) * jax.lax.rsqrt(var + LN_EPS) * g + b
        dinv = jnp.sum(adj, axis=-1) ** (-0.5)
        A = adj * dinv[:, None] * dinv[None, :]
        h1 = x @ W1 + b1
        n1 = _layernorm(jax.nn.relu(A @ h1) + h1, g1, be1)
        h2 = n1 @ W2 + b2
        n2 = _layernorm(jax.nn.relu(A @ h2) + n1, g2, be2)
        h3 = n2 @ W3 + b3
        n3 = _layernorm(jax.nn.relu(A @ h3) + n2, g3, be3)
        return n3

    def _L1_ffn_ref(x, gate_w, gate_b, W1, b1, W2, b2):
        import jax, jax.numpy as jnp
        import numpy as np
        B, T, D, H, E = (16, 4096, 256, 512, 8)
        Bb, Tt, Dd = x.shape
        Ee = gate_w.shape[1]
        xf = x.reshape(-1, Dd)
        N = xf.shape[0]
        logits = xf @ gate_w + gate_b
        probs = jax.nn.softmax(logits, axis=-1)
        top2_vals, top2_idx = jax.lax.top_k(probs, 2)
        cw = jnp.zeros((N, Ee), dtype=xf.dtype).at[jnp.arange(N)[:, None], top2_idx].add(top2_vals)

        def step(acc, params):
            w1, bb1, w2, bb2, we = params
            h = jax.nn.gelu(xf @ w1 + bb1, approximate=False)
            y = h @ w2 + bb2
            return (acc + we[:, None] * y, None)
        out, _ = jax.lax.scan(step, jnp.zeros_like(xf), (W1, b1, W2, b2, cw.T))
        return out.reshape(Bb, Tt, Dd)

    def _L2_gnn_ref(h, adj, simlar, W_proj, b_proj, W_gcn, b_gcn):
        import jax, jax.numpy as jnp
        import numpy as np
        N = 6144
        HID = 256
        T = 700
        DENSITY = 0.05
        sim = jnp.tanh(adj * simlar)
        filt = sim * (adj > 0).astype(sim.dtype)
        vals, idx = jax.lax.top_k(filt, T)
        nnz = jnp.sum(filt != 0, axis=1)
        keep = jnp.arange(T)[None, :] < nnz[:, None]
        rows = jnp.arange(filt.shape[0])[:, None]
        new_adj = jnp.zeros_like(filt).at[rows, idx].set(jnp.where(keep, vals, 0.0))
        h2 = jnp.tanh(h @ W_proj + b_proj)
        feat = jax.nn.relu(new_adj @ (h2 @ W_gcn) + b_gcn)
        return feat

    def _L2_ffn_ref(x, Wg, bg, bias, W1, b1, W2, b2):
        import jax, jax.numpy as jnp
        import numpy as np
        D_MODEL = 256
        EXPERT_DIM = 512
        NUM_EXPERTS = 8
        TOP_K = 2
        SEQ_LEN = 2048
        BATCH = 2
        x_flat = x.reshape(-1, D_MODEL)
        gate_logits = x_flat @ Wg + bg + bias
        topk_vals, topk_idx = jax.lax.top_k(gate_logits, TOP_K)
        topk_w = jax.nn.softmax(topk_vals, axis=-1)
        combine = (jax.nn.one_hot(topk_idx, NUM_EXPERTS, dtype=x.dtype) * topk_w[..., None]).sum(axis=1)
        h = jax.nn.relu(jnp.einsum('td,edh->teh', x_flat, W1) + b1)
        y = jnp.einsum('teh,ehd->ted', h, W2) + b2
        out = jnp.einsum('ted,te->td', y, combine)
        return out.reshape(x.shape)

    def _L3_gnn_ref(h, adj, Wm, al, ar):
        import jax, jax.numpy as jnp
        import numpy as np
        N = 4096
        IN = 256
        F = 64
        H = 4
        n = h.shape[0]
        ht = (h @ Wm).reshape(n, H, F)
        el = jnp.einsum('nhf,f->nh', ht, al)
        er = jnp.einsum('nhf,f->nh', ht, ar)
        scores = jax.nn.leaky_relu(el[:, :, None] + er.T[None, :, :], 0.2)
        scores = jnp.where(adj[:, None, :] == 0, -jnp.inf, scores)
        attn = jax.nn.softmax(scores, axis=-1)
        out = jnp.einsum('nhj,jhf->nhf', attn, ht)
        return out.reshape(n, H * F)

    def _L3_ffn_ref(x, sW1, sb1, sW2, sb2, sW3, sb3, eW1, eb1, eW2, eb2, eW3, eb3, gW, gb):
        import jax, jax.numpy as jnp
        import numpy as np
        B, A = (4096, 8)
        IN, OUT = (256, 256)
        SH1, SH2 = (256, 128)
        EH1, EH2 = (128, 64)
        E, TOPK = (4, 2)

        def _shared_mlp(x, W1, b1, W2, b2, W3, b3):
            h = jax.nn.relu(x @ W1 + b1)
            h = jax.nn.relu(h @ W2 + b2)
            return h @ W3 + b3

        def _experts_mlp(x, eW1, eb1, eW2, eb2, eW3, eb3):
            h = jax.nn.relu(jnp.einsum('baf,efh->ebah', x, eW1) + eb1[:, None, None, :])
            h = jax.nn.relu(jnp.einsum('ebah,ehg->ebag', h, eW2) + eb2[:, None, None, :])
            o = jnp.einsum('ebag,ego->ebao', h, eW3) + eb3[:, None, None, :]
            return jnp.moveaxis(o, 0, -1)
        all_out = _experts_mlp(x, eW1, eb1, eW2, eb2, eW3, eb3)
        shared = _shared_mlp(x, sW1, sb1, sW2, sb2, sW3, sb3)
        gates = jax.nn.softmax(x @ gW + gb, axis=-1)
        topv, topi = jax.lax.top_k(gates, TOPK)
        topw = jax.nn.softmax(topv, axis=-1)
        sel = jnp.take_along_axis(all_out, topi[:, :, None, :], axis=-1)
        gated = jnp.sum(sel * topw[:, :, None, :], axis=-1)
        return shared + gated

    x = x + _L0_gnn_ref(_layernorm(x, axis=-1), adj, L0_gnn_W)
    x = x + _L0_ffn_ref((_layernorm(x, axis=-1))[None], L0_ffn_router_w, L0_ffn_router_b, L0_ffn_W1, L0_ffn_b1, L0_ffn_W2, L0_ffn_b2)[0]
    x = x + _L1_gnn_ref(_layernorm(x, axis=-1), adj, L1_gnn_W1, L1_gnn_b1, L1_gnn_W2, L1_gnn_b2, L1_gnn_W3, L1_gnn_b3, L1_gnn_g1, L1_gnn_be1, L1_gnn_g2, L1_gnn_be2, L1_gnn_g3, L1_gnn_be3)
    x = x + _L1_ffn_ref((_layernorm(x, axis=-1))[None], L1_ffn_gate_w, L1_ffn_gate_b, L1_ffn_W1, L1_ffn_b1, L1_ffn_W2, L1_ffn_b2)[0]
    x = x + _L2_gnn_ref(_layernorm(x, axis=-1), adj, adj, L2_gnn_W_proj, L2_gnn_b_proj, L2_gnn_W_gcn, L2_gnn_b_gcn)
    x = x + _L2_ffn_ref((_layernorm(x, axis=-1))[None], L2_ffn_Wg, L2_ffn_bg, L2_ffn_bias, L2_ffn_W1, L2_ffn_b1, L2_ffn_W2, L2_ffn_b2)[0]
    x = x + _L3_gnn_ref(_layernorm(x, axis=-1), adj, L3_gnn_Wm, L3_gnn_al, L3_gnn_ar)
    x = x + _L3_ffn_ref((_layernorm(x, axis=-1))[None], L3_ffn_sW1, L3_ffn_sb1, L3_ffn_sW2, L3_ffn_sb2, L3_ffn_sW3, L3_ffn_sb3, L3_ffn_eW1, L3_ffn_eb1, L3_ffn_eW2, L3_ffn_eb2, L3_ffn_eW3, L3_ffn_eb3, L3_ffn_gW, L3_ffn_gb)[0]
    return x


_drawn_inputs = setup_inputs


def setup_inputs(seed=0):
    import zlib

    import numpy as np

    out = dict(_drawn_inputs(seed))
    spreads = {'L1_gnn_g1': (1.0, 0.6),
     'L1_gnn_be1': (0.0, 0.8),
     'L1_gnn_g2': (1.0, 0.6),
     'L1_gnn_be2': (0.0, 0.8),
     'L1_gnn_g3': (1.0, 0.6),
     'L1_gnn_be3': (0.0, 0.8),
     'L1_ffn_gate_b': (0.0, 0.8),
     'L1_ffn_b1': (0.0, 0.8),
     'L1_ffn_b2': (0.0, 0.8),
     'L2_gnn_b_proj': (0.0, 0.8),
     'L2_gnn_b_gcn': (0.0, 0.8),
     'L2_ffn_bias': (0.0, 0.8),
     'L3_ffn_sb1': (0.0, 0.8),
     'L3_ffn_sb2': (0.0, 2.0),
     'L3_ffn_sb3': (0.0, 2.0),
     'L3_ffn_eb1': (0.0, 0.8),
     'L3_ffn_eb2': (0.0, 2.0),
     'L3_ffn_eb3': (0.0, 2.0),
     'L3_ffn_gb': (0.0, 0.8)}
    factors = {'L0_ffn_router_w': 6.965,
     'L0_ffn_router_b': 8.0,
     'L0_ffn_W1': 8.0,
     'L0_ffn_b1': 8.0,
     'L0_ffn_W2': 6.959,
     'L0_ffn_b2': 8.0,
     'L1_gnn_b1': 8.0,
     'L1_gnn_b2': 8.0,
     'L1_gnn_b3': 8.0,
     'L1_ffn_gate_w': 8.0,
     'L1_ffn_W1': 8.0,
     'L1_ffn_W2': 8.0,
     'L2_gnn_W_proj': 6.563,
     'L2_gnn_W_gcn': 6.566,
     'L2_ffn_Wg': 8.0,
     'L2_ffn_bg': 8.0,
     'L2_ffn_W1': 8.0,
     'L2_ffn_b1': 8.0,
     'L2_ffn_W2': 8.0,
     'L2_ffn_b2': 33.845,
     'L3_gnn_al': 8.0,
     'L3_gnn_ar': 4.627,
     'L3_ffn_sW1': 7.846,
     'L3_ffn_sW2': 6.964,
     'L3_ffn_sW3': 5.941,
     'L3_ffn_eW1': 8.0,
     'L3_ffn_eW2': 8.0,
     'L3_ffn_eW3': 8.0,
     'L3_ffn_gW': 8.0}
    for name, (base, spread) in spreads.items():
        noise = np.random.default_rng([zlib.crc32(name.encode()), seed]).standard_normal(out[name].shape)
        drawn = base * np.exp(spread * noise) if base else spread * noise
        out[name] = jnp.asarray(drawn.astype(out[name].dtype))
    for name, factor in factors.items():
        out[name] = (out[name] * factor).astype(out[name].dtype)
    return out
```

```python
from contextlib import ExitStack

import numpy as np

import concourse.bass as bass
from concourse import mybir

F32 = mybir.dt.float32
F16 = mybir.dt.float16
ALU = mybir.AluOpType
ACT = mybir.ActivationFunctionType
AX = mybir.AxisListType

N = 2708
D = 256
P = 128
KT = -(-N // P)
NP = KT * P
FT = D // P
CH = 6
CW = 452
NC = CH * CW
HALF = NC // 2
CPH = CH // 2
LAST = N - (KT - 1) * P
RING = 4
STEPS = 2 * KT
LN_EPS = 1e-5
HEADS, HF = 4, 64
THIRD = 2 * CW
TOPK_ROWS = 700

E0, H0 = 32, 64
E1, H1 = 8, 512
E3 = 4

_COLS = {}
_at = 0
for _name, _n in (("L0_b1", 16), ("L1_b1", 32), ("L2_b1", 32), ("g1", 2), ("be1", 2), ("g2", 2), ("be2", 2),
                  ("g3", 2), ("be3", 2), ("gb1", 2), ("b_proj", 2), ("b_gcn", 2), ("sb1", 2), ("eb1", 4),
                  ("sb2", 1), ("eb2", 2)):
    _COLS[_name] = _at
    _at += _n
NCOLS = _at
_ROWS = {}
_at = 0
for _name, _n in (("router_b", E0), ("L1_b1", D), ("L1_b2", D), ("L1_b3", D), ("gate_b", E1), ("bg", E1),
                  ("bias", E1), ("gb", E3), ("sb3", D)):
    _ROWS[_name] = (_at, _n)
    _at += _n
NROWS = _at
WL = 1552
WB = WL // 4
W3 = {"sW1": 0, "sW2": 512, "sW3": 768, "eW1": 1024, "eW2": 2048, "eW3": 2560}
W3N = 4096
ST = 512


def build(nc, io, stop=99):
    ctx = ExitStack()
    with ctx:
        def sb(name, shape, dt=F32):
            return ctx.enter_context(nc.sbuf_tensor(name, shape, dt))

        nsem = [0]

        def sem(name):
            nsem[0] += 1
            return ctx.enter_context(nc.semaphore(name))

        xT = sb("xT", [P, FT, NP])
        R1 = sb("R1", [P, FT * NP])
        nT = R1[:, :].rearrange("p (f n) -> p f n", f=FT)
        XH = sb("XH", [P, FT, NP], F16)
        XL = sb("XL", [P, FT, NP], F16)
        R2 = sb("R2", [P, KT * D])
        HH = R2[:, 0:KT * P].bitcast(F16).rearrange("p (k d) -> p k d", k=KT)
        HL = R2[:, KT * P:KT * D].bitcast(F16).rearrange("p (k d) -> p k d", k=KT)
        BIG = sb("BIG", [P, 16768])
        pair = BIG[:, 0:RING * HALF].bitcast(F16).rearrange("p (r h n) -> p r h n", r=RING, h=2)
        a32 = BIG[:, RING * HALF:2 * RING * HALF].rearrange("p (r n) -> p r n", r=RING)
        dgb = BIG[:, 2 * RING * HALF:2 * RING * HALF + NP]
        cnt = BIG[:, 2 * RING * HALF + NP:2 * RING * HALF + NP + NC] 
        etmp = sb("etmp", [P, 2, CW])
        WH = sb("WH", [P, WL], F16)
        WLo = sb("WLo", [P, WL], F16)
        stage = sb("stage", [P, 2, ST])
        cwh = sb("cwh", [E0, NP], F16)
        cwl = sb("cwl", [E0, NP], F16)
        cols = sb("cols", [P, NCOLS])
        rowsf = BIG[0:1, 0:NROWS]
        rowh = sb("rowh", [1, NROWS], F16)
        rowl = sb("rowl", [1, NROWS], F16)
        b2f = BIG[0:E0, NROWS:NROWS + 4 * D]
        b2h = sb("b2h", [E0, 4, D], F16)
        b2l = sb("b2l", [E0, 4, D], F16)
        sel2 = sb("sel2", [E0, 16 * P], F16)
        sel8 = sb("sel8", [E1, E1 * P], F16)
        sel4f = sb("sel4f", [HEADS, HEADS * P])
        ident = sb("ident", [P, P])
        onesf = sb("onesf", [P, P])
        meanf = sb("meanf", [P, P])
        ones16 = sb("ones16", [1, 512], F16)
        rev = sb("rev", [P, E0])
        eps = sb("eps", [P, 1])
        dinv = sb("dinv", [P, KT])
        al_bc = sb("al_bc", [P, 2, D])
        sm = sb("sm", [P, 4, KT, 1])
        gv = sb("gv", [P, 5, KT * HEADS])
        gm = sb("gm", [P, 2, HEADS])
        ps = ctx.enter_context(nc.psum_tensor("ps", [P, 8, 512], F32))
        scratch = nc.dram_tensor("adj_split", (2, KT, P, 2, HALF), F16).ap()

        ln_d = R2[:, 0:4 * CW].rearrange("p (u f n) -> p u f n", u=2, f=FT)
        ln_sq = R2[:, 4 * CW:8 * CW].rearrange("p (u f n) -> p u f n", u=2, f=FT)
        ln_sd = R2[:, 8 * CW:10 * CW].rearrange("p (u n) -> p u n", u=2)
        LG = KT * E0
        lg = [R2[:, i * LG:(i + 1) * LG] for i in range(6)]
        hact = R1[:, 0:4 * CW].rearrange("p (t n) -> p t n", t=4)
        hwt = R1[:, 4 * CW:8 * CW].rearrange("p (t n) -> p t n", t=4)
        hh = R1[:, 8 * CW:10 * CW].bitcast(F16).rearrange("p (t n) -> p t n", t=4)
        hl = R1[:, 10 * CW:12 * CW].bitcast(F16).rearrange("p (t n) -> p t n", t=4)

        block = ctx.enter_context(nc.Block())

        def chunk(c, w=CW):
            return bass.DynSlice(c * CW, w) if not isinstance(c, int) else slice(c * CW, c * CW + w)

        def dyn(start, size):
            return slice(start, start + size) if isinstance(start, int) else bass.DynSlice(start, size)

        sems, counts = {}, {}

        class Stage:

            def __init__(self, kind, **totals):
                self.kind, self.base = kind, {}
                for n, total in totals.items():
                    key = (kind, n)
                    if key not in sems:
                        sems[key], counts[key] = sem(f"{kind}_{n}"), 0
                    self.base[n] = counts[key]
                    counts[key] += total
                self.totals = totals

            def __getitem__(self, n):
                return sems[self.kind, n]

            def at(self, n):
                return self.base[n]

            def end(self, n):
                return self[n], self.base[n] + self.totals[n]

        def after(eng, *stages):
            for st in stages:
                for s, v in st.done:
                    eng.wait_ge(s, v)

        def mm3(pe, out, ah, al, bh, bl, start=False, stop=False):
            pe.matmul(out, ah, bh, start=start, stop=False)
            pe.matmul(out, ah, bl, start=False, stop=False)
            return pe.matmul(out, al, bh, start=False, stop=stop)

        LC = Stage("const", ld=0, v=0)
        small = [(cols[:, :], "cols"), (rowsf[:, :], "rows"), (b2f[:, :], "b2"), (sel2[:, :], "sel2"),
                 (sel8[:, :], "sel8"), (sel4f[:, :], "sel4f"), (ident[:, :], "ident"), (rev[:, :], "rev"),
                 (ones16[:, :], "ones16"), (al_bc[:, :, :], "al"), (xT[:, :, :], "xT")]
        LC.done = [(LC["ld"], 16 * len(small)), (LC["v"], 9)]

        def const_sp(sp):
            for dst, name in small:
                sp.dma_start(dst, io[name]).then_inc(LC["ld"], 16)

        def const_dve(v):
            v.memset(onesf[:, :], 1.0).then_inc(LC["v"], 1)
            v.memset(meanf[:, :], 1.0 / D).then_inc(LC["v"], 1)
            v.memset(eps[:, :], LN_EPS).then_inc(LC["v"], 1)
            v.memset(XH[:, :, NC:NP], 0.0).then_inc(LC["v"], 1)
            v.memset(XL[:, :, NC:NP], 0.0).then_inc(LC["v"], 1)
            v.wait_ge(LC["ld"], 16 * len(small))
            v.tensor_copy(rowh[:, :], rowsf[:, :]).then_inc(LC["v"], 1)
            v.tensor_copy(b2h[:, :, :].rearrange("p a b -> p (a b)"), b2f[:, :]).then_inc(LC["v"], 1)
            v.wait_ge(LC["v"], 7)
            v.tensor_tensor(rowl[:, :], rowsf[:, :], rowh[:, :], ALU.subtract).then_inc(LC["v"], 1)
            v.tensor_tensor(b2l[:, :, :].rearrange("p a b -> p (a b)"), b2f[:, :],
                            b2h[:, :, :].rearrange("p a b -> p (a b)"), ALU.subtract).then_inc(LC["v"], 1)

        WS = Stage("w", ld0=0, ld1=0, hi=0, lo=0)
        wblocks = [0]

        class Split:
            def __init__(self, src, hi, lo, n, before, width=ST):
                self.src, self.hi, self.lo, self.n, self.before, self.width = src, hi, lo, n, before, width
                self.base = wblocks[0]
                wblocks[0] += n
                self.done = [(WS["lo"], wblocks[0] + 2)]

            def loop(self, eng, body):
                with eng.Fori(0, self.n // 2) as g:
                    for u in range(2):
                        body(2 * g + u, 2 * g + u + self.base, u, g + self.base // 2)

            def sp(self, sp):
                after(sp, *self.before)

                def body(b, m, u, turn):
                    sp.wait_ge(WS["lo"], m + 1)
                    sp.dma_start(stage[:, u, 0:self.width], self.src[:, dyn(b * self.width, self.width)]).then_inc(WS[f"ld{u}"], 16)
                self.loop(sp, body)

            def act(self, act):
                after(act, *self.before)

                def body(b, m, u, turn):
                    act.wait_ge(WS[f"ld{u}"], turn * 16 + 16)
                    act.activation(self.hi[:, dyn(b * self.width, self.width)], stage[:, u, 0:self.width], ACT.Copy).then_inc(WS["hi"], 1)
                self.loop(act, body)

            def pool(self, pool):
                after(pool, *self.before)

                def body(b, m, u, turn):
                    pool.wait_ge(WS["hi"], m + 1)
                    pool.tensor_tensor(self.lo[:, dyn(b * self.width, self.width)], stage[:, u, 0:self.width],
                                       self.hi[:, dyn(b * self.width, self.width)], ALU.subtract).then_inc(WS["lo"], 1)
                self.loop(pool, body)

        class LN:
            def __init__(self, name, src, before, gamma=None):
                self.st = Stage("ln", mean=CH, d=CH, sq=CH, var=CH, sd=CH, rs=CH, y=CH, g=CH * (gamma is not None),
                                hi=CH, lo=CH + 2)
                self.src, self.before, self.gamma = src, before, gamma
                self.done = [self.st.end("lo")]

            def stagger(self, eng, lead, follow):
                lead(0, 0)
                with eng.Fori(0, CH // 2 - 1) as g:
                    lead(2 * g + 1, 1)
                    follow(2 * g, 0)
                    lead(2 * g + 2, 0)
                    follow(2 * g + 1, 1)
                lead(CH - 1, 1)
                follow(CH - 2, 0)
                follow(CH - 1, 1)

            def pe(self, pe):
                after(pe, *self.before)
                s = self.st

                def mean(c, u):
                    for f in range(FT):
                        mm = pe.matmul(ps[:, u, 0:CW], meanf[:, :], self.src[:, f, chunk(c)],
                                       start=f == 0, stop=f == FT - 1)
                    mm.then_inc(s["mean"], 1)

                def var(c, u):
                    pe.wait_ge(s["sq"], s.at("sq") + c + 1)
                    for f in range(FT):
                        mm = pe.matmul(ps[:, 2 + u, 0:CW], meanf[:, :], ln_sq[:, u, f, :],
                                       start=f == 0, stop=f == FT - 1)
                    mm.then_inc(s["var"], 1)
                self.stagger(pe, mean, var)

            def dve(self, v):
                after(v, *self.before)
                s = self.st
                v.sem_inc(s["lo"], 2)

                def centre(c, u):
                    v.wait_ge(s["mean"], s.at("mean") + c + 1)
                    v.wait_ge(s["lo"], s.at("lo") + c + 1)
                    for f in range(FT):
                        op = v.tensor_tensor(ln_d[:, u, f, :], self.src[:, f, chunk(c)], ps[:, u, 0:CW],
                                             ALU.subtract)
                    op.then_inc(s["d"], 1)

                def scale(c, u):
                    v.wait_ge(s["sd"], s.at("sd") + c + 1)
                    v.reciprocal(ln_sd[:, u, :], ln_sd[:, u, :]).then_inc(s["rs"], 1)
                    v.wait_ge(s["rs"], s.at("rs") + c + 1)
                    for f in range(FT):
                        op = v.tensor_tensor(ln_d[:, u, f, :], ln_d[:, u, f, :], ln_sd[:, u, :], ALU.mult)
                    op.then_inc(s["y"], 1)
                    v.wait_ge(s["hi"], s.at("hi") + c + 1)
                    y = ln_d[:, u, :, :] if self.gamma is None else self.src[:, :, chunk(c)]
                    v.tensor_tensor(XL[:, :, chunk(c)], y, XH[:, :, chunk(c)], ALU.subtract).then_inc(s["lo"], 1)
                self.stagger(v, centre, scale)

            def act(self, act):
                after(act, *self.before)
                s = self.st

                def square(c, u):
                    act.wait_ge(s["d"], s.at("d") + c + 1)
                    act.activation(ln_sq[:, u, :, :], ln_d[:, u, :, :], ACT.Square).then_inc(s["sq"], 1)

                def finish(c, u):
                    act.wait_ge(s["var"], s.at("var") + c + 1)
                    act.activation(ln_sd[:, u, :], ps[:, 2 + u, 0:CW], ACT.Sqrt, bias=eps[:, 0:1])\
                       .then_inc(s["sd"], 1)
                    act.wait_ge(s["y"], s.at("y") + c + 1)
                    y = ln_d[:, u, :, :]
                    if self.gamma is not None:
                        g0, b0 = self.gamma
                        y = self.src[:, :, chunk(c)]
                        for f in range(FT):
                            op = act.activation(self.src[:, f, chunk(c)], ln_d[:, u, f, :], ACT.Identity,
                                                scale=cols[:, g0 + f:g0 + f + 1], bias=cols[:, b0 + f:b0 + f + 1])
                        op.then_inc(s["g"], 1)
                        act.wait_ge(s["g"], s.at("g") + c + 1)
                    act.activation(XH[:, :, chunk(c)], y, ACT.Copy).then_inc(s["hi"], 1)
                self.stagger(act, square, finish)

        class TokenLinear:
            def __init__(self, name, w, before, row=None, scaled=False):
                self.st = Stage("tok", mm=KT, hi=KT, lo=KT + 2)
                self.w, self.before, self.row, self.scaled = w, before, row, scaled
                self.done = [self.st.end("lo")]

            def loop(self, eng, body):
                with eng.Fori(0, KT // 2) as g:
                    for u in range(2):
                        body(2 * g + u, u)

            def pe(self, pe):
                after(pe, *self.before)
                pe.sem_inc(self.st["lo"], 2)

                def body(t, u):
                    out = ps[:, 4 + u, 0:D]
                    pe.wait_ge(self.st["lo"], self.st.at("lo") + t + 1)
                    for f in range(FT):
                        tok = dyn(t * P, P)
                        w = self.w + f * D
                        last = f == FT - 1 and self.row is None
                        mm = mm3(pe, out, XH[:, f, tok], XL[:, f, tok], WH[:, w:w + D], WLo[:, w:w + D],
                                 start=f == 0, stop=last)
                    if self.row is not None:
                        a, n = _ROWS[self.row]
                        pe.matmul(out, ones16[:, 0:P], rowh[:, a:a + n], start=False, stop=False)
                        mm = pe.matmul(out, ones16[:, 0:P], rowl[:, a:a + n], start=False, stop=True)
                    mm.then_inc(self.st["mm"], 1)
                self.loop(pe, body)

            def act(self, act):
                after(act, *self.before)

                def body(t, u):
                    act.wait_ge(self.st["mm"], self.st.at("mm") + t + 1)
                    sc = dinv[:, dyn(t, 1)] if self.scaled else 1.0
                    act.activation(HH[:, dyn(t, 1), :], ps[:, 4 + u:5 + u, 0:D], ACT.Identity if self.scaled else ACT.Copy,
                                   scale=sc).then_inc(self.st["hi"], 1)
                self.loop(act, body)

            def dve(self, v):
                after(v, *self.before)

                def body(t, u):
                    v.wait_ge(self.st["hi"], self.st.at("hi") + t + 1)
                    sc = dinv[:, dyn(t, 1)] if self.scaled else 1.0
                    v.scalar_tensor_tensor(HL[:, dyn(t, 1), :], ps[:, 4 + u:5 + u, 0:D], sc, HH[:, dyn(t, 1), :],
                                           ALU.mult, ALU.subtract).then_inc(self.st["lo"], 1)
                self.loop(v, body)

        class FeatLinear:
            def __init__(self, name, w, before, kind, bias=None):
                self.st = Stage("feat", mm=CH, t=CH * (kind == "tanh"), hi=CH * (kind == "tanh"), ev=CH + 2)
                self.w, self.before, self.kind, self.bias = w, before, kind, bias
                self.done = [self.st.end("ev")]

            def loop(self, eng, body):
                with eng.Fori(0, CH // 2) as g:
                    for u in range(2):
                        body(2 * g + u, u)

            def pe(self, pe):
                after(pe, *self.before)
                pe.sem_inc(self.st["ev"], 2)

                def body(c, u):
                    pe.wait_ge(self.st["ev"], self.st.at("ev") + c + 1)
                    for m in range(FT):
                        for f in range(FT):
                            w = self.w + f * D + m * P
                            mm = mm3(pe, ps[:, 2 * u + m, 0:CW], WH[:, w:w + P], WLo[:, w:w + P],
                                     XH[:, f, chunk(c)], XL[:, f, chunk(c)], start=f == 0, stop=f == FT - 1)
                    mm.then_inc(self.st["mm"], 1)
                self.loop(pe, body)

            def act(self, act):
                if self.kind == "add":
                    return
                after(act, *self.before)

                def body(c, u):
                    act.wait_ge(self.st["mm"], self.st.at("mm") + c + 1)
                    for m in range(FT):
                        b = cols[:, self.bias + m:self.bias + m + 1]
                        if self.kind == "nT":
                            op = act.activation(nT[:, m, chunk(c)], ps[:, 2 * u + m, 0:CW], ACT.Identity, bias=b)
                        else:
                            op = act.activation(ln_d[:, u, m, :], ps[:, 2 * u + m, 0:CW], ACT.Tanh, bias=b)
                    if self.kind == "nT":
                        op.then_inc(self.st["ev"], 1)
                        return
                    op.then_inc(self.st["t"], 1)
                    act.wait_ge(self.st["t"], self.st.at("t") + c + 1)
                    act.activation(XH[:, :, chunk(c)], ln_d[:, u, :, :], ACT.Copy).then_inc(self.st["hi"], 1)
                self.loop(act, body)

            def dve(self, v):
                if self.kind == "nT":
                    return
                after(v, *self.before)

                def body(c, u):
                    if self.kind == "add":
                        v.wait_ge(self.st["mm"], self.st.at("mm") + c + 1)
                        for m in range(FT):
                            x = xT[:, m, chunk(c)]
                            op = v.tensor_tensor(x, x, ps[:, 2 * u + m, 0:CW], ALU.add)
                    else:
                        v.wait_ge(self.st["hi"], self.st.at("hi") + c + 1)
                        op = v.tensor_tensor(XL[:, :, chunk(c)], ln_d[:, u, :, :], XH[:, :, chunk(c)], ALU.subtract)
                    op.then_inc(self.st["ev"], 1)
                self.loop(v, body)

        class Product:

            def __init__(self, name, kind, before):
                split, filt = kind == "split", kind == "filter"
                turns = 16 * (STEPS // RING)
                totals = dict(r=STEPS * filt, th=STEPS * filt, hi=STEPS * (split or filt), lo=STEPS * (split or filt),
                              cn=STEPS * split, dg=STEPS * split, z=split, zc=split, dmm=CH * split, dgc=CH * split,
                              rd=4 * split, used=STEPS, e1=2 * FT * CPH, ev=2 * FT * CPH)
                totals |= {f"a{u}": turns for u in range(RING)} | {f"st{u}": turns * split for u in range(RING)}
                self.st = Stage("prod", **totals)
                self.kind, self.before = kind, before
                self.done = [self.st.end("ev")]
                if split:
                    self.done += [self.st.end(f"st{u}") for u in range(RING)]

            def steps(self, eng, body, between=None, end=None):
                for n in range(RING):
                    body(n, n, n, 0, 0)
                with eng.Fori(1, 5) as g:
                    for u in range(RING):
                        body(RING * g + u, RING * g + u, u, g, 0)
                body(20, 20, 0, 5, 0)
                body(21, 21, 1, 5, 0)
                if between:
                    between(0)
                body(22, 0, 2, 5, 1)
                body(23, 1, 3, 5, 1)
                with eng.Fori(6, 10) as g:
                    for u in range(RING):
                        body(RING * g + u, RING * g + u - KT, u, g, 1)
                for u in range(RING):
                    body(40 + u, 40 + u - KT, u, 10, 1)
                if between:
                    between(1)

            def sp(self, sp):
                after(sp, *self.before)
                s = self.st

                def body(n, k, u, turn, h):
                    first = isinstance(n, int) and n < RING
                    if self.kind == "kept":
                        if not first:
                            sp.wait_ge(s["used"], s.at("used") + n - 3)
                        sp.dma_start(pair[:, u, :, :], scratch[h, k]).then_inc(s[f"a{u}"], 16)
                        return
                    if not first:
                        sp.wait_ge(s["lo"], s.at("lo") + n - 3)
                        if self.kind == "split":
                            sp.wait_ge(s["cn"], s.at("cn") + n - 3)
                            sp.wait_ge(s["dg"], s.at("dg") + n - 3)
                    sp.dma_start(a32[:, u, :], io["adjT"][dyn(k * P, P), h * HALF:(h + 1) * HALF])\
                      .then_inc(s[f"a{u}"], 16)
                self.steps(sp, body)

            def pe(self, pe):
                after(pe, *self.before)
                s = self.st

                def body(n, k, u, turn, h):
                    if self.kind == "kept":
                        pe.wait_ge(s[f"a{u}"], s.at(f"a{u}") + turn * 16 + 16)
                    else:
                        pe.wait_ge(s["lo"], s.at("lo") + n + 1)
                    start = isinstance(k, int) and k == 0
                    stop = isinstance(k, int) and k == KT - 1
                    for f in range(FT):
                        fs = slice(f * P, (f + 1) * P)
                        banks = [ps[:, (6 * h + f * CPH + c) % 8, 0:CW] for c in range(CPH)]
                        hi = [pair[:, u, 0, c * CW:(c + 1) * CW] for c in range(CPH)]
                        lo = [pair[:, u, 1, c * CW:(c + 1) * CW] for c in range(CPH)]
                        for c in range(CPH):
                            i = f * CPH + c
                            if start and h == 1:
                                if i >= 2:
                                    pe.wait_ge(s["ev"], s.at("ev") + i - 1)
                                elif self.kind == "split" and i == 0:
                                    pe.wait_ge(s["dgc"], s.at("dgc") + CPH)
                            pe.matmul(banks[c], HH[:, k, fs], hi[c], start=start, stop=False)
                            pe.matmul(banks[c], HH[:, k, fs], lo[c], start=False, stop=False)
                        for c in range(CPH):
                            mm = pe.matmul(banks[c], HL[:, k, fs], hi[c], start=False, stop=stop)
                    mm.then_inc(s["used"], 1)

                def degrees(h):
                    if self.kind != "split":
                        return
                    pe.wait_ge(s["dg"], s.at("dg") + KT * (h + 1))
                    for c in range(CPH):
                        if c == 2:
                            pe.wait_ge(s["dgc"], s.at("dgc") + CPH * h + 1)
                        col = h * HALF + c * CW
                        pe.matmul(ps[:, (6, 4)[h] + c % 2, 0:CW], onesf[:, :], dgb[:, col:col + CW],
                                  start=True, stop=True).then_inc(s["dmm"], 1)
                self.steps(pe, body, degrees)

            def act(self, act):
                if self.kind == "kept":
                    return
                after(act, *self.before)
                s = self.st

                def body(n, k, u, turn, h):
                    static = isinstance(n, int)
                    if self.kind == "split":
                        act.wait_ge(s[f"a{u}"], s.at(f"a{u}") + turn * 16 + 16)
                    else:
                        act.wait_ge(s["r"], s.at("r") + n + 1)
                        act.activation(a32[:, u, :], a32[:, u, :], ACT.Tanh).then_inc(s["th"], 1)
                        act.wait_ge(s["th"], s.at("th") + n + 1)
                    if not (static and n < RING):
                        act.wait_ge(s["used"], s.at("used") + n - 3)
                        if self.kind == "split":
                            act.wait_ge(s[f"st{u}"], s.at(f"st{u}") + turn * 16)
                    act.activation(pair[:, u, 0, :], a32[:, u, :], ACT.Copy).then_inc(s["hi"], 1)
                    if self.kind == "split":
                        act.wait_ge(s["lo"], s.at("lo") + n + 1)
                        act.dma_start(scratch[h, k], pair[:, u, :, :]).then_inc(s[f"st{u}"], 16)

                def relu(h):
                    if self.kind != "filter":
                        return
                    b0 = _COLS["b_gcn"]
                    act.wait_ge(s["used"], s.at("used") + KT * (h + 1))
                    for i in range(FT * CPH):
                        f = i // CPH
                        n = FT * CPH * h + i
                        if n >= 2:
                            act.wait_ge(s["ev"], s.at("ev") + n - 1)
                        act.activation(etmp[:, i % 2, :], ps[:, (6 * h + i) % 8, 0:CW], ACT.Relu,
                                       bias=cols[:, b0 + f:b0 + f + 1]).then_inc(s["e1"], 1)
                self.steps(act, body, relu)

            def pool(self, pool):
                if self.kind != "split":
                    return
                after(pool, *self.before)
                s = self.st
                pool.memset(dgb[:, :], 0.0).then_inc(s["z"], 1)
                pool.wait_ge(s["z"], s.at("z") + 1)

                def body(n, k, u, turn, h):
                    pool.wait_ge(s[f"a{u}"], s.at(f"a{u}") + turn * 16 + 16)
                    if not (isinstance(n, int) and n == 0):
                        pool.wait_ge(s["dg"], s.at("dg") + n)
                    d = dgb[:, h * HALF:(h + 1) * HALF]
                    pool.tensor_tensor(d, d, a32[:, u, :], ALU.add).then_inc(s["dg"], 1)
                self.steps(pool, body)

            def dve(self, v):
                after(v, *self.before)
                s = self.st
                if self.kind == "split":
                    v.memset(cnt, 0.0).then_inc(s["zc"], 1)
                    v.wait_ge(s["zc"], s.at("zc") + 1)

                def low(n, u):
                    v.wait_ge(s["hi"], s.at("hi") + n + 1)
                    v.tensor_tensor(pair[:, u, 1, :], a32[:, u, :], pair[:, u, 0, :], ALU.subtract)\
                     .then_inc(s["lo"], 1)

                def body(n, k, u, turn, h):
                    first = isinstance(n, int) and n == 0
                    if self.kind == "split":
                        v.wait_ge(s[f"a{u}"], s.at(f"a{u}") + turn * 16 + 16)
                        if not first:
                            v.wait_ge(s["cn"], s.at("cn") + n)
                        c = cnt[:, h * HALF:(h + 1) * HALF]
                        v.scalar_tensor_tensor(c, a32[:, u, :], 0.0, c, ALU.is_gt, ALU.add).then_inc(s["cn"], 1)
                        low(n, u)
                    elif self.kind == "filter":
                        v.wait_ge(s[f"a{u}"], s.at(f"a{u}") + turn * 16 + 16)
                        a = a32[:, u, :]
                        v.scalar_tensor_tensor(a, a, 0.0, a, ALU.max, ALU.mult).then_inc(s["r"], 1)
                        if not first and not (isinstance(n, int) and n == KT):
                            low(n - 1, (u - 1) % RING)

                def out(h):
                    if self.kind == "filter":
                        low(KT * (h + 1) - 1, (KT * (h + 1) - 1) % RING)
                    if self.kind == "split":
                        for c in range(CPH):
                            v.wait_ge(s["dmm"], s.at("dmm") + CPH * h + c + 1)
                            col = h * HALF + c * CW
                            v.tensor_copy(dgb[:, col:col + CW], ps[:, (6, 4)[h] + c % 2, 0:CW])\
                             .then_inc(s["dgc"], 1)
                        v.wait_ge(s["dgc"], s.at("dgc") + CPH * (h + 1))
                        rd = nT[:, 0, 0:HALF]
                        if h:
                            v.wait_ge(s["ev"], s.at("ev") + FT * CPH)
                        v.tensor_scalar(rd, dgb[:, h * HALF:(h + 1) * HALF], 1.0, None, ALU.add).then_inc(s["rd"], 1)
                        v.wait_ge(s["rd"], s.at("rd") + 2 * h + 1)
                        v.reciprocal(rd, rd).then_inc(s["rd"], 1)
                        v.wait_ge(s["rd"], s.at("rd") + 2 * h + 2)
                    v.wait_ge(s["used"], s.at("used") + KT * (h + 1))
                    for i in range(FT * CPH):
                        f, c = divmod(i, CPH)
                        n = FT * CPH * h + i
                        acc = ps[:, (6 * h + i) % 8, 0:CW]
                        col = slice(h * HALF + c * CW, h * HALF + (c + 1) * CW)
                        e = etmp[:, i % 2, :]
                        if self.kind == "filter":
                            v.wait_ge(s["e1"], s.at("e1") + n + 1)
                            v.tensor_tensor(xT[:, f, col], xT[:, f, col], e, ALU.add).then_inc(s["ev"], 1)
                            continue
                        by = nT[:, 0, c * CW:(c + 1) * CW] if self.kind == "split" else dgb[:, col]
                        if n >= 2:
                            v.wait_ge(s["ev"], s.at("ev") + n - 1)
                        v.tensor_tensor(e, acc, by, ALU.mult).then_inc(s["e1"], 1)
                        v.wait_ge(s["e1"], s.at("e1") + n + 1)
                        if self.kind == "split":
                            v.tensor_tensor(xT[:, f, col], xT[:, f, col], e, ALU.add).then_inc(s["ev"], 1)
                        else:
                            v.scalar_tensor_tensor(nT[:, f, col], e, 0.0, nT[:, f, col], ALU.max, ALU.add)\
                             .then_inc(s["ev"], 1)
                self.steps(v, body, out)

        class Dinv:
            def __init__(self, before):
                self.st = Stage("dinv", pad=1, sq=1, r=1, mm=1, ev=1)
                self.before = before
                self.done = [(self.st["ev"], 1)]

            def dve(self, v):
                after(v, *self.before)
                s = self.st
                v.memset(dgb[:, N:NP], 1.0).then_inc(s["pad"], 1)
                v.wait_ge(s["sq"], 1)
                v.reciprocal(dgb[:, :], dgb[:, :]).then_inc(s["r"], 1)
                v.wait_ge(s["mm"], 1)
                v.tensor_copy(dinv[:, :], ps[:, 7, 0:KT]).then_inc(s["ev"], 1)

            def act(self, act):
                act.wait_ge(self.st["pad"], 1)
                act.activation(dgb[:, :], dgb[:, :], ACT.Sqrt).then_inc(self.st["sq"], 1)

            def pe(self, pe):
                pe.wait_ge(self.st["r"], 1)
                for t in range(KT):
                    mm = pe.matmul(ps[:, 7, t:t + 1], dgb[0:1, t * P:(t + 1) * P], onesf[0:1, 0:1],
                                   start=True, stop=True)
                mm.then_inc(self.st["mm"], 1)

        gate_links = [0]

        class Gates:
            def __init__(self, name, E, w, rows, kind, before):
                self.groups = -(-KT // 4)
                self.st = Stage("gate", lg=KT, v=0, a={"argmax": 0, "softmax": 2, "top2": 2, "soft2": 4}[kind], cw=1,
                                tr=self.groups, hi=self.groups, lo=self.groups)
                self.E, self.w, self.rows, self.kind, self.before = E, w, rows, kind, before
                self.done = [self.st.end("lo")]

            def view(self, i, e=None):
                return lg[i][:, 0:KT * self.E].rearrange("p (t e) -> p t e", e=self.E)

            def pe(self, pe):
                after(pe, *self.before)
                s, E = self.st, self.E
                for b in range(2):
                    with pe.Fori(0, KT // 2) as g:
                        t = g + b * (KT // 2)
                        out = ps[:, b, dyn(g * E, E)]
                        for f in range(FT):
                            w = self.w + f * E
                            mm3(pe, out, XH[:, f, dyn(t * P, P)], XL[:, f, dyn(t * P, P)],
                                WH[:, w:w + E], WLo[:, w:w + E], start=f == 0, stop=False)
                        for i, r in enumerate(self.rows):
                            a, n = _ROWS[r]
                            pe.matmul(out, ones16[:, 0:P], rowh[:, a:a + n], start=False, stop=False)
                            mm = pe.matmul(out, ones16[:, 0:P], rowl[:, a:a + n], start=False,
                                           stop=i == len(self.rows) - 1)
                        mm.then_inc(s["lg"], 1)
                pe.wait_ge(s["cw"], s.at("cw") + 1)
                cw = self.view(5)
                for g in range(self.groups):
                    if g >= 2:
                        pe.wait_ge(s["lo"], s.at("lo") + g - 1)
                    ts = range(4 * g, min(4 * g + 4, KT))
                    for j, t in enumerate(ts):
                        mm = pe.transpose(ps[0:E, 2 + g % 2, j * P:(j + 1) * P], cw[:, t, :], ident[:, :])
                    mm.then_inc(s["tr"], 1)

            def act(self, act):
                s = self.st
                L, M = self.view(0), self.view(1)
                if self.kind in ("softmax", "soft2"):
                    act.wait_ge(s["a"], s.at("a") + 1)
                    act.activation(M, M, ACT.Exp).then_inc(s["a"], 1)
                if self.kind in ("top2", "soft2"):
                    act.wait_ge(s["a"], s.at("a") + 1 + 2 * (self.kind == "soft2"))
                    act.activation(sm[:, 3, :, :], sm[:, 3, :, :], ACT.Exp).then_inc(s["a"], 1)
                for g in range(self.groups):
                    n = min(4 * P, NP - 4 * P * g)
                    act.wait_ge(s["tr"], s.at("tr") + g + 1)
                    act.activation(cwh[0:self.E, 4 * P * g:4 * P * g + n], ps[0:self.E, 2 + g % 2, 0:n], ACT.Copy)\
                       .then_inc(s["hi"], 1)

            def dve(self, v):
                s, E = self.st, self.E
                shape = [P, KT, E]

                def link(op):
                    gate_links[0] += 1
                    op.then_inc(s["v"], 1)
                    v.wait_ge(s["v"], gate_links[0])

                after(v, *self.before)
                L, M, K1, K2, F1, C = (self.view(i) for i in range(6))
                hk = KT // 2
                v.wait_ge(s["lg"], s.at("lg") + KT)
                for b in range(2):
                    op = v.tensor_copy(L[:, b * hk:(b + 1) * hk, :],
                                       ps[:, b, 0:hk * E].rearrange("p (t e) -> p t e", e=E))
                link(op)

                def bc(x):
                    return x.to_broadcast(shape)

                def first_max(src, top, onehot):
                    link(v.tensor_reduce(top, src, AX.X, ALU.max))
                    link(v.tensor_tensor(K1, src, bc(top), ALU.is_equal))
                    link(v.tensor_tensor(K1, K1, rev[:, 0:E].rearrange("p (o e) -> p o e", o=1).to_broadcast(shape),
                                         ALU.mult))
                    link(v.tensor_reduce(sm[:, 2, :, :], K1, AX.X, ALU.max))
                    link(v.tensor_tensor(onehot, K1, bc(sm[:, 2, :, :]), ALU.is_equal))

                m1, m2 = sm[:, 0, :, :], sm[:, 1, :, :]
                if self.kind == "argmax":
                    first_max(L, m1, C)
                else:
                    if self.kind in ("softmax", "soft2"):
                        link(v.tensor_reduce(m1, L, AX.X, ALU.max))
                        link(v.tensor_tensor(M, L, bc(m1), ALU.subtract))
                        v.sem_inc(s["a"], 1)
                        v.wait_ge(s["a"], s.at("a") + 2)
                        link(v.tensor_reduce(sm[:, 3, :, :], M, AX.X, ALU.add))
                        link(v.reciprocal(sm[:, 3, :, :], sm[:, 3, :, :]))
                        link(v.tensor_tensor(L, M, bc(sm[:, 3, :, :]), ALU.mult))
                    first_max(L, m1, C)
                    link(v.scalar_tensor_tensor(M, C, -3.0e38, L, ALU.mult, ALU.add))
                    first_max(M, m2, F1)
                    if self.kind == "softmax":
                        link(v.tensor_tensor(C, C, F1, ALU.add))
                        link(v.tensor_tensor(C, C, L, ALU.mult))
                    else:
                        ex = sm[:, 3, :, :]
                        link(v.tensor_tensor(ex, m2, m1, ALU.subtract))
                        v.sem_inc(s["a"], 1)
                        v.wait_ge(s["a"], s.at("a") + 2 + 2 * (self.kind == "soft2"))
                        link(v.tensor_scalar(m1, ex, 1.0, None, ALU.add))
                        link(v.reciprocal(m1, m1))
                        link(v.tensor_tensor(m2, ex, m1, ALU.mult))
                        link(v.tensor_tensor(C, C, bc(m1), ALU.mult))
                        link(v.tensor_tensor(F1, F1, bc(m2), ALU.mult))
                        link(v.tensor_tensor(C, C, F1, ALU.add))
                v.sem_inc(s["cw"], 1)
                for g in range(self.groups):
                    n = min(4 * P, NP - 4 * P * g)
                    v.wait_ge(s["hi"], s.at("hi") + g + 1)
                    cs = slice(4 * P * g, 4 * P * g + n)
                    v.tensor_tensor(cwl[0:E, cs], ps[0:E, 2 + g % 2, 0:n], cwh[0:E, cs], ALU.subtract)\
                     .then_inc(s["lo"], 1)

        class FFN:
            def __init__(self, name, E, hid, b1, b2, func, before, relu_out=False):
                n = CH * (hid // P)
                self.st = Stage("ffn", hm=n, ha=n + 4, hw=n + 4, hi=n, lo=n + 4, yy=n + 4, yev=CH + 1)
                self.E, self.T, self.G = E, hid // P, hid // (4 * P)
                self.hid, self.b1, self.b2, self.func, self.before, self.relu_out = hid, b1, b2, func, before, relu_out
                self.done = [self.st.end("yev")]
                n = 4 * hid
                self.wh = BIG[:, 0:n // 2].bitcast(F16)
                self.wl = BIG[:, n // 2:n].bitcast(F16)
                self.nw = n

            def pe(self, pe):
                after(pe, *self.before)
                s, E, T = self.st, self.E, self.T
                W1h = self.wh[:, 0:2 * self.hid].rearrange("p (f h) -> p f h", f=FT)
                W1l = self.wl[:, 0:2 * self.hid].rearrange("p (f h) -> p f h", f=FT)
                W2h = self.wh[:, 2 * self.hid:].rearrange("p (t d) -> p t d", t=T)
                W2l = self.wl[:, 2 * self.hid:].rearrange("p (t d) -> p t d", t=T)
                pe.sem_inc(s["ha"], 4)
                pe.sem_inc(s["hw"], 4)
                pe.sem_inc(s["yy"], 4)
                pe.sem_inc(s["lo"], 4)
                pe.sem_inc(s["yev"], 1)
                with pe.Fori(0, CH) as c:
                    def h(g, t):
                        m = c * T + 4 * g + t
                        tile = 4 * g + t
                        pe.wait_ge(s["ha"], s.at("ha") + m + 1)
                        if E == E0:
                            pe.wait_ge(s["hw"], s.at("hw") + m + 3)
                        elif t % 2 == 0:
                            pe.wait_ge(s["hw"], s.at("hw") + m + 2)
                        for f in range(FT):
                            w = dyn(tile * P, P)
                            mm = mm3(pe, ps[:, t, 0:CW], W1h[:, f, w], W1l[:, f, w],
                                     XH[:, f, chunk(c)], XL[:, f, chunk(c)], start=f == 0, stop=f == FT - 1)
                        if E == E0:
                            mm = pe.matmul(ps[:, 6 + t % 2, 0:CW], sel2[:, dyn(tile * P, P)], cwh[:, chunk(c)],
                                           start=True, stop=True)
                        elif t % 2 == 0:
                            for i, cw in enumerate((cwh, cwl)):
                                mm = pe.matmul(ps[:, 6 + t // 2, 0:CW], sel8[:, dyn(g * P, P)], cw[0:E, chunk(c)],
                                               start=i == 0, stop=i == 1)
                        mm.then_inc(s["hm"], 1)

                    def y(g, t, stop=False):
                        m = c * T + 4 * g + t
                        pe.wait_ge(s["lo"], s.at("lo") + m + 5)
                        for f in range(FT):
                            fs = slice(f * P, (f + 1) * P)
                            mm = mm3(pe, ps[:, 4 + f, 0:CW], W2h[:, 4 * g + t, fs], W2l[:, 4 * g + t, fs],
                                     hh[:, t, :], hl[:, t, :], stop=stop)
                        mm.then_inc(s["yy"], 1)

                    h(0, 0)
                    pe.wait_ge(s["yev"], s.at("yev") + c + 1)
                    h(0, 1)
                    for f in range(FT):
                        fs = slice(f * P, (f + 1) * P)
                        mm3(pe, ps[:, 4 + f, 0:CW], b2h[0:E, self.b2, fs], b2l[0:E, self.b2, fs],
                            cwh[0:E, chunk(c)], cwl[0:E, chunk(c)], start=True)
                    with pe.Fori(0, self.G - 1) as g:
                        h(g, 2)
                        y(g, 0)
                        h(g, 3)
                        y(g, 1)
                        h(g + 1, 0)
                        y(g, 2)
                        h(g + 1, 1)
                        y(g, 3)
                    g = self.G - 1
                    h(g, 2)
                    y(g, 0)
                    h(g, 3)
                    y(g, 1)
                    y(g, 2)
                    y(g, 3, True)

            def act(self, act):
                after(act, *self.before)
                s, T = self.st, self.T
                with act.Fori(0, CH) as c:
                    with act.Fori(0, self.G) as g:
                        for t in range(4):
                            m = c * T + 4 * g + t
                            act.wait_ge(s["hm"], s.at("hm") + m + 1)
                            act.wait_ge(s["hw"], s.at("hw") + m + 1)
                            act.activation(hact[:, t, :], ps[:, t, 0:CW], self.func,
                                           bias=cols[:, dyn(self.b1 + 4 * g + t, 1)]).then_inc(s["ha"], 1)
                            act.wait_ge(s["hw"], s.at("hw") + m + 5)
                            act.wait_ge(s["yy"], s.at("yy") + m + 1)
                            act.activation(hh[:, t, :], hwt[:, t, :], ACT.Copy).then_inc(s["hi"], 1)

            def dve(self, v):
                after(v, *self.before)
                s, T = self.st, self.T
                with v.Fori(0, CH) as c:
                    with v.Fori(0, self.G) as g:
                        for t in range(4):
                            m = c * T + 4 * g + t
                            bank = 6 + (t % 2 if self.E == E0 else t // 2)
                            v.wait_ge(s["ha"], s.at("ha") + m + 5)
                            v.wait_ge(s["lo"], s.at("lo") + m + 1)
                            v.tensor_tensor(hwt[:, t, :], hact[:, t, :], ps[:, bank, 0:CW], ALU.mult)\
                             .then_inc(s["hw"], 1)
                            v.wait_ge(s["hi"], s.at("hi") + m + 1)
                            v.tensor_tensor(hl[:, t, :], hwt[:, t, :], hh[:, t, :], ALU.subtract)\
                             .then_inc(s["lo"], 1)
                    v.wait_ge(s["yy"], s.at("yy") + c * T + T + 4)
                    for f in range(FT):
                        x = xT[:, f, chunk(c)]
                        if self.relu_out:
                            op = v.scalar_tensor_tensor(x, ps[:, 4 + f, 0:CW], 0.0, x, ALU.max, ALU.add)
                        else:
                            op = v.tensor_tensor(x, x, ps[:, 4 + f, 0:CW], ALU.add)
                    op.then_inc(s["yev"], 1)

        class GAT:
            def __init__(self, name, before):
                self.st = Stage("gat", fr=0, mm=0, ht=0, v=0, mx=0, ar=0, e=0, ex=0, tr=0, qt=0, qmm=0, qb=0, a0=0, a1=0, mk=0, pp=0, gg=0, used=0, ev=0)
                self.before = before
                self.done = [(self.st["ev"], 3)]

            ht = R1[:, :].rearrange("p (t d) -> p t d", t=KT)
            prod = R2[:, :].rearrange("p (t d) -> p t d", t=KT)
            QT = R2[0:HEADS, 0:NP]
            inv = R2[:, NP:NP + THIRD].rearrange("p (c n) -> p c n", c=2)
            num = R2[:, NP + THIRD:NP + 2 * THIRD].rearrange("p (c n) -> p c n", c=2)
            Qb = BIG[:, 0:4 * THIRD].rearrange("p (h n) -> p h n", h=HEADS)
            PT = BIG[:, 4 * THIRD:12 * THIRD].rearrange("p (u h n) -> p u h n", u=2, h=HEADS)
            A = BIG[:, 12 * THIRD:14 * THIRD].rearrange("p (u n) -> p u n", u=2)
            MK = BIG[:, 14 * THIRD:16 * THIRD].rearrange("p (u n) -> p u n", u=2)
            G = BIG[:, 16 * THIRD:16 * THIRD + 1024].rearrange("p (u n) -> p u n", u=2)

            def tiles(self, eng, body):
                with eng.Fori(0, KT // 2) as g:
                    for u in range(2):
                        body(2 * g + u, u)

            def steps(self, eng, x, body):
                n0 = KT * x
                for u in range(2):
                    body(n0 + u, u, u, n0 // 2)
                with eng.Fori(1, KT // 2 - 1) as g:
                    for u in range(2):
                        body(2 * g + u + n0, 2 * g + u, u, g + n0 // 2)
                for u in range(2):
                    body(n0 + KT - 2 + u, KT - 2 + u, u, n0 // 2 + KT // 2 - 1)

            def sp(self, sp):
                after(sp, *self.before)
                s = self.st
                for x in range(3):
                    def body(n, k, u, turn):
                        if not (isinstance(n, int) and n < 2):
                            sp.wait_ge(s["mk"], n - 1)
                        sp.dma_start(self.A[:, u, :], io["adjT"][dyn(k * P, P), x * THIRD:(x + 1) * THIRD])\
                          .then_inc(s[f"a{u}"], 16)
                    self.steps(sp, x, body)

            def pe(self, pe):
                after(pe, *self.before)
                s = self.st
                pe.sem_inc(s["fr"], 2)

                def body(t, u):
                    pe.wait_ge(s["fr"], t + 1)
                    for f in range(FT):
                        mm = mm3(pe, ps[:, 4 + u, 0:D], XH[:, f, dyn(t * P, P)], XL[:, f, dyn(t * P, P)],
                                 WH[:, f * D:f * D + D], WLo[:, f * D:f * D + D], start=f == 0, stop=f == FT - 1)
                    mm.then_inc(s["mm"], 1)
                self.tiles(pe, body)
                q = gv[:, 4, :].rearrange("p (t h) -> p t h", h=HEADS)
                pe.wait_ge(s["ex"], 3)
                for g in range(6):
                    if g >= 2:
                        pe.wait_ge(s["qt"], g - 1)
                    for j, t in enumerate(range(4 * g, min(4 * g + 4, KT))):
                        mm = pe.transpose(ps[0:HEADS, g % 2, j * P:(j + 1) * P], q[:, t, :], ident[:, :])
                    mm.then_inc(s["tr"], 1)
                for x in range(3):
                    pe.wait_ge(s["qt"], 6)
                    if x:
                        pe.wait_ge(s["ev"], x)
                    for h in range(HEADS):
                        for c in range(2):
                            col = x * THIRD + c * CW
                            mm = pe.matmul(ps[:, 2 * h + c, 0:CW], sel4f[:, h * P:(h + 1) * P],
                                           self.QT[:, col:col + CW], start=True, stop=True)
                    mm.then_inc(s["qmm"], 1)
                    pe.wait_ge(s["qb"], x + 1)

                    def body(n, k, u, turn):
                        pe.wait_ge(s["pp"], n + 1)
                        pe.wait_ge(s["gg"], n + 1)
                        start, stop = isinstance(k, int) and k == 0, isinstance(k, int) and k == KT - 1
                        for h in range(HEADS):
                            for c in range(2):
                                mm = pe.matmul(ps[:, 2 * h + c, 0:CW], self.G[:, u, h * P:(h + 1) * P],
                                               self.PT[:, u, h, c * CW:(c + 1) * CW], start=start, stop=stop)
                        mm.then_inc(s["used"], 1)
                    self.steps(pe, x, body)

            def act(self, act):
                after(act, *self.before)
                s = self.st

                def body(t, u):
                    act.wait_ge(s["mm"], t + 1)
                    act.activation(self.ht[:, dyn(t, 1), :], ps[:, 4 + u:5 + u, 0:D], ACT.Copy).then_inc(s["fr"], 1)
                self.tiles(act, body)
                act.wait_ge(s["e"], 1)
                act.activation(gv[:, 2, :], gv[:, 1, :], ACT.Exp, scale=0.8).then_inc(s["ex"], 1)
                act.activation(gv[:, 3, :], gv[:, 1, :], ACT.Exp, scale=0.2).then_inc(s["ex"], 1)
                act.activation(gv[:, 4, :], gv[:, 0, :], ACT.Exp).then_inc(s["ex"], 1)
                for g in range(6):
                    n = min(4 * P, NP - 4 * P * g)
                    act.wait_ge(s["tr"], g + 1)
                    act.activation(self.QT[:, 4 * P * g:4 * P * g + n], ps[0:HEADS, g % 2, 0:n], ACT.Copy)\
                       .then_inc(s["qt"], 1)
                act.wait_ge(s["ex"], 3)
                zp = gv[:, 3, :]
                for x in range(3):
                    act.wait_ge(s["qmm"], x + 1)
                    if x:
                        act.wait_ge(s["pp"], KT * x)
                    act.activation(self.Qb.rearrange("p h (c n) -> p (h c) n", c=2), ps[:, :, 0:CW], ACT.Copy)\
                       .then_inc(s["qb"], 1)

                    def body(n, k, u, turn):
                        if not (isinstance(n, int) and n < 2):
                            act.wait_ge(s["used"], n - 1)
                        for h in range(HEADS):
                            z = zp[:, dyn(HEADS * k + h, 1)]
                            a, b = (h * P, h * P + HF) if h % 2 == 0 else (h * P + HF, h * P)
                            act.activation(self.G[:, u:u + 1, a:a + HF], self.ht[:, dyn(k, 1), h * HF:(h + 1) * HF],
                                           ACT.Copy, scale=z)
                            op = act.activation(self.G[:, u, b:b + HF], onesf[:, 0:HF], ACT.Copy, scale=z)
                        op.then_inc(s["gg"], 1)
                    self.steps(act, x, body)

            def pool(self, pool):
                s = self.st
                pool.wait_ge(s["mx"], 1)
                pool.partition_all_reduce(gm[:, 1, :], gm[:, 0, :], P, bass.bass_isa.ReduceOp.max).then_inc(s["ar"], 1)

            def dve(self, v):
                s = self.st
                links = [0]

                def link(op):
                    links[0] += 1
                    op.then_inc(s["v"], 1)
                    v.wait_ge(s["v"], links[0])

                after(v, *self.before)
                v.wait_ge(s["fr"], KT + 2)
                for i in range(2):
                    w = al_bc[:, i, :].rearrange("p (o d) -> p o d", o=1).to_broadcast([P, KT, D])
                    link(v.tensor_tensor(self.prod, self.ht, w, ALU.mult))
                    link(v.tensor_reduce(gv[:, i, :], self.prod.rearrange("p t (h f) -> p (t h) f", h=HEADS),
                                         AX.X, ALU.add))
                er = gv[:, 1, :].rearrange("p (t h) -> p h t", h=HEADS)
                link(v.tensor_reduce(gm[:, 0, :], er[:, :, 0:KT - 1], AX.X, ALU.max))
                v.tensor_tensor(gm[0:LAST, 0, :], gm[0:LAST, 0, :], gv[0:LAST, 1, HEADS * (KT - 1):HEADS * KT],
                                ALU.max).then_inc(s["mx"], 1)
                v.wait_ge(s["ar"], 1)
                M = gm[:, 1, :].rearrange("p (o h) -> p o h", o=1).to_broadcast([P, KT, HEADS])
                el3 = gv[:, 0, :].rearrange("p (t h) -> p t h", h=HEADS)
                er3 = gv[:, 1, :].rearrange("p (t h) -> p t h", h=HEADS)
                link(v.tensor_tensor(el3, el3, M, ALU.add))
                link(v.tensor_scalar(gv[:, 0, :], gv[:, 0, :], -0.8, 0.0, ALU.mult, ALU.min))
                link(v.tensor_tensor(er3, er3, M, ALU.subtract))
                v.sem_inc(s["e"], 1)
                v.wait_ge(s["ex"], 3)
                Z = gv[:, 2, :]
                for x in range(3):
                    v.wait_ge(s["qb"], x + 1)

                    def body(n, k, u, turn):
                        v.wait_ge(s[f"a{u}"], turn * 16 + 16)
                        if not (isinstance(n, int) and n < 2):
                            v.wait_ge(s["used"], n - 1)
                        v.tensor_scalar(self.MK[:, u, :], self.A[:, u, :], 0.0, None, ALU.not_equal)\
                         .then_inc(s["mk"], 1)
                        v.wait_ge(s["mk"], n + 1)
                        for h in range(HEADS):
                            op = v.scalar_tensor_tensor(self.PT[:, u, h, :], self.Qb[:, h, :],
                                                        Z[:, dyn(HEADS * k + h, 1)], self.MK[:, u, :],
                                                        ALU.max, ALU.mult)
                        op.then_inc(s["pp"], 1)
                    self.steps(v, x, body)
                    v.wait_ge(s["used"], KT * (x + 1))
                    for h in range(HEADS):
                        fr, dr = (slice(0, HF), slice(HF, P)) if h % 2 == 0 else (slice(HF, P), slice(0, HF))
                        acc = ps[:, 2 * h:2 * h + 2, 0:CW]
                        xs = xT[fr, h // 2, x * THIRD:(x + 1) * THIRD].rearrange("p (c n) -> p c n", c=2)
                        inv, num = self.inv[fr], self.num[fr]
                        link(v.tensor_scalar(inv, acc[dr], 1e-37, None, ALU.max))
                        link(v.reciprocal(inv, inv))
                        link(v.tensor_tensor(num, acc[fr], inv, ALU.mult))
                        link(v.tensor_tensor(xs, xs, num, ALU.add))
                    v.sem_inc(s["ev"], 1)

        class FFN3:
            def __init__(self, name, before):
                self.st = Stage("last", bc=0, hm=0, ha=0, hw=0, hi=0, lo=0, yd=0, ev=0)
                self.before = before
                self.done = [(self.st["ev"], CH + 1)]

            a = BIG[:, W3N:W3N + 9 * CW].rearrange("p (t n) -> p t n", t=9)
            hi = BIG[:, W3N + 9 * CW:W3N + 9 * CW + 9 * CW // 2].bitcast(F16).rearrange("p (t n) -> p t n", t=9)
            lo = BIG[:, W3N + 9 * CW + 9 * CW // 2:W3N + 18 * CW].bitcast(F16).rearrange("p (t n) -> p t n", t=9)
            hwx = BIG[:, W3N + 18 * CW:W3N + 20 * CW].rearrange("p (t n) -> p t n", t=2)
            wh = BIG[:, 0:W3N // 2].bitcast(F16)
            wl = BIG[:, W3N // 2:W3N].bitcast(F16)
            bank = [0, 1, 2, 3, 4, 5, 0, 1, 2]

            def bias(self, i):
                name, o = (("sb1", i) if i < 2 else ("eb1", i - 2) if i < 6 else ("sb2", 0) if i == 6
                           else ("eb2", i - 7))
                return cols[:, _COLS[name] + o:_COLS[name] + o + 1]

            def pe(self, pe):
                after(pe, *self.before)
                s, wh, wl = self.st, self.wh, self.wl
                pe.sem_inc(s["ev"], 1)
                with pe.Fori(0, CH) as c:
                    pe.wait_ge(s["ev"], c + 1)
                    X = [(XH[:, f, chunk(c)], XL[:, f, chunk(c)]) for f in range(FT)]
                    H = [(self.hi[:, t, :], self.lo[:, t, :]) for t in range(9)]

                    def tile(i, terms, out=None, inc=True, start=True, stop=True):
                        out = ps[:, self.bank[i], 0:CW] if out is None else out
                        for n, (at, (bh, bl)) in enumerate(terms):
                            mm = mm3(pe, out, wh[:, at:at + P], wl[:, at:at + P], bh, bl,
                                     start=start and n == 0, stop=stop and n == len(terms) - 1)
                        if inc:
                            mm.then_inc(s["hm"], 1)
                        return mm

                    for i in range(2):
                        tile(i, [(W3["sW1"] + f * D + i * P, X[f]) for f in range(FT)])
                    for e in range(4):
                        tile(2 + e, [(W3["eW1"] + f * 512 + e * P, X[f]) for f in range(FT)])
                    pe.wait_ge(s["lo"], c * 9 + 2)
                    pe.wait_ge(s["ha"], c * 9 + 1)
                    tile(6, [(W3["sW2"] + f * P, H[f]) for f in range(FT)])
                    for p in range(2):
                        pe.wait_ge(s["lo"], c * 9 + 4 + 2 * p)
                        tile(7 + p, [(W3["eW2"] + e * P, H[2 + e]) for e in (2 * p, 2 * p + 1)])
                    for p in range(2):
                        for i, cw in enumerate((cwh, cwl)):
                            mm = pe.matmul(ps[:, 3 + p, 0:CW], sel2[0:E3, p * P:(p + 1) * P], cw[0:E3, chunk(c)],
                                           start=i == 0, stop=i == 1)
                    mm.then_inc(s["bc"], 1)
                    for f in range(FT):
                        out, fs = ps[:, 6 + f, 0:CW], slice(f * P, (f + 1) * P)
                        mm3(pe, out, b2h[0:E3, 3, fs], b2l[0:E3, 3, fs], cwh[0:E3, chunk(c)], cwl[0:E3, chunk(c)],
                            start=True)
                        a = _ROWS["sb3"][0] + f * P
                        pe.matmul(out, rowh[:, a:a + P], ones16[:, 0:CW], start=False, stop=False)
                        pe.matmul(out, rowl[:, a:a + P], ones16[:, 0:CW], start=False, stop=False)
                    pe.wait_ge(s["lo"], c * 9 + 9)
                    for f in range(FT):
                        mm = tile(0, [(W3["sW3"] + f * P, H[6])] + [(W3["eW3"] + p * D + f * P, H[7 + p]) for p in range(2)],
                                  out=ps[:, 6 + f, 0:CW], inc=False, start=False)
                    mm.then_inc(s["yd"], 1)

            def act(self, act):
                after(act, *self.before)
                s = self.st
                with act.Fori(0, CH) as c:
                    for i in range(9):
                        act.wait_ge(s["hm"], c * 9 + i + 1)
                        act.activation(self.a[:, i, :], ps[:, self.bank[i], 0:CW], ACT.Relu, bias=self.bias(i))\
                           .then_inc(s["ha"], 1)
                        if i < 7:
                            act.wait_ge(s["ha"], c * 9 + i + 1)
                            src = self.a[:, i, :]
                        else:
                            act.wait_ge(s["hw"], c * 2 + i - 6)
                            src = self.hwx[:, i - 7, :]
                        act.activation(self.hi[:, i, :], src, ACT.Copy).then_inc(s["hi"], 1)

            def dve(self, v):
                after(v, *self.before)
                s = self.st
                with v.Fori(0, CH) as c:
                    for i in range(9):
                        src = self.a[:, i, :]
                        if i >= 7:
                            v.wait_ge(s["ha"], c * 9 + i + 1)
                            v.wait_ge(s["bc"], c + 1)
                            src = self.hwx[:, i - 7, :]
                            v.tensor_tensor(src, self.a[:, i, :], ps[:, 3 + i - 7, 0:CW], ALU.mult).then_inc(s["hw"], 1)
                        v.wait_ge(s["hi"], c * 9 + i + 1)
                        v.tensor_tensor(self.lo[:, i, :], src, self.hi[:, i, :], ALU.subtract).then_inc(s["lo"], 1)
                    v.wait_ge(s["yd"], c + 1)
                    for f in range(FT):
                        x = xT[:, f, chunk(c)]
                        op = v.tensor_tensor(x, x, ps[:, 6 + f, 0:CW], ALU.add)
                    op.then_inc(s["ev"], 1)

        plan = []

        def add(stage):
            plan.append(stage)
            return stage

        B = [LC]
        w = add(Split(io["w0"], WH, WLo, WL // WB, [LC], WB))
        last = [w, LC]

        def go(cls, name, *args, **kw):
            nonlocal last
            st = add(cls(name, *args, before=last, **kw))
            last = [st]
            return st

        def finished(i):
            return stop <= i

        def ffn_layer(i, E, hid, gw, rows, kind, func, wname, b1, b2, relu_out=False):
            nonlocal last
            ln = go(LN, f"ln{i}b", xT)
            f = FFN(f"ffn{i}", E, hid, b1, b2, func, last, relu_out)
            sp = add(Split(io[wname], f.wh, f.wl, f.nw // ST, [ln]))
            last = [ln]
            gts = add(Gates(f"gate{i}", E, gw, rows, kind, before=[ln]))
            f.before = [gts, sp]
            add(f)
            last = [f]

        def small_weights(i):
            nonlocal last
            w = add(Split(io[f"w{i}"], WH, WLo, WL // WB, last, WB))
            last = [w] + last

        def network():
            nonlocal last
            go(LN, "ln0a", xT)
            go(TokenLinear, "tl0", 2 * D)
            go(FeatLinear, "fl0", 0, kind="add")
            go(Product, "pr0", "split")
            if stop == 0:
                return
            st = add(Dinv(last))
            last = [st] + last
            ffn_layer(0, E0, E0 * H0, 4 * D, ["router_b"], "argmax", ACT.Relu, "f0", _COLS["L0_b1"], 0, True)
            if stop == 1:
                return
            small_weights(1)
            go(LN, "ln1a", xT)
            go(TokenLinear, "tl1a", 0, row="L1_b1", scaled=True)
            go(FeatLinear, "fl1", 0, kind="nT", bias=_COLS["gb1"])
            for i in range(3):
                go(Product, f"pr1{i}", "kept")
                go(LN, f"ln1n{i}", nT, gamma=(_COLS[f"g{i + 1}"], _COLS[f"be{i + 1}"]))
                if i < 2:
                    go(TokenLinear, f"tl1{'bc'[i]}", 2 * D * (i + 1), row=f"L1_b{i + 2}", scaled=True)
            go(AddN, "addn")
            if stop == 2:
                return
            ffn_layer(1, E1, E1 * H1, 6 * D, ["gate_b"], "softmax", ACT.Gelu, "f1", _COLS["L1_b1"], 1)
            if stop == 3:
                return
            small_weights(2)
            go(LN, "ln2a", xT)
            go(FeatLinear, "fl2", 0, kind="tanh", bias=_COLS["b_proj"])
            go(TokenLinear, "tl2", 2 * D)
            go(Product, "pr2", "filter")
            if stop == 4:
                return
            ffn_layer(2, E1, E1 * H1, 4 * D, ["bg", "bias"], "top2", ACT.Relu, "f2", _COLS["L2_b1"], 2)
            if stop == 5:
                return
            small_weights(3)
            go(LN, "ln3a", xT)
            gat = go(GAT, "gat")
            if stop == 6:
                return
            ln = go(LN, "ln3b", xT)
            sp = add(Split(io["f3"], BIG[:, 0:W3N // 2].bitcast(F16), BIG[:, W3N // 2:W3N].bitcast(F16), W3N // ST, [ln]))
            gts = add(Gates("gate3", E3, 2 * D, ["gb"], "soft2", before=[ln]))
            last = [gts, sp]
            go(FFN3, "ffn3")

        class AddN:

            def __init__(self, name, before):
                self.st, self.before = Stage("addn", v=1), before
                self.done = [(self.st["v"], 1)]

            def dve(self, v):
                after(v, *self.before)
                v.tensor_tensor(xT[:, :, 0:NC], xT[:, :, 0:NC], nT[:, :, 0:NC], ALU.add).then_inc(self.st["v"], 1)

        network()
        out_done = sem("out_done")

        def run(eng, part):
            for st in plan:
                if part in dir(st):
                    {"sp": lambda: st.sp(eng), "act": lambda: st.act(eng), "pe": lambda: st.pe(eng),
                     "dve": lambda: st.dve(eng), "pool": lambda: st.pool(eng)}[part]()

        @block.sync
        def _(sp):
            sp.sem_inc(WS["lo"], 2)
            const_sp(sp)
            run(sp, "sp")
            after(sp, *last)
            sp.dma_start(io["out"], xT[:, :, 0:NC]).then_inc(out_done, 16)
            sp.wait_ge(out_done, 16)

        @block.scalar
        def _(act):
            run(act, "act")

        @block.vector
        def _(v):
            const_dve(v)
            run(v, "dve")

        @block.gpsimd
        def _(pool):
            run(pool, "pool")

        @block.tensor
        def _(pe):
            run(pe, "pe")


def _lay(w, tiles):
    w = np.asarray(w)
    return np.ascontiguousarray(w.reshape(tiles, P, -1).transpose(1, 0, 2).reshape(P, -1))


def _pad(a, cols):
    return np.concatenate([a, np.zeros((a.shape[0], cols - a.shape[1]), a.dtype)], axis=1)


def _column(v):
    return np.asarray(v).reshape(-1, P).T


def layout(i):
    i = {k: np.asarray(v) for k, v in i.items()}
    f32 = np.float32
    a = {}
    xT = np.zeros((D, NP), f32)
    xT[:, :N] = i["x"].T
    a["xT"] = np.ascontiguousarray(xT.reshape(FT, P, NP).transpose(1, 0, 2))
    adjT = np.zeros((NP, NC), f32)
    adjT[:N, :N] = i["adj"].T
    a["adjT"] = adjT
    g = i["L0_gnn_W"].T
    a["w0"] = _pad(np.concatenate([_lay(g[:D], 2), _lay(g[D:], 2), _lay(i["L0_ffn_router_w"].T, 2)], 1), WL)
    a["w1"] = _pad(np.concatenate([_lay(i[f"L1_gnn_W{n}"], 2) for n in (1, 2, 3)] + [_lay(i["L1_ffn_gate_w"], 2)], 1), WL)
    a["w2"] = _pad(np.concatenate([_lay(i["L2_gnn_W_proj"], 2), _lay(i["L2_gnn_W_gcn"], 2), _lay(i["L2_ffn_Wg"], 2)], 1), WL)
    a["w3"] = _pad(np.concatenate([_lay(i["L3_gnn_Wm"], 2), _lay(i["L3_ffn_gW"], 2)], 1), WL)
    for n, E, H in ((0, E0, H0), (1, E1, H1), (2, E1, H1)):
        w1 = i[f"L{n}_ffn_W1"].transpose(1, 0, 2).reshape(D, E * H)
        w2 = i[f"L{n}_ffn_W2"].reshape(E * H, D)
        a[f"f{n}"] = np.concatenate([_lay(w1, 2), _lay(w2, E * H // P)], 1)
    eW2 = np.zeros((4, P, P), f32)
    for e in range(4):
        eW2[e, :, (e % 2) * HF:(e % 2 + 1) * HF] = i["L3_ffn_eW2"][e]
    a["f3"] = _pad(np.concatenate([
        _lay(i["L3_ffn_sW1"], 2), _lay(i["L3_ffn_sW2"], 2), _lay(i["L3_ffn_sW3"], 1),
        _lay(i["L3_ffn_eW1"].transpose(1, 0, 2).reshape(D, 512), 2), _lay(eW2.reshape(4 * P, P), 4),
        _lay(i["L3_ffn_eW3"].reshape(4 * HF, D), 2)], 1), W3N)
    vectors = [i["L0_ffn_b1"], i["L1_ffn_b1"], i["L2_ffn_b1"]]
    for n in (1, 2, 3):
        vectors += [i[f"L1_gnn_g{n}"], i[f"L1_gnn_be{n}"]]
    vectors += [i["L1_gnn_b1"], i["L2_gnn_b_proj"], i["L2_gnn_b_gcn"], i["L3_ffn_sb1"], i["L3_ffn_eb1"],
                i["L3_ffn_sb2"], i["L3_ffn_eb2"]]
    a["cols"] = np.ascontiguousarray(np.concatenate([_column(v) for v in vectors], 1))
    a["rows"] = np.concatenate([i[k] for k in (
        "L0_ffn_router_b", "L1_gnn_b1", "L1_gnn_b2", "L1_gnn_b3", "L1_ffn_gate_b", "L2_ffn_bg", "L2_ffn_bias",
        "L3_ffn_gb", "L3_ffn_sb3")])[None, :]
    b2 = np.zeros((E0, 4, D), f32)
    for n, k in enumerate(("L0_ffn_b2", "L1_ffn_b2", "L2_ffn_b2", "L3_ffn_eb3")):
        b2[:i[k].shape[0], n] = i[k]
    a["b2"] = b2.reshape(E0, 4 * D)
    al = np.stack([np.tile(i["L3_gnn_al"], HEADS), np.tile(i["L3_gnn_ar"], HEADS)])
    a["al"] = np.ascontiguousarray(np.broadcast_to(al, (P, 2, D)))
    m = np.arange(16 * P)
    a["sel2"] = (m[None, :] // HF == np.arange(E0)[:, None]).astype(np.float16)
    a["sel8"] = (np.arange(E1 * P)[None, :] // P == np.arange(E1)[:, None]).astype(np.float16)
    a["sel4f"] = (np.arange(HEADS * P)[None, :] // P == np.arange(HEADS)[:, None]).astype(f32)
    a["ident"] = np.eye(P, dtype=f32)
    a["rev"] = np.ascontiguousarray(np.broadcast_to(E0 - np.arange(E0, dtype=f32), (P, E0)))
    a["ones16"] = np.ones((1, 512), np.float16)
    return a


def kernel(**inputs):
    import concourse.bacc as _bacc
    from concourse.bass_utils import run_bass_kernel_spmd as _run

    arrays = {f"in_{k}": v for k, v in layout(inputs).items()}
    nc = _bacc.Bacc("TRN2", target_bir_lowering=False, num_devices=1)
    io = {k[3:]: nc.dram_tensor(k, v.shape, mybir.dt.from_np(v.dtype), kind="ExternalInput").ap()
          for k, v in arrays.items()}
    io["out"] = nc.dram_tensor("out_xT", (P, FT, NC), F32, kind="ExternalOutput").ap()
    build(nc, io)
    r = _run(nc, [arrays], core_ids=[0])
    got = np.asarray(r.results[0]["out_xT"])
    return np.ascontiguousarray(got.transpose(1, 0, 2).reshape(D, NC)[:, :N].T)
```

```python
from contextlib import ExitStack

import numpy as np

import concourse.bass as bass
from concourse import mybir

F32 = mybir.dt.float32
F16 = mybir.dt.float16
ALU = mybir.AluOpType
ACT = mybir.ActivationFunctionType
AX = mybir.AxisListType

N = 2708
D = 256
P = 128
KT = -(-N // P)
NP = KT * P
FT = D // P
CH = 6
CW = 452
NC = CH * CW
HALF = NC // 2
CPH = CH // 2
LAST = N - (KT - 1) * P
RING = 4
STEPS = 2 * KT
LN_EPS = 1e-5
HEADS, HF = 4, 64
THIRD = 2 * CW
TOPK_ROWS = 700
U32, I32 = mybir.dt.uint32, mybir.dt.int32


def expert_tiles(E, A):
    n = (A * NP + E * (P - 1)) // P
    return n + n % 2


E0, H0 = 32, 64
E1, H1 = 8, 512
E3 = 4
TILES = {E0: expert_tiles(E0, 1), E1: expert_tiles(E1, 2)}
SLOTS = P * max(TILES.values())
SLOTS_RUN = 4

_COLS = {}
_at = 0
for _name, _n in (("L0_b1", E0), ("L0_half", E0), ("L1_b1", 32), ("L2_b1", 32), ("g1", 2), ("be1", 2), ("g2", 2), ("be2", 2),
                  ("g3", 2), ("be3", 2), ("gb1", 2), ("b_proj", 2), ("b_gcn", 2), ("sb1", 2), ("eb1", 4),
                  ("sb2", 1), ("eb2", 2)):
    _COLS[_name] = _at
    _at += _n
NCOLS = _at
_ROWS = {}
_at = 0
for _name, _n in (("router_b", E0), ("L1_b1", D), ("L1_b2", D), ("L1_b3", D), ("gate_b", E1), ("bg", E1),
                  ("bias", E1), ("gb", E3), ("sb3", D)):
    _ROWS[_name] = (_at, _n)
    _at += _n
NROWS = _at
WL = 1552
WB = WL // 4
W3 = {"sW1": 0, "sW2": 512, "sW3": 768, "eW1": 1024, "eW2": 2048, "eW3": 2560}
W3N = 4096
ST = 512


def build(nc, io):
    ctx = ExitStack()
    with ctx:
        def sb(name, shape, dt=F32):
            return ctx.enter_context(nc.sbuf_tensor(name, shape, dt))

        nsem = [0]

        def sem(name):
            nsem[0] += 1
            return ctx.enter_context(nc.semaphore(name))

        xT = sb("xT", [P, FT, NP])
        R1 = sb("R1", [P, FT * NP])
        nT = R1[:, :].rearrange("p (f n) -> p f n", f=FT)
        XH = sb("XH", [P, FT, NP], F16)
        XL = sb("XL", [P, FT, NP], F16)
        R2 = sb("R2", [P, KT * D])
        HH = R2[:, 0:KT * P].bitcast(F16).rearrange("p (k d) -> p k d", k=KT)
        HL = R2[:, KT * P:KT * D].bitcast(F16).rearrange("p (k d) -> p k d", k=KT)
        BIG = sb("BIG", [P, 16768])
        pair = BIG[:, 0:RING * HALF].bitcast(F16).rearrange("p (r h n) -> p r h n", r=RING, h=2)
        a32 = BIG[:, RING * HALF:2 * RING * HALF].rearrange("p (r n) -> p r n", r=RING)
        dgb = BIG[:, 2 * RING * HALF:2 * RING * HALF + NP]
        cnt = BIG[:, 2 * RING * HALF + NP:2 * RING * HALF + NP + NC // 2].bitcast(F16)
        many = sb("many", [1, 1], I32)
        many_f = sb("many_f", [1, 2, 8])
        bits = sb("bits", [P, 4, 1], U32)
        room = sb("room", [P, 2, 1])
        etmp = sb("etmp", [P, 2, CW])
        WH = sb("WH", [P, WL], F16)
        WLo = sb("WLo", [P, WL], F16)
        stage = sb("stage", [P, 2, ST])
        cwh = R1[:, 0:NP // 2].bitcast(F16)
        cwl = R1[:, NP // 2:NP].bitcast(F16)
        cols = sb("cols", [P, NCOLS])
        rowsf = BIG[0:1, 0:NROWS]
        rowh = sb("rowh", [1, NROWS], F16)
        rowl = sb("rowl", [1, NROWS], F16)
        b2f = BIG[:, NROWS:NROWS + 4 * D]
        b2h = sb("b2h", [P, 4, D], F16)
        b2l = sb("b2l", [P, 4, D], F16)
        selE = sb("selE", [P, E0 * P], F16)
        sel2 = sb("sel2", [P, 2 * P], F16)
        lt = sb("lt", [P, P], F16)
        one2 = sb("one2", [P, P], F16)
        ident16 = sb("ident16", [P, P], F16)
        iota = sb("iota", [1, max(TILES.values())])
        posu = sb("posu", [P, 2, KT], U32)
        idx = sb("idx", [P, SLOTS_RUN, 2], U32)
        idg = sb("idg", [P, SLOTS_RUN, 2], U32)
        eid = sb("eid", [1, max(TILES.values())], I32)
        rt = sb("rt", [P, 4, E0])
        rt2 = sb("rt2", [1, max(TILES.values()) + 2, 1])
        packed = sb("packed", [1, max(TILES.values()), 1])
        rti = sb("rti", [P, 2, E0], I32)
        ident = sb("ident", [P, P])
        onesf = sb("onesf", [P, P])
        meanf = sb("meanf", [P, P])
        ones16 = sb("ones16", [1, 512], F16)
        rev = sb("rev", [P, E0])
        eps = sb("eps", [P, 1])
        dinv = sb("dinv", [P, KT])
        al_bc = sb("al_bc", [P, 2, D])
        sm = sb("sm", [P, 4, KT, 1])
        gv = sb("gv", [P, 5, KT * HEADS])
        gm = sb("gm", [P, 2, HEADS])
        ps = ctx.enter_context(nc.psum_tensor("ps", [P, 8, 512], F32))
        scratch = nc.dram_tensor("adj_split", (2, KT, P, 2, HALF), F16).ap()
        q_dram = nc.dram_tensor("attention_rows", (HEADS, NP), F32).ap()
        adj_top = nc.dram_tensor("adj_top", (NP, NP), F32).ap()

        ln_d = R2[:, 0:4 * CW].rearrange("p (u f n) -> p u f n", u=2, f=FT)
        ln_sq = R2[:, 4 * CW:8 * CW].rearrange("p (u f n) -> p u f n", u=2, f=FT)
        ln_sd = R2[:, 8 * CW:10 * CW].rearrange("p (u n) -> p u n", u=2)
        ln_r2 = R2[:, 10 * CW:12 * CW].rearrange("p (u n) -> p u n", u=2)
        LG = KT * E0
        lg = [R2[:, i * LG:(i + 1) * LG] for i in range(8)]
        def work(at, n, dt=F32):
            v = R1[:, at:at + n]
            return v if dt == F32 else v.bitcast(dt)

        row = work(0, 1024, F16).rearrange("p (u n) -> p u n", u=SLOTS_RUN)
        xg = work(512, 512, F16).rearrange("p (u n) -> p u n", u=2)
        xf = work(1024, 512, F16).rearrange("p (u i n) -> p u i n", u=2, i=4)
        hact = work(1536, 1024).rearrange("p (u t n) -> p u t n", u=2, t=4)
        hh = work(2560, 512, F16).rearrange("p (u t n) -> p u t n", u=2, t=4)
        hl = work(3072, 512, F16).rearrange("p (u t n) -> p u t n", u=2, t=4)
        yo = work(3584, 512).rearrange("p (u n) -> p u n", u=2)
        yg = work(0, 2048).rearrange("p (u a n) -> p u a n", u=SLOTS_RUN, a=2)
        zt = work(5120, 512).rearrange("p (u n) -> p u n", u=2)
        xs_dram = nc.dram_tensor("expert_rows", (SLOTS, 2 * D), F16).ap()
        ys_dram = nc.dram_tensor("expert_out", (SLOTS, D), F32).ap()

        block = ctx.enter_context(nc.Block())

        def chunk(c, w=CW):
            return bass.DynSlice(c * CW, w) if not isinstance(c, int) else slice(c * CW, c * CW + w)

        def dyn(start, size):
            return slice(start, start + size) if isinstance(start, int) else bass.DynSlice(start, size)

        sems, counts = {}, {}

        class Stage:

            def __init__(self, kind, **totals):
                self.kind, self.base = kind, {}
                for n, total in totals.items():
                    key = (kind, n)
                    if key not in sems:
                        sems[key], counts[key] = sem(f"{kind}_{n}"), 0
                    self.base[n] = counts[key]
                    counts[key] += total
                self.totals = totals

            def __getitem__(self, n):
                return sems[self.kind, n]

            def at(self, n):
                return self.base[n]

            def end(self, n):
                return self[n], self.base[n] + self.totals[n]

        def after(eng, *stages):
            for st in stages:
                for s, v in st.done:
                    eng.wait_ge(s, v)

        def mm3(pe, out, ah, al, bh, bl, start=False, stop=False):
            pe.matmul(out, ah, bh, start=start, stop=False)
            pe.matmul(out, ah, bl, start=False, stop=False)
            return pe.matmul(out, al, bh, start=False, stop=stop)

        LC = Stage("const", ld=0, v=0, cl=0)
        small = [(cols[:, :], "cols"), (rowsf[:, :], "rows"), (b2f[:, :], "b2"), (sel2[:, :], "sel2"),
                 (selE[:, :], "selE"), (lt[:, :], "lt"), (one2[:, :], "one2"), (ident16[:, :], "ident16"),
                 (iota[:, :], "iota"), (ident[:, :], "ident"), (rev[:, :], "rev"),
                 (ones16[:, :], "ones16"), (al_bc[:, :, :], "al"), (xT[:, :, :], "xT")]
        LC.done = [(LC["ld"], 16 * len(small)), (LC["v"], 11), (LC["cl"], 16)]

        def const_sp(sp):
            for dst, name in small:
                sp.dma_start(dst, io[name]).then_inc(LC["ld"], 16)

        def clear_slots(act):
            act.wait_ge(LC["v"], 6)
            act.dma_start(xs_dram.rearrange("(t p) n -> p t n", p=P),
                          row[:, 0:1, :].to_broadcast([P, SLOTS // P, 2 * D])).then_inc(LC["cl"], 16)

        def const_dve(v):
            v.memset(onesf[:, :], 1.0).then_inc(LC["v"], 1)
            v.memset(meanf[:, :], 1.0 / D).then_inc(LC["v"], 1)
            v.memset(eps[:, :], LN_EPS).then_inc(LC["v"], 1)
            v.memset(XH[:, :, NC:NP], 0.0).then_inc(LC["v"], 1)
            v.memset(XL[:, :, NC:NP], 0.0).then_inc(LC["v"], 1)
            v.memset(row[:, 0, :], 0.0).then_inc(LC["v"], 1)
            v.memset(idx[:, :, :], 0).then_inc(LC["v"], 1)
            v.wait_ge(LC["ld"], 16 * len(small))
            v.tensor_copy(rowh[:, :], rowsf[:, :]).then_inc(LC["v"], 1)
            v.tensor_copy(b2h[:, :, :].rearrange("p a b -> p (a b)"), b2f[:, :]).then_inc(LC["v"], 1)
            v.wait_ge(LC["v"], 9)
            v.tensor_tensor(rowl[:, :], rowsf[:, :], rowh[:, :], ALU.subtract).then_inc(LC["v"], 1)
            v.tensor_tensor(b2l[:, :, :].rearrange("p a b -> p (a b)"), b2f[:, :],
                            b2h[:, :, :].rearrange("p a b -> p (a b)"), ALU.subtract).then_inc(LC["v"], 1)

        WS = Stage("w", ld0=0, ld1=0, hi=0, lo=0)
        wblocks = [0]

        class Split:
            def __init__(self, src, hi, lo, n, before, width=ST):
                self.src, self.hi, self.lo, self.n, self.before, self.width = src, hi, lo, n, before, width
                self.base = wblocks[0]
                wblocks[0] += n
                self.done = [(WS["lo"], wblocks[0] + 2)]

            def loop(self, eng, body):
                with eng.Fori(0, self.n // 2) as g:
                    for u in range(2):
                        body(2 * g + u, 2 * g + u + self.base, u, g + self.base // 2)

            def sp(self, sp):
                after(sp, *self.before)

                def body(b, m, u, turn):
                    sp.wait_ge(WS["lo"], m + 1)
                    sp.dma_start(stage[:, u, 0:self.width], self.src[:, dyn(b * self.width, self.width)]).then_inc(WS[f"ld{u}"], 16)
                self.loop(sp, body)

            def pool(self, pool):
                after(pool, *self.before)

                def body(b, m, u, turn):
                    pool.wait_ge(WS[f"ld{u}"], turn * 16 + 16)
                    pool.tensor_copy(self.hi[:, dyn(b * self.width, self.width)], stage[:, u, 0:self.width])\
                        .then_inc(WS["hi"], 1)
                    pool.wait_ge(WS["hi"], m + 1)
                    pool.tensor_tensor(self.lo[:, dyn(b * self.width, self.width)], stage[:, u, 0:self.width],
                                       self.hi[:, dyn(b * self.width, self.width)], ALU.subtract).then_inc(WS["lo"], 1)
                self.loop(pool, body)

        class LN:
            def __init__(self, name, src, before, gamma=None):
                self.st = Stage("ln", mean=CH, d=CH, sq=CH, var=CH, sd=2 * CH, rs=CH, nt=2 * CH, y=CH, g=CH * (gamma is not None),
                                hi=CH, lo=CH + 2)
                self.src, self.before, self.gamma = src, before, gamma
                self.done = [self.st.end("lo")]

            def stagger(self, lead, follow):
                def step(k, u):
                    lead(k, u)
                    follow(k - 1, 1 - u)
                lead(0, 0)
                step(1, 1)
                self.loop(nc.tensor, step)
                follow(CH - 1, 1)

            def loop(self, eng, step):
                with eng.Fori(1, CH // 2) as g:
                    for u in range(2):
                        step(2 * g + u, u)

            def pe(self, pe):
                after(pe, *self.before)
                s = self.st

                def mean(c, u):
                    for f in range(FT):
                        mm = pe.matmul(ps[:, u, 0:CW], meanf[:, :], self.src[:, f, chunk(c)],
                                       start=f == 0, stop=f == FT - 1)
                    mm.then_inc(s["mean"], 1)

                def var(c, u):
                    pe.wait_ge(s["sq"], s.at("sq") + c + 1)
                    for f in range(FT):
                        mm = pe.matmul(ps[:, 2 + u, 0:CW], meanf[:, :], ln_sq[:, u, f, :],
                                       start=f == 0, stop=f == FT - 1)
                    mm.then_inc(s["var"], 1)
                self.stagger(mean, var)

            def dve(self, v):
                after(v, *self.before)
                s = self.st
                v.sem_inc(s["lo"], 2)

                def centre(c, u):
                    v.wait_ge(s["mean"], s.at("mean") + c + 1)
                    v.wait_ge(s["lo"], s.at("lo") + c + 1)
                    for f in range(FT):
                        op = v.tensor_tensor(ln_d[:, u, f, :], self.src[:, f, chunk(c)], ps[:, u, 0:CW],
                                             ALU.subtract)
                    op.then_inc(s["d"], 1)

                def scale(c, u):
                    v.wait_ge(s["rs"], s.at("rs") + c + 1)
                    v.scalar_tensor_tensor(ln_r2[:, u, :], ps[:, 2 + u, 0:CW], LN_EPS, ln_r2[:, u, :],
                                           ALU.add, ALU.mult).then_inc(s["nt"], 1)
                    v.wait_ge(s["nt"], s.at("nt") + 2 * c + 1)
                    v.scalar_tensor_tensor(ln_sd[:, u, :], ln_r2[:, u, :], 3.0, ln_sd[:, u, :],
                                           ALU.subtract, ALU.mult).then_inc(s["nt"], 1)
                    v.wait_ge(s["nt"], s.at("nt") + 2 * c + 2)
                    for f in range(FT):
                        op = v.scalar_tensor_tensor(ln_d[:, u, f, :], ln_d[:, u, f, :], -0.5, ln_sd[:, u, :],
                                                    ALU.mult, ALU.mult)
                    op.then_inc(s["y"], 1)

                def low(c, u):
                    v.wait_ge(s["hi"], s.at("hi") + c + 1)
                    y = ln_d[:, u, :, :] if self.gamma is None else self.src[:, :, chunk(c)]
                    v.tensor_tensor(XL[:, :, chunk(c)], y, XH[:, :, chunk(c)], ALU.subtract).then_inc(s["lo"], 1)

                def step(k, u):
                    low(k - 2, u)
                    centre(k, u)
                    scale(k - 1, 1 - u)
                centre(0, 0)
                centre(1, 1)
                scale(0, 0)
                self.loop(v, step)
                low(CH - 2, 0)
                scale(CH - 1, 1)
                low(CH - 1, 1)

            def act(self, act):
                act.preload_act_table_set("natural_log_exp_and_others")
                after(act, *self.before)
                s = self.st

                def square(c, u):
                    act.wait_ge(s["d"], s.at("d") + c + 1)
                    act.activation(ln_sq[:, u, :, :], ln_d[:, u, :, :], ACT.Square).then_inc(s["sq"], 1)

                def root(c, u):
                    act.wait_ge(s["var"], s.at("var") + c + 1)
                    act.activation(ln_sd[:, u, :], ps[:, 2 + u, 0:CW], ACT.Ln, bias=eps[:, 0:1])\
                       .then_inc(s["sd"], 1)
                    act.wait_ge(s["sd"], s.at("sd") + 2 * c + 1)
                    act.activation(ln_sd[:, u, :], ln_sd[:, u, :], ACT.Exp, scale=-0.5).then_inc(s["sd"], 1)
                    act.wait_ge(s["sd"], s.at("sd") + 2 * c + 2)
                    act.activation(ln_r2[:, u, :], ln_sd[:, u, :], ACT.Square).then_inc(s["rs"], 1)

                def high(c, u):
                    act.wait_ge(s["y"], s.at("y") + c + 1)
                    y = ln_d[:, u, :, :]
                    if self.gamma is not None:
                        g0, b0 = self.gamma
                        y = self.src[:, :, chunk(c)]
                        for f in range(FT):
                            op = act.activation(self.src[:, f, chunk(c)], ln_d[:, u, f, :], ACT.Identity,
                                                scale=cols[:, g0 + f:g0 + f + 1], bias=cols[:, b0 + f:b0 + f + 1])
                        op.then_inc(s["g"], 1)
                        act.wait_ge(s["g"], s.at("g") + c + 1)
                    act.activation(XH[:, :, chunk(c)], y, ACT.Copy).then_inc(s["hi"], 1)

                def step(k, u):
                    high(k - 2, u)
                    root(k - 1, 1 - u)
                    square(k, u)
                square(0, 0)
                root(0, 0)
                square(1, 1)
                self.loop(act, step)
                high(CH - 2, 0)
                root(CH - 1, 1)
                high(CH - 1, 1)

        class TokenLinear:
            R = 4

            def __init__(self, name, w, before, row=None, scaled=False):
                self.st = Stage("tok", mm=KT, hi=KT, lo=KT + self.R)
                self.w, self.before, self.row, self.scaled = w, before, row, scaled
                self.done = [self.st.end("lo")]

            def loop(self, eng, body):
                with eng.Fori(0, KT // self.R) as g:
                    for u in range(self.R):
                        body(self.R * g + u, u)
                for t in range(KT // self.R * self.R, KT):
                    body(t, t % self.R)

            def pe(self, pe):
                after(pe, *self.before)
                pe.sem_inc(self.st["lo"], self.R)

                def body(t, u):
                    out = ps[:, 4 + u, 0:D]
                    pe.wait_ge(self.st["lo"], self.st.at("lo") + t + 1)
                    for f in range(FT):
                        tok = dyn(t * P, P)
                        w = self.w + f * D
                        last = f == FT - 1 and self.row is None
                        mm = mm3(pe, out, XH[:, f, tok], XL[:, f, tok], WH[:, w:w + D], WLo[:, w:w + D],
                                 start=f == 0, stop=last)
                    if self.row is not None:
                        a, n = _ROWS[self.row]
                        pe.matmul(out, ones16[:, 0:P], rowh[:, a:a + n], start=False, stop=False)
                        mm = pe.matmul(out, ones16[:, 0:P], rowl[:, a:a + n], start=False, stop=True)
                    mm.then_inc(self.st["mm"], 1)
                self.loop(pe, body)

            def act(self, act):
                after(act, *self.before)

                def body(t, u):
                    act.wait_ge(self.st["mm"], self.st.at("mm") + t + 1)
                    sc = dinv[:, dyn(t, 1)] if self.scaled else 1.0
                    act.activation(HH[:, dyn(t, 1), :], ps[:, 4 + u:5 + u, 0:D], ACT.Identity if self.scaled else ACT.Copy,
                                   scale=sc).then_inc(self.st["hi"], 1)
                self.loop(act, body)

            def dve(self, v):
                after(v, *self.before)

                def body(t, u):
                    v.wait_ge(self.st["hi"], self.st.at("hi") + t + 1)
                    sc = dinv[:, dyn(t, 1)] if self.scaled else 1.0
                    v.scalar_tensor_tensor(HL[:, dyn(t, 1), :], ps[:, 4 + u:5 + u, 0:D], sc, HH[:, dyn(t, 1), :],
                                           ALU.mult, ALU.subtract).then_inc(self.st["lo"], 1)
                self.loop(v, body)

        class FeatLinear:
            def __init__(self, name, w, before, kind, bias=None):
                self.st = Stage("feat", mm=CH, t=CH * (kind == "tanh"), hi=CH * (kind == "tanh"), ev=CH + 2)
                self.w, self.before, self.kind, self.bias = w, before, kind, bias
                self.done = [self.st.end("ev")]

            def loop(self, eng, body):
                with eng.Fori(0, CH // 2) as g:
                    for u in range(2):
                        body(2 * g + u, u)

            def pe(self, pe):
                after(pe, *self.before)
                pe.sem_inc(self.st["ev"], 2)

                def body(c, u):
                    pe.wait_ge(self.st["ev"], self.st.at("ev") + c + 1)
                    for m in range(FT):
                        for f in range(FT):
                            w = self.w + f * D + m * P
                            mm = mm3(pe, ps[:, 2 * u + m, 0:CW], WH[:, w:w + P], WLo[:, w:w + P],
                                     XH[:, f, chunk(c)], XL[:, f, chunk(c)], start=f == 0, stop=f == FT - 1)
                    mm.then_inc(self.st["mm"], 1)
                self.loop(pe, body)

            def act(self, act):
                if self.kind == "add":
                    return
                after(act, *self.before)

                def body(c, u):
                    act.wait_ge(self.st["mm"], self.st.at("mm") + c + 1)
                    for m in range(FT):
                        b = cols[:, self.bias + m:self.bias + m + 1]
                        if self.kind == "nT":
                            op = act.activation(nT[:, m, chunk(c)], ps[:, 2 * u + m, 0:CW], ACT.Identity, bias=b)
                        else:
                            op = act.activation(ln_d[:, u, m, :], ps[:, 2 * u + m, 0:CW], ACT.Tanh, bias=b)
                    if self.kind == "nT":
                        op.then_inc(self.st["ev"], 1)
                        return
                    op.then_inc(self.st["t"], 1)
                    act.wait_ge(self.st["t"], self.st.at("t") + c + 1)
                    act.activation(XH[:, :, chunk(c)], ln_d[:, u, :, :], ACT.Copy).then_inc(self.st["hi"], 1)
                self.loop(act, body)

            def dve(self, v):
                if self.kind == "nT":
                    return
                after(v, *self.before)

                def body(c, u):
                    if self.kind == "add":
                        v.wait_ge(self.st["mm"], self.st.at("mm") + c + 1)
                        for m in range(FT):
                            x = xT[:, m, chunk(c)]
                            op = v.tensor_tensor(x, x, ps[:, 2 * u + m, 0:CW], ALU.add)
                    else:
                        v.wait_ge(self.st["hi"], self.st.at("hi") + c + 1)
                        op = v.tensor_tensor(XL[:, :, chunk(c)], ln_d[:, u, :, :], XH[:, :, chunk(c)], ALU.subtract)
                    op.then_inc(self.st["ev"], 1)
                self.loop(v, body)

        class Product:

            def __init__(self, name, kind, before, free, count=False):
                split, filt = kind == "split", kind == "filter"
                self.count = count
                turns = 16 * (STEPS // RING)
                totals = dict(r=STEPS * filt, th=STEPS * filt, hi=STEPS * (split or filt), lo=STEPS * (split or filt),
                              cn=STEPS * count, go=STEPS * count, dg=STEPS * split, z=split, zc=int(count), dmm=CH * split, dgc=CH * split,
                              rd=8 * split, used=STEPS, e1=2 * FT * CPH, ev=2 * FT * CPH)
                totals |= {f"a{u}": turns for u in range(RING)} | {f"st{u}": turns * split for u in range(RING)}
                self.st = Stage("prod", **totals)
                self.kind, self.before = kind, before
                self.source = io["adjT"]
                self.free = free
                self.done = [self.st.end("ev")]
                if split:
                    self.done += [self.st.end(f"st{u}") for u in range(RING)]

            def steps(self, eng, body, between=None, end=None):
                for n in range(RING):
                    body(n, n, n, 0, 0)
                with eng.Fori(1, 5) as g:
                    for u in range(RING):
                        body(RING * g + u, RING * g + u, u, g, 0)
                body(20, 20, 0, 5, 0)
                body(21, 21, 1, 5, 0)
                if between:
                    between(0)
                body(22, 0, 2, 5, 1)
                body(23, 1, 3, 5, 1)
                with eng.Fori(6, 10) as g:
                    for u in range(RING):
                        body(RING * g + u, RING * g + u - KT, u, g, 1)
                for u in range(RING):
                    body(40 + u, 40 + u - KT, u, 10, 1)
                if between:
                    between(1)

            def sp(self, sp):
                after(sp, *self.free)
                s = self.st

                def body(n, k, u, turn, h):
                    first = isinstance(n, int) and n < RING
                    if self.kind == "kept":
                        if not first:
                            sp.wait_ge(s["used"], s.at("used") + n - 3)
                            if self.count:
                                sp.sem_inc(s["go"], 1)
                                sp.wait_ge(s["cn"], s.at("cn") + n - 3)
                        sp.dma_start(pair[:, u, :, :], scratch[h, k]).then_inc(s[f"a{u}"], 16)
                        return
                    if not first:
                        sp.wait_ge(s["lo"], s.at("lo") + n - 3)
                        if self.kind == "split":
                            sp.wait_ge(s["dg"], s.at("dg") + n - 3)
                    sp.dma_start(a32[:, u, :], self.source[dyn(k * P, P), h * HALF:(h + 1) * HALF])\
                      .then_inc(s[f"a{u}"], 16)
                if self.kind != "filter":
                    self.steps(sp, body)
                    return
                with sp.If(sp.value_load(many[0:1, 0:1], min_val=0, max_val=1) > 0):
                    self.source = adj_top
                    self.steps(sp, body)
                with sp.Else():
                    self.source = io["adjT"]
                    self.steps(sp, body)

            def pe(self, pe):
                after(pe, *self.before)
                s = self.st

                def body(n, k, u, turn, h):
                    if self.kind == "kept":
                        pe.wait_ge(s[f"a{u}"], s.at(f"a{u}") + turn * 16 + 16)
                    else:
                        pe.wait_ge(s["lo"], s.at("lo") + n + 1)
                    start = isinstance(k, int) and k == 0
                    stop = isinstance(k, int) and k == KT - 1
                    for f in range(FT):
                        fs = slice(f * P, (f + 1) * P)
                        banks = [ps[:, (6 * h + f * CPH + c) % 8, 0:CW] for c in range(CPH)]
                        hi = [pair[:, u, 0, c * CW:(c + 1) * CW] for c in range(CPH)]
                        lo = [pair[:, u, 1, c * CW:(c + 1) * CW] for c in range(CPH)]
                        for c in range(CPH):
                            i = f * CPH + c
                            if start and h == 1:
                                if i >= 2:
                                    pe.wait_ge(s["e1"], s.at("e1") + i - 1)
                                elif self.kind == "split" and i == 0:
                                    pe.wait_ge(s["dgc"], s.at("dgc") + CPH)
                            pe.matmul(banks[c], HH[:, k, fs], hi[c], start=start, stop=False)
                            pe.matmul(banks[c], HH[:, k, fs], lo[c], start=False, stop=False)
                        for c in range(CPH):
                            mm = pe.matmul(banks[c], HL[:, k, fs], hi[c], start=False, stop=stop)
                    mm.then_inc(s["used"], 1)

                def degrees(h):
                    if self.kind != "split":
                        return
                    pe.wait_ge(s["dg"], s.at("dg") + KT * (h + 1))
                    for c in range(CPH):
                        if c == 2:
                            pe.wait_ge(s["dgc"], s.at("dgc") + CPH * h + 1)
                        col = h * HALF + c * CW
                        pe.matmul(ps[:, (6, 4)[h] + c % 2, 0:CW], onesf[:, :], dgb[:, col:col + CW],
                                  start=True, stop=True).then_inc(s["dmm"], 1)
                self.steps(pe, body, degrees)

            def act(self, act):
                if self.kind == "kept":
                    return
                after(act, *self.before)
                s = self.st

                def body(n, k, u, turn, h):
                    static = isinstance(n, int)
                    if self.kind == "split":
                        act.wait_ge(s[f"a{u}"], s.at(f"a{u}") + turn * 16 + 16)
                    else:
                        act.wait_ge(s["r"], s.at("r") + n + 1)
                        act.activation(a32[:, u, :], a32[:, u, :], ACT.Tanh).then_inc(s["th"], 1)
                        act.wait_ge(s["th"], s.at("th") + n + 1)
                    if not (static and n < RING):
                        act.wait_ge(s["used"], s.at("used") + n - 3)
                        if self.kind == "split":
                            act.wait_ge(s[f"st{u}"], s.at(f"st{u}") + turn * 16)
                    act.activation(pair[:, u, 0, :], a32[:, u, :], ACT.Copy).then_inc(s["hi"], 1)
                    if self.kind == "split":
                        act.wait_ge(s["lo"], s.at("lo") + n + 1)
                        act.dma_start(scratch[h, k], pair[:, u, :, :]).then_inc(s[f"st{u}"], 16)

                def relu(h):
                    if self.kind == "split":
                        rd = nT[:, 0, 0:HALF]
                        act.wait_ge(s["dgc"], s.at("dgc") + CPH * (h + 1))
                        if h:
                            act.wait_ge(s["ev"], s.at("ev") + FT * CPH)
                        act.activation(rd, dgb[:, h * HALF:(h + 1) * HALF], ACT.Ln, bias=onesf[:, 0:1])\
                           .then_inc(s["rd"], 1)
                        act.wait_ge(s["rd"], s.at("rd") + 4 * h + 1)
                        act.activation(rd, rd, ACT.Exp, scale=-1.0).then_inc(s["rd"], 1)
                    if self.kind != "filter":
                        return
                    b0 = _COLS["b_gcn"]
                    act.wait_ge(s["used"], s.at("used") + KT * (h + 1))
                    for i in range(FT * CPH):
                        f = i // CPH
                        n = FT * CPH * h + i
                        if n >= 2:
                            act.wait_ge(s["ev"], s.at("ev") + n - 1)
                        act.activation(etmp[:, i % 2, :], ps[:, (6 * h + i) % 8, 0:CW], ACT.Relu,
                                       bias=cols[:, b0 + f:b0 + f + 1]).then_inc(s["e1"], 1)
                self.steps(act, body, relu)

            def pool(self, pool):
                if self.kind != "split":
                    return
                after(pool, *self.before)
                s = self.st
                pool.memset(dgb[:, :], 0.0).then_inc(s["z"], 1)
                pool.wait_ge(s["z"], s.at("z") + 1)

                def body(n, k, u, turn, h):
                    pool.wait_ge(s[f"a{u}"], s.at(f"a{u}") + turn * 16 + 16)
                    if not (isinstance(n, int) and n == 0):
                        pool.wait_ge(s["dg"], s.at("dg") + n)
                    d = dgb[:, h * HALF:(h + 1) * HALF]
                    pool.tensor_tensor(d, d, a32[:, u, :], ALU.add).then_inc(s["dg"], 1)
                self.steps(pool, body)

            def dve(self, v):
                after(v, *self.before)
                s = self.st
                if self.count:
                    v.memset(cnt, 0.0).then_inc(s["zc"], 1)
                    v.wait_ge(s["zc"], s.at("zc") + 1)

                def low(n, u):
                    v.wait_ge(s["hi"], s.at("hi") + n + 1)
                    v.tensor_tensor(pair[:, u, 1, :], a32[:, u, :], pair[:, u, 0, :], ALU.subtract)\
                     .then_inc(s["lo"], 1)

                def body(n, k, u, turn, h):
                    first = isinstance(n, int) and n == 0
                    if self.kind == "split":
                        low(n, u)
                    elif self.count:
                        v.wait_ge(s[f"a{u}"], s.at(f"a{u}") + turn * 16 + 16)
                        if not first:
                            v.wait_ge(s["cn"], s.at("cn") + n)
                        c = cnt[:, h * HALF:(h + 1) * HALF]
                        v.scalar_tensor_tensor(c, pair[:, u, 0, :], 0.0, c, ALU.is_gt, ALU.add).then_inc(s["cn"], 1)
                    elif self.kind == "filter":
                        v.wait_ge(s[f"a{u}"], s.at(f"a{u}") + turn * 16 + 16)
                        a = a32[:, u, :]
                        v.scalar_tensor_tensor(a, a, 0.0, a, ALU.max, ALU.mult).then_inc(s["r"], 1)
                        if not first and not (isinstance(n, int) and n == KT):
                            low(n - 1, (u - 1) % RING)

                def out(h):
                    if self.kind == "filter":
                        low(KT * (h + 1) - 1, (KT * (h + 1) - 1) % RING)
                    if self.kind == "split":
                        for c in range(CPH):
                            v.wait_ge(s["dmm"], s.at("dmm") + CPH * h + c + 1)
                            col = h * HALF + c * CW
                            v.tensor_copy(dgb[:, col:col + CW], ps[:, (6, 4)[h] + c % 2, 0:CW])\
                             .then_inc(s["dgc"], 1)
                        v.wait_ge(s["dgc"], s.at("dgc") + CPH * (h + 1))
                        v.wait_ge(s["rd"], s.at("rd") + 4 * h + 2)
                        rd, rt = nT[:, 0, 0:HALF], nT[:, 1, 0:HALF]
                        v.scalar_tensor_tensor(rt, dgb[:, h * HALF:(h + 1) * HALF], 1.0, rd, ALU.add, ALU.mult)\
                         .then_inc(s["rd"], 1)
                        v.wait_ge(s["rd"], s.at("rd") + 4 * h + 3)
                        v.scalar_tensor_tensor(rd, rt, 2.0, rd, ALU.subtract, ALU.mult).then_inc(s["rd"], 1)
                        v.wait_ge(s["rd"], s.at("rd") + 4 * h + 4)
                    v.wait_ge(s["used"], s.at("used") + KT * (h + 1))
                    for i in range(FT * CPH):
                        f, c = divmod(i, CPH)
                        n = FT * CPH * h + i
                        acc = ps[:, (6 * h + i) % 8, 0:CW]
                        col = slice(h * HALF + c * CW, h * HALF + (c + 1) * CW)
                        e = etmp[:, i % 2, :]
                        if self.kind == "filter":
                            v.wait_ge(s["e1"], s.at("e1") + n + 1)
                            v.tensor_tensor(xT[:, f, col], xT[:, f, col], e, ALU.add).then_inc(s["ev"], 1)
                            continue
                        by = nT[:, 0, c * CW:(c + 1) * CW] if self.kind == "split" else dgb[:, col]
                        if n >= 2:
                            v.wait_ge(s["ev"], s.at("ev") + n - 1)
                        v.tensor_tensor(e, acc, by, ALU.mult).then_inc(s["e1"], 1)
                        v.wait_ge(s["e1"], s.at("e1") + n + 1)
                        if self.kind == "split":
                            v.tensor_tensor(xT[:, f, col], xT[:, f, col], e, ALU.subtract).then_inc(s["ev"], 1)
                        else:
                            v.scalar_tensor_tensor(nT[:, f, col], e, 0.0, nT[:, f, col], ALU.max, ALU.add)\
                             .then_inc(s["ev"], 1)
                self.steps(v, body, out)

        class Dinv:
            def __init__(self, before):
                self.st = Stage("dinv", pad=1, sq=1, r=1, mm=1, ev=1)
                self.before = before
                self.done = [(self.st["ev"], 1)]

            def dve(self, v):
                after(v, *self.before)
                s = self.st
                v.memset(dgb[:, N:NP], 1.0).then_inc(s["pad"], 1)
                v.wait_ge(s["mm"], 1)
                v.tensor_copy(dinv[:, :], ps[:, 7, 0:KT]).then_inc(s["ev"], 1)

            def act(self, act):
                act.wait_ge(self.st["pad"], 1)
                act.activation(dgb[:, :], dgb[:, :], ACT.Ln).then_inc(self.st["sq"], 1)
                act.wait_ge(self.st["sq"], 1)
                act.activation(dgb[:, :], dgb[:, :], ACT.Exp, scale=-0.5).then_inc(self.st["r"], 1)

            def pe(self, pe):
                pe.wait_ge(self.st["r"], 1)
                for t in range(KT):
                    mm = pe.matmul(ps[:, 7, t:t + 1], dgb[0:1, t * P:(t + 1) * P], onesf[0:1, 0:1],
                                   start=True, stop=True)
                mm.then_inc(self.st["mm"], 1)

        gate_links = [0]

        class Gates:
            def __init__(self, name, E, w, rows, kind, before):
                self.groups, soft = -(-KT // 4), int(kind == "soft2")
                self.st = Stage("gate", lg=KT, v=0, a={"argmax": 0, "softmax": 2, "top2": 2, "soft2": 4}[kind], cw=1,
                                mk=int(not soft), rk=int(not soft), tr=soft * self.groups, hi=soft * self.groups,
                                lo=soft * self.groups)
                self.E, self.w, self.rows, self.kind, self.before = E, w, rows, kind, before
                self.routed = kind != "soft2"
                self.done = [self.st.end("cw" if self.routed else "lo")]

            def view(self, i, e=None):
                return lg[i][:, 0:KT * self.E].rearrange("p (t e) -> p t e", e=self.E)

            def mask16(self):
                return lg[0][:, 0:KT * self.E // 2].bitcast(F16)

            def pe(self, pe):
                after(pe, *self.before)
                s, E = self.st, self.E
                with pe.Fori(0, 2) as b:
                    for g in range(KT // 2):
                        t = b * (KT // 2) + g
                        out = ps[:, dyn(b, 1), g * E:(g + 1) * E]
                        for f in range(FT):
                            w = self.w + f * E
                            mm3(pe, out, XH[:, f, dyn(t * P, P)], XL[:, f, dyn(t * P, P)],
                                WH[:, w:w + E], WLo[:, w:w + E], start=f == 0, stop=False)
                        for i, r in enumerate(self.rows):
                            a, n = _ROWS[r]
                            pe.matmul(out, ones16[:, 0:P], rowh[:, a:a + n], start=False, stop=False)
                            mm = pe.matmul(out, ones16[:, 0:P], rowl[:, a:a + n], start=False,
                                           stop=i == len(self.rows) - 1)
                        mm.then_inc(s["lg"], 1)
                if self.routed:
                    pe.wait_ge(s["mk"], s.at("mk") + 1)
                    n = KT // 2 * E
                    for b in range(2):
                        pe.matmul(ps[:, 2 + b, 0:n], lt[:, :], self.mask16()[:, b * n:(b + 1) * n], start=True, stop=True)
                        mm = pe.matmul(ps[:, 4 + b, 0:n], one2[:, :], self.mask16()[:, b * n:(b + 1) * n],
                                       start=True, stop=True)
                    mm.then_inc(s["rk"], 1)
                    return
                pe.wait_ge(s["cw"], s.at("cw") + 1)
                cw = self.view(5)
                for g in range(self.groups):
                    if g >= 2:
                        pe.wait_ge(s["lo"], s.at("lo") + g - 1)
                    ts = range(4 * g, min(4 * g + 4, KT))
                    for j, t in enumerate(ts):
                        mm = pe.transpose(ps[0:E, 2 + g % 2, j * P:(j + 1) * P], cw[:, t, :], ident[:, :])
                    mm.then_inc(s["tr"], 1)

            def act(self, act):
                s = self.st
                L, M = self.view(0), self.view(1)
                if self.kind in ("softmax", "soft2"):
                    act.wait_ge(s["a"], s.at("a") + 1)
                    act.activation(M, M, ACT.Exp).then_inc(s["a"], 1)
                if self.kind in ("top2", "soft2"):
                    act.wait_ge(s["a"], s.at("a") + 1 + 2 * (self.kind == "soft2"))
                    act.activation(sm[:, 3, :, :], sm[:, 3, :, :], ACT.Exp).then_inc(s["a"], 1)
                for g in range(0 if self.routed else self.groups):
                    n = min(4 * P, NP - 4 * P * g)
                    act.wait_ge(s["tr"], s.at("tr") + g + 1)
                    act.activation(cwh[0:self.E, 4 * P * g:4 * P * g + n], ps[0:self.E, 2 + g % 2, 0:n], ACT.Copy)\
                       .then_inc(s["hi"], 1)

            def dve(self, v):
                s, E = self.st, self.E
                shape = [P, KT, E]

                def link(op):
                    gate_links[0] += 1
                    op.then_inc(s["v"], 1)
                    v.wait_ge(s["v"], gate_links[0])

                after(v, *self.before)
                L, M, K1, K2, F1, C = (self.view(i) for i in range(6))
                hk = KT // 2
                v.wait_ge(s["lg"], s.at("lg") + KT)
                for b in range(2):
                    op = v.tensor_copy(L[:, b * hk:(b + 1) * hk, :],
                                       ps[:, b, 0:hk * E].rearrange("p (t e) -> p t e", e=E))
                link(op)

                def bc(x):
                    return x.to_broadcast(shape)

                def first_max(src, top, onehot):
                    link(v.tensor_reduce(top, src, AX.X, ALU.max))
                    link(v.tensor_tensor(K1, src, bc(top), ALU.is_equal))
                    link(v.tensor_tensor(K1, K1, rev[:, 0:E].rearrange("p (o e) -> p o e", o=1).to_broadcast(shape),
                                         ALU.mult))
                    link(v.tensor_reduce(sm[:, 2, :, :], K1, AX.X, ALU.max))
                    link(v.tensor_tensor(onehot, K1, bc(sm[:, 2, :, :]), ALU.is_equal))

                m1, m2 = sm[:, 0, :, :], sm[:, 1, :, :]
                if self.kind == "argmax":
                    first_max(L, m1, C)
                else:
                    if self.kind in ("softmax", "soft2"):
                        link(v.tensor_reduce(m1, L, AX.X, ALU.max))
                        link(v.tensor_tensor(M, L, bc(m1), ALU.subtract))
                        v.sem_inc(s["a"], 1)
                        v.wait_ge(s["a"], s.at("a") + 2)
                        link(v.tensor_reduce(sm[:, 3, :, :], M, AX.X, ALU.add))
                        link(v.reciprocal(sm[:, 3, :, :], sm[:, 3, :, :]))
                        link(v.tensor_tensor(L, M, bc(sm[:, 3, :, :]), ALU.mult))
                    first_max(L, m1, C)
                    link(v.scalar_tensor_tensor(M, C, -3.0e38, L, ALU.mult, ALU.add))
                    first_max(M, m2, F1)
                    if self.kind != "softmax":
                        ex = sm[:, 3, :, :]
                        link(v.tensor_tensor(ex, m2, m1, ALU.subtract))
                        v.sem_inc(s["a"], 1)
                        v.wait_ge(s["a"], s.at("a") + 2 + 2 * (self.kind == "soft2"))
                        link(v.tensor_scalar(m1, ex, 1.0, None, ALU.add))
                        link(v.reciprocal(m1, m1))
                        link(v.tensor_tensor(m2, ex, m1, ALU.mult))
                if self.routed:
                    self.slots(v, link)
                    return
                link(v.tensor_tensor(C, C, bc(m1), ALU.mult))
                link(v.tensor_tensor(F1, F1, bc(m2), ALU.mult))
                link(v.tensor_tensor(C, C, F1, ALU.add))
                link(v.memset(cwh, 0.0))
                link(v.memset(cwl, 0.0))
                v.sem_inc(s["cw"], 1)
                for g in range(self.groups):
                    n = min(4 * P, NP - 4 * P * g)
                    v.wait_ge(s["hi"], s.at("hi") + g + 1)
                    cs = slice(4 * P * g, 4 * P * g + n)
                    v.tensor_tensor(cwl[0:E, cs], ps[0:E, 2 + g % 2, 0:n], cwh[0:E, cs], ALU.subtract)\
                     .then_inc(s["lo"], 1)

            def slots(self, v, link):
                s, E = self.st, self.E
                two = self.kind != "argmax"
                T, S, S2, F1, C, K = (self.view(i) for i in (1, 3, 6, 4, 5, 2))
                hk, n = KT // 2, KT // 2 * E
                m16 = self.mask16().rearrange("p (t e) -> p t e", e=E)
                if two:
                    v.tensor_tensor(m16, C, F1, ALU.add).then_inc(s["mk"], 1)
                else:
                    v.tensor_copy(m16, C).then_inc(s["mk"], 1)

                def scan(src, a, b, size, part):
                    step = 1
                    while step < size:
                        link(v.tensor_copy(part(a, 0, step), part(src, 0, step)))
                        link(v.tensor_tensor(part(a, step, size), part(src, step, size),
                                             part(src, 0, size - step), ALU.add))
                        src, a, b = a, b, a
                        step *= 2
                    return src

                v.wait_ge(s["rk"], s.at("rk") + 1)
                for b in range(2):
                    op = v.tensor_copy(T[:, b * hk:(b + 1) * hk, :],
                                       ps[:, 4 + b, 0:n].rearrange("p (t e) -> p t e", e=E))
                link(op)
                upto = scan(T, S, S2, KT, lambda x, i, j: x[:, i:j, :])
                link(v.tensor_scalar(rti[:, 0:1, 0:E], upto[:, KT - 1:KT, :], float(P - 1), None, ALU.add))
                link(v.tensor_scalar(rti[:, 1, 0:E], rti[:, 0, 0:E], 7, None, ALU.logical_shift_right))
                tiles = rt[:, 0, 0:E]
                link(v.tensor_copy(tiles, rti[:, 1, 0:E]))
                ends = scan(tiles, rt[:, 1, 0:E], rt[:, 2, 0:E], E, lambda x, i, j: x[:, i:j])
                first = rt[:, 3, 0:E]
                link(v.tensor_tensor(first, ends, tiles, ALU.subtract))
                link(v.tensor_tensor(upto, upto, T, ALU.subtract))
                link(v.scalar_tensor_tensor(upto, first.rearrange("p (o e) -> p o e", o=1).to_broadcast([P, KT, E]),
                                            float(P), upto, ALU.mult, ALU.add))
                for b in range(2):
                    part = upto[:, b * hk:(b + 1) * hk, :]
                    op = v.tensor_tensor(part, part, ps[:, 2 + b, 0:n].rearrange("p (t e) -> p t e", e=E), ALU.add)
                link(op)
                for a, onehot in enumerate((C, F1) if two else (C,)):
                    link(v.tensor_tensor(K, onehot, upto, ALU.mult))
                    link(v.tensor_reduce(sm[:, 2, :, :], K, AX.X, ALU.add))
                    link(v.tensor_copy(posu[:, a:a + 1, :].rearrange("p a t -> p t a"), sm[:, 2, :, :]))
                J = TILES[E]
                cmp = R2[0:1, 4 * LG:4 * LG + J * E].rearrange("p (j e) -> p j e", e=E)
                link(v.tensor_tensor(cmp, iota[:, 0:J].rearrange("p (j o) -> p j o", o=1).to_broadcast([1, J, E]),
                                     ends[0:1, :].rearrange("p (o e) -> p o e", o=1).to_broadcast([1, J, E]),
                                     ALU.is_ge))
                link(v.tensor_reduce(rt2[:, 0:J, :], cmp, AX.X, ALU.add))
                link(v.tensor_scalar(rt2[:, 0:J, :], rt2[:, 0:J, :], float(E - 1), None, ALU.min))
                link(v.memset(rt2[:, J:J + 2, :], 0.0))
                link(v.scalar_tensor_tensor(packed[:, 0:J, :], rt2[:, 2:J + 2, :], float(E), rt2[:, 1:J + 1, :],
                                            ALU.mult, ALU.add))
                v.scalar_tensor_tensor(eid[:, 0:J].rearrange("p (j o) -> p j o", o=1), packed[:, 0:J, :], float(E),
                                       rt2[:, 0:J, :], ALU.mult, ALU.add).then_inc(s["cw"], 1)

        def in_turns(eng, body):
            R = SLOTS_RUN
            for u in range(R):
                body(u, u, 0)
            with eng.Fori(1, KT // R) as g:
                for u in range(R):
                    body(R * g + u, u, g)
            for t in range(KT // R * R, KT):
                body(t, t % R, t // R)

        def turns(u):
            return len(range(u, KT, SLOTS_RUN))

        def again(turn):
            return not isinstance(turn, int) or turn > 0

        class Scatter:
            def __init__(self, name, A, before):
                self.st = Stage("scat", go=KT, tr=KT, row=KT + SLOTS_RUN, ix=KT,
                                **{f"sc{u}": 16 * A * turns(u) for u in range(SLOTS_RUN)})
                self.A, self.before = A, before
                self.done = [self.st.end(f"sc{u}") for u in range(SLOTS_RUN)]

            def pe(self, pe):
                after(pe, *self.before)
                s = self.st
                pe.sem_inc(s["row"], SLOTS_RUN)

                def body(t, u, g):
                    pe.wait_ge(s["row"], s.at("row") + t + 1)
                    for i in range(4):
                        x = (XH, XL)[i // 2][:, i % 2, dyn(t * P, P)]
                        mm = pe.transpose(ps[:, u, 0:D].bitcast(F16)[:, i * P:(i + 1) * P], x, ident16[:, :])
                    mm.then_inc(s["tr"], 1)
                in_turns(pe, body)

            def act(self, act):
                after(act, *self.before)
                s, n = self.st, 16 * self.A

                def body(t, u, g):
                    act.wait_ge(s["tr"], s.at("tr") + t + 1)
                    if again(g):
                        act.wait_ge(s[f"sc{u}"], s.at(f"sc{u}") + n * g)
                    act.activation(row[:, u, :], ps[:, u, 0:D].bitcast(F16), ACT.Copy).then_inc(s["row"], 1)
                in_turns(act, body)

            def dve(self, v):
                after(v, *self.before)
                s, n = self.st, 16 * self.A

                def body(t, u, g):
                    if again(g):
                        v.wait_ge(s[f"sc{u}"], s.at(f"sc{u}") + n * g)
                    v.tensor_copy(idx[:, u, 0:self.A], posu[:, 0:self.A, dyn(t, 1)].rearrange("p a o -> p (a o)"))\
                     .then_inc(s["ix"], 1)
                in_turns(v, body)

            def pool(self, pool):
                after(pool, *self.before)
                s = self.st
                def body(t, u, g):
                    pool.wait_ge(s["row"], s.at("row") + t + SLOTS_RUN + 1)
                    pool.wait_ge(s["ix"], s.at("ix") + t + 1)
                    pool.sem_inc(s["go"], 1)
                    for a in range(self.A):
                        pool.indirect_dma_start(
                            xs_dram[:, :], bass.IndirectOffsetOnAxis(ap=idx[:, u, a:a + 1], axis=0), row[:, u, :], None
                        ).then_inc(s[f"sc{u}"], 16)
                in_turns(pool, body)

        class Experts:

            def __init__(self, name, E, hid, b1, b2, func):
                self.J, self.E, self.HT = TILES[E], E, max(1, hid // E // P)
                J, n = self.J, 16 * (TILES[E] // 2)
                self.st = Stage("ex", xg0=n, xg1=n, t3=J + 2, xf=J + 2, hm=J + 2, ha=J + 2, hi=J, lo=J + 2, ym=J + 2,
                                yo=J + 2, st0=n + 16, st1=n + 16)
                self.hid, self.b1, self.b2, self.func = hid, b1, b2, func
                self.done = [self.st.end("st0"), self.st.end("st1")]
                n = 4 * hid
                self.wh = BIG[:, 0:n // 2].bitcast(F16)
                self.wl = BIG[:, n // 2:n].bitcast(F16)
                self.nw = n

            def experts(self, eng, j):
                E = self.E
                v = eng.value_load(eid[0:1, dyn(j, 1)], min_val=0, max_val=E ** 3 - 1)
                return v % E, (v // E) % E, v // E ** 2

            def sp(self, sp):
                after(sp, *self.before)
                s = self.st

                def load(j, u):
                    sp.wait_ge(s["t3"], s.at("t3") + j + 1)
                    sp.dma_start(xg[:, u, :], xs_dram[dyn(j * P, P), :]).then_inc(s[f"xg{u}"], 16)

                def store(j, u):
                    sp.wait_ge(s["yo"], s.at("yo") + j + 3)
                    sp.dma_start(ys_dram[dyn(j * P, P), :], yo[:, u, :]).then_inc(s[f"st{u}"], 16)

                for j in range(4):
                    load(j, j % 2)
                with sp.Fori(0, self.J // 2 - 2) as g:
                    for u in range(2):
                        load(2 * g + 4 + u, u)
                        store(2 * g + u, u)
                for j in range(self.J - 4, self.J):
                    store(j, j % 2)

            def pe(self, pe):
                after(pe, *self.before)
                s, E, HT = self.st, self.E, self.HT
                W1h = self.wh[:, 0:2 * self.hid].rearrange("p (f h) -> p f h", f=FT)
                W1l = self.wl[:, 0:2 * self.hid].rearrange("p (f h) -> p f h", f=FT)
                W2h = self.wh[:, 2 * self.hid:].rearrange("p (t d) -> p t d", d=D)
                W2l = self.wl[:, 2 * self.hid:].rearrange("p (t d) -> p t d", d=D)
                for n in ("t3", "xf", "hm", "ha", "lo", "ym", "yo"):
                    pe.sem_inc(s[n], 2)
                for u in range(2):
                    pe.sem_inc(s[f"st{u}"], 16)

                def first(e):
                    return e // 2 if E == E0 else e * HT

                def turn(j, u, g):
                    pe.wait_ge(s[f"xg{u}"], s.at(f"xg{u}") + 16 * g + 16)
                    pe.wait_ge(s["xf"], s.at("xf") + j + 1)
                    for i in range(4):
                        mm = pe.transpose(ps[:, u, 0:D].bitcast(F16)[:, i * P:(i + 1) * P],
                                          xg[:, u, i * P:(i + 1) * P], ident16[:, :])
                    mm.then_inc(s["t3"], 1)

                def hidden(j, u, e):
                    t0 = first(e)
                    pe.wait_ge(s["xf"], s.at("xf") + j + 3)
                    pe.wait_ge(s["ha"], s.at("ha") + j + 1)
                    for t in range(HT):
                        for f in range(FT):
                            w = dyn((t0 + t) * P, P)
                            mm = mm3(pe, ps[:, 2 + u, t * P:(t + 1) * P], W1h[:, f, w], W1l[:, f, w],
                                     xf[:, u, f, :], xf[:, u, 2 + f, :], start=f == 0, stop=f == FT - 1)
                    mm.then_inc(s["hm"], 1)

                def result(j, u, e):
                    t0 = first(e)
                    pe.wait_ge(s["lo"], s.at("lo") + j + 3)
                    pe.wait_ge(s["yo"], s.at("yo") + j + 1)
                    out = ps[:, 4 + u, 0:D]
                    for t in range(HT):
                        mm3(pe, out, hh[:, u, t, :], hl[:, u, t, :], W2h[:, t0 + t, :], W2l[:, t0 + t, :], start=t == 0)
                    sel = selE[:, dyn(e * P, P)]
                    pe.matmul(out, sel, b2h[:, self.b2, :], start=False, stop=False)
                    pe.matmul(out, sel, b2l[:, self.b2, :], start=False, stop=True).then_inc(s["ym"], 1)

                J = self.J
                turn(0, 0, 0)
                turn(1, 1, 0)
                hidden(0, 0, self.experts(pe, 0)[0])
                with pe.Fori(0, J // 2 - 1) as g:
                    e0, e1, e2 = self.experts(pe, 2 * g)
                    turn(2 * g + 2, 0, g + 1)
                    hidden(2 * g + 1, 1, e1)
                    result(2 * g, 0, e0)
                    turn(2 * g + 3, 1, g + 1)
                    hidden(2 * g + 2, 0, e2)
                    result(2 * g + 1, 1, e1)
                e0, e1, _ = self.experts(pe, J - 2)
                hidden(J - 1, 1, e1)
                result(J - 2, 0, e0)
                result(J - 1, 1, e1)

            def act(self, act):
                after(act, *self.before)
                s, E, HT = self.st, self.E, self.HT

                def turned(j, u):
                    act.wait_ge(s["t3"], s.at("t3") + j + 3)
                    act.wait_ge(s["hm"], s.at("hm") + j + 1)
                    act.activation(xf[:, u, :, :].rearrange("p i n -> p (i n)"), ps[:, u, 0:D].bitcast(F16), ACT.Copy)\
                       .then_inc(s["xf"], 1)

                def hidden(j, u, e):
                    act.wait_ge(s["hm"], s.at("hm") + j + 3)
                    act.wait_ge(s["lo"], s.at("lo") + j + 1)
                    for t in range(HT):
                        sc = cols[:, dyn(e + _COLS["L0_half"], 1)] if E == E0 else 1.0
                        op = act.activation(hact[:, u, t, :], ps[:, 2 + u, t * P:(t + 1) * P], self.func,
                                            bias=cols[:, dyn(e * HT + (self.b1 + t), 1)], scale=sc)
                    op.then_inc(s["ha"], 1)
                    act.wait_ge(s["ha"], s.at("ha") + j + 3)
                    act.wait_ge(s["ym"], s.at("ym") + j + 1)
                    act.activation(hh[:, u, 0:HT, :], hact[:, u, 0:HT, :], ACT.Copy).then_inc(s["hi"], 1)

                turned(0, 0)
                turned(1, 1)
                hidden(0, 0, self.experts(act, 0)[0])
                with act.Fori(0, self.J // 2 - 1) as g:
                    _, e1, e2 = self.experts(act, 2 * g)
                    turned(2 * g + 2, 0)
                    hidden(2 * g + 1, 1, e1)
                    turned(2 * g + 3, 1)
                    hidden(2 * g + 2, 0, e2)
                hidden(self.J - 1, 1, self.experts(act, self.J - 2)[1])

            def dve(self, v):
                after(v, *self.before)
                s, HT = self.st, self.HT

                def low(j, u):
                    v.wait_ge(s["hi"], s.at("hi") + j + 1)
                    v.tensor_tensor(hl[:, u, 0:HT, :], hact[:, u, 0:HT, :], hh[:, u, 0:HT, :], ALU.subtract)\
                     .then_inc(s["lo"], 1)

                def result(j, u, g):
                    v.wait_ge(s["ym"], s.at("ym") + j + 3)
                    v.wait_ge(s[f"st{u}"], s.at(f"st{u}") + 16 * g + 16)
                    v.tensor_copy(yo[:, u, :], ps[:, 4 + u, 0:D]).then_inc(s["yo"], 1)

                low(0, 0)
                with v.Fori(0, self.J // 2 - 1) as g:
                    result(2 * g, 0, g)
                    low(2 * g + 1, 1)
                    result(2 * g + 1, 1, g)
                    low(2 * g + 2, 0)
                J = self.J
                result(J - 2, 0, J // 2 - 1)
                low(J - 1, 1)
                result(J - 1, 1, J // 2 - 1)

        class Combine:

            def __init__(self, name, A, before):
                self.st = Stage("comb", go=KT, ix=KT, **{f"g{u}": 16 * A * turns(u) for u in range(SLOTS_RUN)},
                                za=KT * (A - 1), z=KT + SLOTS_RUN, zt=KT + 2, out=KT + 2)
                self.A, self.before = A, before
                self.done = [self.st.end("out")]

            def pool(self, pool):
                after(pool, *self.before)
                s = self.st

                def body(t, u, g):
                    pool.wait_ge(s["ix"], s.at("ix") + t + 1)
                    pool.wait_ge(s["z"], s.at("z") + t + 1)
                    pool.sem_inc(s["go"], 1)
                    for a in range(self.A):
                        pool.indirect_dma_start(
                            yg[:, u, a, :], None, ys_dram[:, :], bass.IndirectOffsetOnAxis(ap=idg[:, u, a:a + 1], axis=0)
                        ).then_inc(s[f"g{u}"], 16)
                in_turns(pool, body)

            def pe(self, pe):
                after(pe, *self.before)
                s = self.st
                pe.sem_inc(s["z"], SLOTS_RUN)
                pe.sem_inc(s["zt"], 2)
                pe.sem_inc(s["out"], 2)

                def body(t, u, g):
                    u = u % 2
                    pe.wait_ge(s["z"], s.at("z") + t + SLOTS_RUN + 1)
                    pe.wait_ge(s["out"], s.at("out") + t + 1)
                    for f in range(FT):
                        mm = pe.transpose(ps[:, 6 + u, f * P:(f + 1) * P], zt[:, u, f * P:(f + 1) * P], ident[:, :])
                    mm.then_inc(s["zt"], 1)
                in_turns(pe, body)

            def dve(self, v):
                after(v, *self.before)
                s, A = self.st, self.A

                def indices(t, u, g):
                    if again(g):
                        v.wait_ge(s[f"g{u}"], s.at(f"g{u}") + 16 * A * g)
                    v.tensor_copy(idg[:, u, 0:A], posu[:, 0:A, dyn(t, 1)].rearrange("p a o -> p (a o)"))\
                     .then_inc(s["ix"], 1)

                def weigh(t, u, g):
                    v.wait_ge(s[f"g{u}"], s.at(f"g{u}") + 16 * A * (g + 1))
                    v.wait_ge(s["zt"], s.at("zt") + t + 1)
                    z = zt[:, u % 2, :]
                    if A == 1:
                        v.tensor_scalar(z, yg[:, u, 0, :], 0.0, None, ALU.max).then_inc(s["z"], 1)
                        return
                    v.tensor_scalar(z, yg[:, u, 0, :], sm[:, 0, dyn(t, 1), 0], None, ALU.mult).then_inc(s["za"], 1)
                    v.wait_ge(s["za"], s.at("za") + t + 1)
                    v.scalar_tensor_tensor(z, yg[:, u, 1, :], sm[:, 1, dyn(t, 1), 0], z, ALU.mult, ALU.add)\
                     .then_inc(s["z"], 1)

                def add(t, u):
                    v.wait_ge(s["zt"], s.at("zt") + t + 3)
                    x = xT[:, :, dyn(t * P, P)]
                    v.tensor_tensor(x, x, ps[:, 6 + u, 0:D].rearrange("p (f n) -> p f n", f=FT), ALU.add)\
                     .then_inc(s["out"], 1)

                R = SLOTS_RUN

                def step(t, u, g):
                    weigh(t, u, g)
                    if not isinstance(t, int) or t + R < KT:
                        indices(t + R, u, g + 1)
                    if not isinstance(t, int) or t > 0:
                        add(t - 1, (u - 1) % 2)
                for t in range(R):
                    indices(t, t, 0)
                for t in range(R):
                    step(t, t, 0)
                with v.Fori(1, KT // R - 1) as g:
                    for u in range(R):
                        step(R * g + u, u, g)
                for t in range((KT // R - 1) * R, KT):
                    step(t, t % R, t // R)
                add(KT - 1, (KT - 1) % 2)

        class Many:

            def __init__(self, name, before):
                self.st = Stage("many", mm=CH, mx=CH, v=0)
                self.before = before
                self.done = [(self.st["v"], 3)]

            def pe(self, pe):
                after(pe, *self.before)
                for c in range(CH):
                    if c >= 2:
                        pe.wait_ge(self.st["mx"], c - 1)
                    pe.matmul(ps[:, 6 + c % 2, 0:CW], one2[:, :], cnt[:, chunk(c)], start=True, stop=True)\
                      .then_inc(self.st["mm"], 1)

            def dve(self, v):
                after(v, *self.before)
                s = self.st
                for c in range(CH):
                    v.wait_ge(s["mm"], c + 1)
                    v.tensor_reduce(many_f[:, 0, c:c + 1], ps[0:1, 6 + c % 2, 0:CW], AX.X, ALU.max).then_inc(s["mx"], 1)
                v.wait_ge(s["mx"], CH)
                v.tensor_reduce(many_f[:, 1, 0:1], many_f[:, 0, 0:CH], AX.X, ALU.max).then_inc(s["v"], 1)
                v.wait_ge(s["v"], 1)
                v.tensor_scalar(many_f[:, 1, 1:2], many_f[:, 1, 0:1], float(TOPK_ROWS), None, ALU.is_gt)\
                 .then_inc(s["v"], 1)
                v.wait_ge(s["v"], 2)
                v.tensor_copy(many[:, :], many_f[:, 1, 1:2]).then_inc(s["v"], 1)

        class TopRows:

            BITS, STEP, REST = 31, 7, 6 + 24 + 3

            def __init__(self, name, before):
                self.st = Stage("top", ld=0, f=0, th=0, v=0, kp=0, tr=0, cp=0, st=0, go=0, ok=1)
                self.before = before
                self.done = [self.st.end("ok")]

            A, F, S, E, O = (BIG[:, i * NP:(i + 1) * NP] for i in range(5))
            X, Y = R1[:, 0:NP], R1[:, NP:2 * NP]

            def branch(self, eng):
                after(eng, *self.before)
                return eng.If(eng.value_load(many[0:1, 0:1], min_val=0, max_val=1) > 0)

            def sp(self, sp):
                s = self.st
                with self.branch(sp):
                    with sp.Fori(0, KT) as t:
                        sp.dma_start(self.A, io["adj"][dyn(t * P, P), :]).then_inc(s["ld"], 16)
                        sp.wait_ge(s["cp"], t + 1)
                        sp.sem_inc(s["go"], 1)
                        sp.dma_start(adj_top.rearrange("(k p) i -> p k i", p=P)[:, :, dyn(t * P, P)],
                                     self.O.rearrange("p (k i) -> p k i", k=KT)).then_inc(s["st"], 16)
                        sp.wait_ge(s["st"], 16 * t + 16)
                        sp.sem_inc(s["go"], 1)
                sp.sem_inc(s["ok"], 1)

            def act(self, act):
                s = self.st
                with self.branch(act):
                    with act.Fori(0, KT) as t:
                        act.wait_ge(s["f"], t + 1)
                        act.activation(self.F, self.F, ACT.Tanh).then_inc(s["th"], 1)

            def pe(self, pe):
                s = self.st
                with self.branch(pe):
                    with pe.Fori(0, KT) as t:
                        pe.wait_ge(s["kp"], t + 1)
                        for k in range(KT):
                            mm = pe.transpose(ps[:, k // 4, k % 4 * P:(k % 4 + 1) * P], self.A[:, k * P:(k + 1) * P],
                                              ident[:, :])
                        mm.then_inc(s["tr"], 1)

            def dve(self, v):
                s = self.st
                A, F, S, E, O = self.A, self.F, self.S, self.E, self.O
                cand, bit, trial, ge = (bits[:, i, :] for i in range(4))
                left, n = room[:, 0, :], room[:, 1, :]
                with self.branch(v), v.Fori(0, KT) as t:
                    at = t * (self.BITS * self.STEP + self.REST)
                    done = 0

                    def link(op, more=0):
                        nonlocal done
                        op.then_inc(s["v"], 1)
                        done += 1
                        v.wait_ge(s["v"], at + more + done)

                    v.wait_ge(s["ld"], 16 * t + 16)
                    v.scalar_tensor_tensor(F, A, 0.0, A, ALU.max, ALU.mult).then_inc(s["f"], 1)
                    link(v.memset(cand, 0))
                    link(v.memset(bit, 1 << self.BITS - 1))
                    v.wait_ge(s["th"], t + 1)
                    v.sem_inc(s["go"], 1)
                    with v.Fori(0, self.BITS) as b:
                        more = b * self.STEP
                        link(v.tensor_tensor(trial, cand, bit, ALU.bitwise_or), more)
                        link(v.tensor_scalar(S, F, trial.bitcast(F32), None, ALU.is_ge), more)
                        link(v.tensor_reduce(n, S, AX.X, ALU.add), more)
                        link(v.tensor_scalar(ge, n, float(TOPK_ROWS), None, ALU.is_ge), more)
                        link(v.tensor_tensor(ge, ge, bit, ALU.mult), more)
                        link(v.tensor_tensor(cand, cand, ge, ALU.bitwise_or), more)
                        link(v.tensor_scalar(bit, bit, 1, None, ALU.logical_shift_right), more)
                        v.sem_inc(s["go"], 1)
                    at = at + (self.BITS - 1) * self.STEP
                    value = cand.bitcast(F32)
                    link(v.tensor_scalar(S, F, value, None, ALU.is_gt))
                    link(v.tensor_reduce(n, S, AX.X, ALU.add))
                    link(v.tensor_scalar(left, n, -1.0, float(TOPK_ROWS), ALU.mult, ALU.add))
                    link(v.tensor_scalar(E, F, value, None, ALU.is_equal))
                    src, a, b, step = E, self.X, self.Y, 1
                    while step < NP:
                        link(v.tensor_copy(a[:, 0:step], src[:, 0:step]))
                        link(v.tensor_tensor(a[:, step:NP], src[:, step:NP], src[:, 0:NP - step], ALU.add))
                        src, a, b = a, b, a
                        step *= 2
                    link(v.scalar_tensor_tensor(src, src, left, E, ALU.is_le, ALU.mult))
                    link(v.tensor_tensor(src, src, S, ALU.add))
                    link(v.tensor_tensor(A, A, src, ALU.mult))
                    v.sem_inc(s["kp"], 1)
                    assert done == self.STEP + self.REST, done
                    v.wait_ge(s["tr"], t + 1)
                    for k in range(0, KT, 4):
                        w = min(4, KT - k) * P
                        op = v.tensor_copy(O[:, k * P:k * P + w], ps[:, k // 4, 0:w])
                    op.then_inc(s["cp"], 1)

        class GAT:
            def __init__(self, name, before):
                self.st = Stage("gat", fr=0, mm=0, ht=0, v=0, mx=0, ar=0, e=0, ex=0, tr=0, qt=0, qs=0, q0=0, q1=0,
                                q2=0, a0=0, a1=0, mk=0, pp=0, gg=0, used=0, ev=0, den=0, inv=0, out=0, nt=0, pad=0)
                self.before = before
                self.done = [(self.st["out"], 3 * 2), (self.st["pad"], 2)]

            ht = R1[:, :].rearrange("p (t d) -> p t d", t=KT)
            prod = R2[:, :].rearrange("p (t d) -> p t d", t=KT)
            QT = R2[:, 0:NP]

            @staticmethod
            def rows(h):
                return (slice(0, HF), slice(HF, P)) if h % 2 == 0 else (slice(HF, P), slice(0, HF))

            @staticmethod
            def inv(h):
                a = NP + (h // 2) * THIRD
                return R2[:, a:a + THIRD].rearrange("p (c n) -> p c n", c=2)

            spare = [x[:, :, :].rearrange("p f n -> p (f n)").bitcast(F32) for x in (XH, XL)]

            def den(self, h):
                return self.spare[h // 2][:, 2 * THIRD:3 * THIRD].rearrange("p (c n) -> p c n", c=2)

            def Qb(self, x):
                tiles = [BIG[:, 0:2 * THIRD], BIG[:, 2 * THIRD:4 * THIRD]] if x != 1 else \
                    [y[:, 0:2 * THIRD] for y in self.spare]
                return [y.rearrange("p (h n) -> p h n", h=2) for y in tiles]

            PT = BIG[:, 4 * THIRD:12 * THIRD].rearrange("p (u h n) -> p u h n", u=2, h=HEADS)
            A = BIG[:, 12 * THIRD:14 * THIRD].rearrange("p (u n) -> p u n", u=2)
            MK = BIG[:, 14 * THIRD:16 * THIRD].rearrange("p (u n) -> p u n", u=2)
            G = BIG[:, 16 * THIRD:16 * THIRD + 1024].rearrange("p (u n) -> p u n", u=2)

            def tiles(self, eng, body):
                with eng.Fori(0, KT // 2) as g:
                    for u in range(2):
                        body(2 * g + u, u)

            def steps(self, eng, x, body, between=None):
                n0 = KT * x
                for u in range(2):
                    body(n0 + u, u, u, n0 // 2)
                if between and x:
                    between(x - 1)
                with eng.Fori(1, KT // 2 - 1) as g:
                    for u in range(2):
                        body(2 * g + u + n0, 2 * g + u, u, g + n0 // 2)
                for u in range(2):
                    body(n0 + KT - 2 + u, KT - 2 + u, u, n0 // 2 + KT // 2 - 1)

            def sp(self, sp):
                after(sp, *self.before)
                s = self.st

                def spread(x):
                    cols = slice(x * THIRD, (x + 1) * THIRD)
                    for i, tile in enumerate(self.Qb(x)):
                        q = q_dram[2 * i:2 * i + 2, cols].rearrange("(o h) n -> o h n", o=1)
                        sp.dma_start(tile, q.to_broadcast([P, 2, THIRD])).then_inc(s[f"q{x}"], 16)

                def body(n, k, u, turn, x):
                    if not (isinstance(n, int) and n < 2):
                        sp.wait_ge(s["mk"], n - 1)
                    sp.dma_start(self.A[:, u, :], io["adjT"][dyn(k * P, P), x * THIRD:(x + 1) * THIRD])\
                      .then_inc(s[f"a{u}"], 16)
                    if isinstance(n, int) and n == 1:
                        spread(1)

                def ahead(done):
                    if done == 0:
                        sp.wait_ge(s["pp"], KT)
                        spread(2)

                sp.wait_ge(s["qt"], 6)
                sp.dma_start(q_dram, self.QT[0:HEADS, :]).then_inc(s["qs"], 16)
                sp.wait_ge(s["qs"], 16)
                spread(0)
                for x in range(3):
                    self.steps(sp, x, lambda n, k, u, turn: body(n, k, u, turn, x), ahead)

            def pe(self, pe):
                after(pe, *self.before)
                s = self.st
                pe.sem_inc(s["fr"], 2)

                def body(t, u):
                    pe.wait_ge(s["fr"], t + 1)
                    for f in range(FT):
                        mm = mm3(pe, ps[:, 4 + u, 0:D], XH[:, f, dyn(t * P, P)], XL[:, f, dyn(t * P, P)],
                                 WH[:, f * D:f * D + D], WLo[:, f * D:f * D + D], start=f == 0, stop=f == FT - 1)
                    mm.then_inc(s["mm"], 1)
                self.tiles(pe, body)
                q = gv[:, 4, :].rearrange("p (t h) -> p t h", h=HEADS)
                pe.wait_ge(s["ex"], 3)
                for g in range(6):
                    if g >= 2:
                        pe.wait_ge(s["qt"], g - 1)
                    for j, t in enumerate(range(4 * g, min(4 * g + 4, KT))):
                        mm = pe.transpose(ps[0:HEADS, g % 2, j * P:(j + 1) * P], q[:, t, :], ident[:, :])
                    mm.then_inc(s["tr"], 1)
                for x in range(3):
                    def body(n, k, u, turn):
                        pe.wait_ge(s["pp"], n + 1)
                        pe.wait_ge(s["gg"], n + 1)
                        start, stop = isinstance(k, int) and k == 0, isinstance(k, int) and k == KT - 1
                        for h in range(HEADS):
                            if start and x:
                                pe.wait_ge(s["ev"], HEADS * (x - 1) + h + 1)
                            for c in range(2):
                                mm = pe.matmul(ps[:, 2 * h + c, 0:CW], self.G[:, u, h * P:(h + 1) * P],
                                               self.PT[:, u, h, c * CW:(c + 1) * CW], start=start, stop=stop)
                        mm.then_inc(s["used"], 1)
                    self.steps(pe, x, body)

            def act(self, act):
                after(act, *self.before)
                s = self.st

                def body(t, u):
                    act.wait_ge(s["mm"], t + 1)
                    act.activation(self.ht[:, dyn(t, 1), :], ps[:, 4 + u:5 + u, 0:D], ACT.Copy).then_inc(s["fr"], 1)
                self.tiles(act, body)
                act.wait_ge(s["e"], 1)
                act.activation(gv[:, 2, :], gv[:, 1, :], ACT.Exp, scale=0.8).then_inc(s["ex"], 1)
                act.activation(gv[:, 3, :], gv[:, 1, :], ACT.Exp, scale=0.2).then_inc(s["ex"], 1)
                act.activation(gv[:, 4, :], gv[:, 0, :], ACT.Exp).then_inc(s["ex"], 1)
                for g in range(6):
                    n = min(4 * P, NP - 4 * P * g)
                    act.wait_ge(s["tr"], g + 1)
                    act.activation(self.QT[0:HEADS, 4 * P * g:4 * P * g + n], ps[0:HEADS, g % 2, 0:n], ACT.Copy)\
                       .then_inc(s["qt"], 1)
                act.wait_ge(s["ex"], 3)
                zp = gv[:, 3, :]

                def body(n, k, u, turn):
                    if not (isinstance(n, int) and n < 2):
                        act.wait_ge(s["used"], n - 1)
                    for h in range(HEADS):
                        z = zp[:, dyn(HEADS * k + h, 1)]
                        a, b = (h * P, h * P + HF) if h % 2 == 0 else (h * P + HF, h * P)
                        act.activation(self.G[:, u:u + 1, a:a + HF], self.ht[:, dyn(k, 1), h * HF:(h + 1) * HF],
                                       ACT.Copy, scale=z)
                        op = act.activation(self.G[:, u, b:b + HF], onesf[:, 0:HF], ACT.Copy, scale=z)
                    op.then_inc(s["gg"], 1)

                def invert(x):
                    for p in range(2):
                        inv = self.inv(2 * p)
                        act.wait_ge(s["den"], HEADS * x + 2 * p + 2)
                        act.activation(inv, self.den(2 * p), ACT.Ln).then_inc(s["inv"], 1)
                        act.wait_ge(s["inv"], 2 * (2 * x + p) + 1)
                        act.activation(inv, inv, ACT.Exp, scale=-1.0).then_inc(s["inv"], 1)
                for x in range(3):
                    self.steps(act, x, body, invert)
                invert(2)

            def pool(self, pool):
                s = self.st
                pool.wait_ge(s["mx"], 1)
                pool.partition_all_reduce(gm[:, 1, :], gm[:, 0, :], P, bass.bass_isa.ReduceOp.max).then_inc(s["ar"], 1)

            def dve(self, v):
                s = self.st
                links = [0]

                def link(op):
                    links[0] += 1
                    op.then_inc(s["v"], 1)
                    v.wait_ge(s["v"], links[0])

                after(v, *self.before)
                half = KT // 2
                for g in range(2):
                    ts, cs = slice(g * half, (g + 1) * half), slice(HEADS * g * half, HEADS * (g + 1) * half)
                    v.wait_ge(s["fr"], half * (g + 1) + 2)
                    for i in range(2):
                        w = al_bc[:, i, :].rearrange("p (o d) -> p o d", o=1).to_broadcast([P, half, D])
                        link(v.tensor_tensor(self.prod[:, ts, :], self.ht[:, ts, :], w, ALU.mult))
                        link(v.tensor_reduce(gv[:, i, cs], self.prod[:, ts, :].rearrange("p t (h f) -> p (t h) f", h=HEADS),
                                             AX.X, ALU.add))
                er = gv[:, 1, :].rearrange("p (t h) -> p h t", h=HEADS)
                link(v.tensor_reduce(gm[:, 0, :], er[:, :, 0:KT - 1], AX.X, ALU.max))
                v.tensor_tensor(gm[0:LAST, 0, :], gm[0:LAST, 0, :], gv[0:LAST, 1, HEADS * (KT - 1):HEADS * KT],
                                ALU.max).then_inc(s["mx"], 1)
                v.wait_ge(s["ar"], 1)
                M = gm[:, 1, :].rearrange("p (o h) -> p o h", o=1).to_broadcast([P, KT, HEADS])
                el3 = gv[:, 0, :].rearrange("p (t h) -> p t h", h=HEADS)
                er3 = gv[:, 1, :].rearrange("p (t h) -> p t h", h=HEADS)
                link(v.tensor_tensor(el3, el3, M, ALU.add))
                link(v.tensor_scalar(gv[:, 0, :], gv[:, 0, :], -0.8, 0.0, ALU.mult, ALU.min))
                link(v.tensor_tensor(er3, er3, M, ALU.subtract))
                v.sem_inc(s["e"], 1)
                v.wait_ge(s["ex"], 3)
                Z = gv[:, 2, :]

                def body(n, k, u, turn, x):
                    v.wait_ge(s[f"a{u}"], turn * 16 + 16)
                    if not (isinstance(n, int) and n < 2):
                        v.wait_ge(s["used"], n - 1)
                    v.tensor_scalar(self.MK[:, u, :], self.A[:, u, :], 0.0, None, ALU.not_equal)\
                     .then_inc(s["mk"], 1)
                    v.wait_ge(s["mk"], n + 1)
                    Q = self.Qb(x)
                    for h in range(HEADS):
                        op = v.scalar_tensor_tensor(self.PT[:, u, h, :], Q[h // 2][:, h % 2, :],
                                                    Z[:, dyn(HEADS * k + h, 1)], self.MK[:, u, :],
                                                    ALU.max, ALU.mult)
                    op.then_inc(s["pp"], 1)

                def finish(x):
                    v.wait_ge(s["used"], KT * (x + 1))
                    for h in range(HEADS):
                        fr, dr = self.rows(h)
                        if x:
                            v.wait_ge(s["out"], 2 * (x - 1) + h // 2 + 1)
                        v.tensor_scalar(self.den(h)[fr], ps[dr, 2 * h:2 * h + 2, 0:CW], 1e-37, None, ALU.max)\
                         .then_inc(s["den"], 1)
                    for p in range(2):
                        den, inv = self.den(2 * p), self.inv(2 * p)
                        v.wait_ge(s["inv"], 2 * (2 * x + p + 1))
                        v.tensor_tensor(den, den, inv, ALU.mult).then_inc(s["nt"], 1)
                    for p in range(2):
                        v.wait_ge(s["nt"], 4 * x + p + 1)
                        v.scalar_tensor_tensor(self.inv(2 * p), self.den(2 * p), 2.0, self.inv(2 * p),
                                               ALU.subtract, ALU.mult).then_inc(s["nt"], 1)
                    for h in range(HEADS):
                        fr, dr = self.rows(h)
                        v.wait_ge(s["nt"], 4 * x + 3 + h // 2)
                        v.tensor_tensor(self.inv(h)[fr], ps[fr, 2 * h:2 * h + 2, 0:CW], self.inv(h)[fr], ALU.mult)\
                         .then_inc(s["ev"], 1)
                    for p in range(2):
                        xs = xT[:, p, x * THIRD:(x + 1) * THIRD].rearrange("p (c n) -> p c n", c=2)
                        v.wait_ge(s["ev"], HEADS * x + 2 * p + 2)
                        v.tensor_tensor(xs, xs, self.inv(2 * p), ALU.subtract).then_inc(s["out"], 1)

                for x in range(3):
                    v.wait_ge(s[f"q{x}"], 32)
                    self.steps(v, x, lambda n, k, u, turn: body(n, k, u, turn, x), finish)
                finish(2)
                v.wait_ge(s["pp"], 3 * KT)
                for x in (XH, XL):
                    v.memset(x[:, :, NC:NP], 0.0).then_inc(s["pad"], 1)

        class FFN3:
            def __init__(self, name, before):
                self.st = Stage("last", bc=0, hm=0, ha=0, hw=0, hi=0, lo=0, yd=0, ev=0)
                self.before = before
                self.done = [(self.st["ev"], CH + 1)]

            a = BIG[:, W3N:W3N + 9 * CW].rearrange("p (t n) -> p t n", t=9)
            hi = BIG[:, W3N + 9 * CW:W3N + 9 * CW + 9 * CW // 2].bitcast(F16).rearrange("p (t n) -> p t n", t=9)
            lo = BIG[:, W3N + 9 * CW + 9 * CW // 2:W3N + 18 * CW].bitcast(F16).rearrange("p (t n) -> p t n", t=9)
            hwx = BIG[:, W3N + 18 * CW:W3N + 20 * CW].rearrange("p (t n) -> p t n", t=2)
            wh = BIG[:, 0:W3N // 2].bitcast(F16)
            wl = BIG[:, W3N // 2:W3N].bitcast(F16)
            bank = [0, 1, 2, 3, 4, 5, 0, 1, 2]

            def bias(self, i):
                name, o = (("sb1", i) if i < 2 else ("eb1", i - 2) if i < 6 else ("sb2", 0) if i == 6
                           else ("eb2", i - 7))
                return cols[:, _COLS[name] + o:_COLS[name] + o + 1]

            def pe(self, pe):
                after(pe, *self.before)
                s, wh, wl = self.st, self.wh, self.wl
                pe.sem_inc(s["ev"], 1)
                with pe.Fori(0, CH) as c:
                    X = [(XH[:, f, chunk(c)], XL[:, f, chunk(c)]) for f in range(FT)]
                    H = [(self.hi[:, t, :], self.lo[:, t, :]) for t in range(9)]

                    def tile(i, terms, out=None, inc=True, start=True, stop=True):
                        out = ps[:, self.bank[i], 0:CW] if out is None else out
                        for n, (at, (bh, bl)) in enumerate(terms):
                            mm = mm3(pe, out, wh[:, at:at + P], wl[:, at:at + P], bh, bl,
                                     start=start and n == 0, stop=stop and n == len(terms) - 1)
                        if inc:
                            mm.then_inc(s["hm"], 1)
                        return mm

                    for i in range(2):
                        tile(i, [(W3["sW1"] + f * D + i * P, X[f]) for f in range(FT)])
                    for e in range(4):
                        tile(2 + e, [(W3["eW1"] + f * 512 + e * P, X[f]) for f in range(FT)])
                    pe.wait_ge(s["lo"], c * 9 + 2)
                    pe.wait_ge(s["ha"], c * 9 + 1)
                    tile(6, [(W3["sW2"] + f * P, H[f]) for f in range(FT)])
                    for p in range(2):
                        pe.wait_ge(s["lo"], c * 9 + 4 + 2 * p)
                        tile(7 + p, [(W3["eW2"] + e * P, H[2 + e]) for e in (2 * p, 2 * p + 1)])
                    for p in range(2):
                        for i, cw in enumerate((cwh, cwl)):
                            mm = pe.matmul(ps[:, 3 + p, 0:CW], sel2[:, p * P:(p + 1) * P], cw[:, chunk(c)],
                                           start=i == 0, stop=i == 1)
                    mm.then_inc(s["bc"], 1)
                    pe.wait_ge(s["ev"], c + 1)
                    for f in range(FT):
                        out, fs = ps[:, 6 + f, 0:CW], slice(f * P, (f + 1) * P)
                        mm3(pe, out, b2h[:, 3, fs], b2l[:, 3, fs], cwh[:, chunk(c)], cwl[:, chunk(c)],
                            start=True)
                        a = _ROWS["sb3"][0] + f * P
                        pe.matmul(out, rowh[:, a:a + P], ones16[:, 0:CW], start=False, stop=False)
                        pe.matmul(out, rowl[:, a:a + P], ones16[:, 0:CW], start=False, stop=False)
                    pe.wait_ge(s["lo"], c * 9 + 9)
                    for f in range(FT):
                        mm = tile(0, [(W3["sW3"] + f * P, H[6])] + [(W3["eW3"] + p * D + f * P, H[7 + p]) for p in range(2)],
                                  out=ps[:, 6 + f, 0:CW], inc=False, start=False)
                    mm.then_inc(s["yd"], 1)

            def act(self, act):
                after(act, *self.before)
                s = self.st
                with act.Fori(0, CH) as c:
                    for i in range(9):
                        act.wait_ge(s["hm"], c * 9 + i + 1)
                        act.activation(self.a[:, i, :], ps[:, self.bank[i], 0:CW], ACT.Relu, bias=self.bias(i))\
                           .then_inc(s["ha"], 1)
                        if i < 7:
                            act.wait_ge(s["ha"], c * 9 + i + 1)
                            src = self.a[:, i, :]
                        else:
                            act.wait_ge(s["hw"], c * 2 + i - 6)
                            src = self.hwx[:, i - 7, :]
                        act.activation(self.hi[:, i, :], src, ACT.Copy).then_inc(s["hi"], 1)

            def dve(self, v):
                after(v, *self.before)
                s = self.st
                with v.Fori(0, CH) as c:
                    for i in range(9):
                        src = self.a[:, i, :]
                        if i >= 7:
                            v.wait_ge(s["ha"], c * 9 + i + 1)
                            v.wait_ge(s["bc"], c + 1)
                            src = self.hwx[:, i - 7, :]
                            v.tensor_tensor(src, self.a[:, i, :], ps[:, 3 + i - 7, 0:CW], ALU.mult).then_inc(s["hw"], 1)
                        v.wait_ge(s["hi"], c * 9 + i + 1)
                        v.tensor_tensor(self.lo[:, i, :], src, self.hi[:, i, :], ALU.subtract).then_inc(s["lo"], 1)
                    v.wait_ge(s["yd"], c + 1)
                    for f in range(FT):
                        x = xT[:, f, chunk(c)]
                        op = v.tensor_tensor(x, x, ps[:, 6 + f, 0:CW], ALU.add)
                    op.then_inc(s["ev"], 1)

        plan = []

        def add(stage):
            plan.append(stage)
            return stage

        w = add(Split(io["w0"], WH, WLo, WL // WB, [LC], WB))
        last = [w, LC]

        def go(cls, name, *args, **kw):
            nonlocal last
            st = add(cls(name, *args, before=last, **kw))
            last = [st]
            return st

        def ffn_layer(i, E, hid, gw, rows, kind, func, wname, b1, b2):
            nonlocal last
            A = 1 if kind == "argmax" else 2
            ex = Experts(f"ffn{i}", E, hid, b1, b2, func)
            sp = add(Split(io[wname], ex.wh, ex.wl, ex.nw // ST, last))
            ln = go(LN, f"ln{i}b", xT)
            go(Gates, f"gate{i}", E, gw, rows, kind)
            go(Scatter, f"sc{i}", A)
            ex.before = last + [sp]
            add(ex)
            last = [ex]
            go(Combine, f"co{i}", A)

        def small_weights(i):
            nonlocal last
            w = add(Split(io[f"w{i}"], WH, WLo, WL // WB, last, WB))
            last = [w] + last

        def network():
            nonlocal last
            ln = go(LN, "ln0a", xT)
            tl = go(TokenLinear, "tl0", 2 * D)
            last = [ln]
            fl = go(FeatLinear, "fl0", 0, kind="add")
            last = [tl, fl]
            go(Product, "pr0", "split", free=[LC])
            st = add(Dinv(last))
            last = [st] + last
            ffn_layer(0, E0, E0 * H0, 4 * D, ["router_b"], "argmax", ACT.Relu, "f0", _COLS["L0_b1"], 0)
            free = last
            small_weights(1)
            ln = go(LN, "ln1a", xT)
            tl = go(TokenLinear, "tl1a", 0, row="L1_b1", scaled=True)
            last = [ln]
            fl = go(FeatLinear, "fl1", 0, kind="nT", bias=_COLS["gb1"])
            last = [tl, fl]
            for i in range(3):
                free = [go(Product, f"pr1{i}", "kept", free=free, count=i == 0)]
                if i == 0:
                    asked = add(Many("many", last))
                    free.append(asked)
                go(LN, f"ln1n{i}", nT, gamma=(_COLS[f"g{i + 1}"], _COLS[f"be{i + 1}"]))
                if i < 2:
                    go(TokenLinear, f"tl1{'bc'[i]}", 2 * D * (i + 1), row=f"L1_b{i + 2}", scaled=True)
            go(AddN, "addn")
            ffn_layer(1, E1, E1 * H1, 6 * D, ["gate_b"], "softmax", ACT.Gelu, "f1", _COLS["L1_b1"], 1)
            last = last + [asked]
            free = [go(TopRows, "top")]
            small_weights(2)
            go(LN, "ln2a", xT)
            go(FeatLinear, "fl2", 0, kind="tanh", bias=_COLS["b_proj"])
            go(TokenLinear, "tl2", 2 * D)
            go(Product, "pr2", "filter", free=free)
            ffn_layer(2, E1, E1 * H1, 4 * D, ["bg", "bias"], "top2", ACT.Relu, "f2", _COLS["L2_b1"], 2)
            small_weights(3)
            go(LN, "ln3a", xT)
            gat = go(GAT, "gat")
            sp = add(Split(io["f3"], BIG[:, 0:W3N // 2].bitcast(F16), BIG[:, W3N // 2:W3N].bitcast(F16), W3N // ST, last))
            ln = go(LN, "ln3b", xT)
            gts = add(Gates("gate3", E3, 2 * D, ["gb"], "soft2", before=[ln]))
            last = [gts, sp]
            go(FFN3, "ffn3")

        class AddN:

            def __init__(self, name, before):
                self.st, self.before = Stage("addn", v=1), before
                self.done = [(self.st["v"], 1)]

            def dve(self, v):
                after(v, *self.before)
                v.tensor_tensor(xT[:, :, 0:NC], xT[:, :, 0:NC], nT[:, :, 0:NC], ALU.add).then_inc(self.st["v"], 1)

        network()
        out_done = sem("out_done")

        def run(eng, part):
            for st in plan:
                if part in dir(st):
                    {"sp": lambda: st.sp(eng), "act": lambda: st.act(eng), "pe": lambda: st.pe(eng),
                     "dve": lambda: st.dve(eng), "pool": lambda: st.pool(eng)}[part]()

        @block.sync
        def _(sp):
            sp.sem_inc(WS["lo"], 2)
            const_sp(sp)
            run(sp, "sp")
            after(sp, *last)
            sp.dma_start(io["out"], xT[:, :, 0:NC]).then_inc(out_done, 16)
            sp.wait_ge(out_done, 16)

        @block.scalar
        def _(act):
            clear_slots(act)
            run(act, "act")

        @block.vector
        def _(v):
            const_dve(v)
            run(v, "dve")

        @block.gpsimd
        def _(pool):
            run(pool, "pool")

        @block.tensor
        def _(pe):
            run(pe, "pe")


def _lay(w, tiles):
    w = np.asarray(w)
    return np.ascontiguousarray(w.reshape(tiles, P, -1).transpose(1, 0, 2).reshape(P, -1))


def _pad(a, cols):
    return np.concatenate([a, np.zeros((a.shape[0], cols - a.shape[1]), a.dtype)], axis=1)


def _column(v):
    return np.asarray(v).reshape(-1, P).T


def layout(i):
    i = {k: np.asarray(v) for k, v in i.items()}
    f32 = np.float32
    a = {}
    xT = np.zeros((D, NP), f32)
    xT[:, :N] = i["x"].T
    a["xT"] = np.ascontiguousarray(xT.reshape(FT, P, NP).transpose(1, 0, 2))
    adjT = np.zeros((NP, NC), f32)
    adjT[:N, :N] = i["adj"].T
    a["adjT"] = adjT
    a["adj"] = np.zeros((NP, NP), f32)
    a["adj"][:N, :N] = i["adj"]
    g = i["L0_gnn_W"].T
    a["w0"] = _pad(np.concatenate([_lay(g[:D], 2), _lay(g[D:], 2), _lay(i["L0_ffn_router_w"].T, 2)], 1), WL)
    a["w1"] = _pad(np.concatenate([_lay(i[f"L1_gnn_W{n}"], 2) for n in (1, 2, 3)] + [_lay(i["L1_ffn_gate_w"], 2)], 1), WL)
    a["w2"] = _pad(np.concatenate([_lay(i["L2_gnn_W_proj"], 2), _lay(i["L2_gnn_W_gcn"], 2), _lay(i["L2_ffn_Wg"], 2)], 1), WL)
    a["w3"] = _pad(np.concatenate([_lay(i["L3_gnn_Wm"], 2), _lay(i["L3_ffn_gW"], 2)], 1), WL)
    for n, E, H in ((0, E0, H0), (1, E1, H1), (2, E1, H1)):
        w1 = i[f"L{n}_ffn_W1"].transpose(1, 0, 2).reshape(D, E * H)
        w2 = i[f"L{n}_ffn_W2"].reshape(E * H, D)
        a[f"f{n}"] = np.concatenate([_lay(w1, 2), _lay(w2, E * H // P)], 1)
    eW2 = np.zeros((4, P, P), f32)
    for e in range(4):
        eW2[e, :, (e % 2) * HF:(e % 2 + 1) * HF] = i["L3_ffn_eW2"][e]
    a["f3"] = _pad(np.concatenate([
        _lay(i["L3_ffn_sW1"], 2), _lay(i["L3_ffn_sW2"], 2), _lay(i["L3_ffn_sW3"], 1),
        _lay(i["L3_ffn_eW1"].transpose(1, 0, 2).reshape(D, 512), 2), _lay(eW2.reshape(4 * P, P), 4),
        _lay(i["L3_ffn_eW3"].reshape(4 * HF, D), 2)], 1), W3N)
    vectors = [i["L1_ffn_b1"], i["L2_ffn_b1"]]
    for n in (1, 2, 3):
        vectors += [i[f"L1_gnn_g{n}"], i[f"L1_gnn_be{n}"]]
    vectors += [i["L1_gnn_b1"], i["L2_gnn_b_proj"], i["L2_gnn_b_gcn"], i["L3_ffn_sb1"], i["L3_ffn_eb1"],
                i["L3_ffn_sb2"], i["L3_ffn_eb2"]]
    b1, half = np.zeros((P, E0), f32), np.zeros((P, E0), f32)
    for e in range(E0):
        at = slice(e % 2 * H0, (e % 2 + 1) * H0)
        b1[at, e], half[at, e] = i["L0_ffn_b1"][e], 1.0
    a["cols"] = np.ascontiguousarray(np.concatenate([b1, half] + [_column(v) for v in vectors], 1))
    a["rows"] = np.concatenate([i[k] for k in (
        "L0_ffn_router_b", "L1_gnn_b1", "L1_gnn_b2", "L1_gnn_b3", "L1_ffn_gate_b", "L2_ffn_bg", "L2_ffn_bias",
        "L3_ffn_gb", "L3_ffn_sb3")])[None, :]
    b2 = np.zeros((P, 4, D), f32)
    for n, k in enumerate(("L0_ffn_b2", "L1_ffn_b2", "L2_ffn_b2", "L3_ffn_eb3")):
        b2[:i[k].shape[0], n] = i[k]
    a["b2"] = b2.reshape(P, 4 * D)
    al = np.stack([np.tile(i["L3_gnn_al"], HEADS), np.tile(i["L3_gnn_ar"], HEADS)])
    a["al"] = np.ascontiguousarray(np.broadcast_to(al, (P, 2, D)))
    p = np.arange(P)[:, None]
    a["sel2"] = (np.arange(2 * P)[None, :] // HF == p).astype(np.float16)
    a["selE"] = (np.arange(E0 * P)[None, :] // P == p).astype(np.float16)
    a["lt"] = (p < np.arange(P)[None, :]).astype(np.float16)
    a["one2"] = np.ones((P, P), np.float16)
    a["ident16"] = np.eye(P, dtype=np.float16)
    a["iota"] = np.arange(max(TILES.values()), dtype=f32)[None, :]
    a["ident"] = np.eye(P, dtype=f32)
    a["rev"] = np.ascontiguousarray(np.broadcast_to(E0 - np.arange(E0, dtype=f32), (P, E0)))
    a["ones16"] = np.ones((1, 512), np.float16)
    return a


def kernel(**inputs):
    import concourse.bacc as _bacc
    from concourse.bass_utils import run_bass_kernel_spmd as _run

    arrays = {f"in_{k}": v for k, v in layout(inputs).items()}
    nc = _bacc.Bacc("TRN2", target_bir_lowering=False, num_devices=1)
    io = {k[3:]: nc.dram_tensor(k, v.shape, mybir.dt.from_np(v.dtype), kind="ExternalInput").ap()
          for k, v in arrays.items()}
    io["out"] = nc.dram_tensor("out_xT", (P, FT, NC), F32, kind="ExternalOutput").ap()
    build(nc, io)
    r = _run(nc, [arrays], core_ids=[0])
    got = np.asarray(r.results[0]["out_xT"])
    return np.ascontiguousarray(got.transpose(1, 0, 2).reshape(D, NC)[:, :N].T)
```
